# Optimizing a Trainium2 kernel written in Bass

```python
import numpy as np
import jax
import jax.numpy as jnp

def _softmax(x, axis=-1):
    return jax.nn.softmax(x, axis=axis)

def _gelu(x):
    return jax.nn.gelu(x, approximate=True)

def _silu(x):
    return jax.nn.silu(x)

def _sigmoid(x):
    return jax.nn.sigmoid(x)

def _layernorm(x, axis=-1, eps=1e-05):
    m = jnp.mean(x, axis=axis, keepdims=True)
    v = jnp.var(x, axis=axis, keepdims=True)
    return (x - m) / jnp.sqrt(v + eps)

def _scatter_add(tgt, idx, src, axis=0):
    return tgt.at[idx].add(src)

def _segment_sum(src, seg, n):
    return jax.ops.segment_sum(src, seg, n)
kernel_name = 'mk_prb_d2_jaxref_r8_e17c00'

def setup_inputs(seed: int=0):
    np.random.seed(seed)
    _w = jnp.asarray

    def _L0_attn_setup():
        import jax, jax.numpy as jnp
        import numpy as np
        D_MODEL = 128
        H = 4
        DK = 128
        DV = 32
        EPS = 1e-05
        SCALE = DK ** (-0.5)

        def _delta_rule(q, k, v, beta):
            b = q.shape[0]
            qt = jnp.moveaxis(q, 1, 0)
            kt = jnp.moveaxis(k, 1, 0)
            vt = jnp.moveaxis(v, 1, 0)
            bt = jnp.moveaxis(beta, 1, 0)
            S0 = jnp.zeros((b, H, DK, DV), q.dtype)

            def step(S, inp):
                q_t, k_t, v_t, b_t = inp
                pred = jnp.einsum('bhk,bhkv->bhv', k_t, S)
                delta = (v_t - pred) * b_t[..., None]
                S = S + k_t[..., :, None] * delta[..., None, :]
                o_t = jnp.einsum('bhk,bhkv->bhv', q_t, S)
                return (S, o_t)
            _, o = jax.lax.scan(step, S0, (qt, kt, vt, bt))
            return jnp.moveaxis(o, 0, 1)
        key = jax.random.key(seed)
        ks = jax.random.split(key, 8)
        w = lambda k, i, o: jax.random.normal(k, (i, o), jnp.float32) * 2.0 ** (-2.5) * (6.0 / (i + o)) ** 0.5 * 2
        return {'x': jax.random.normal(ks[0], (2, 512, D_MODEL), jnp.float32), 'Wq': w(ks[1], D_MODEL, H * DK), 'Wk': w(ks[2], D_MODEL, H * DK), 'Wv': w(ks[3], D_MODEL, H * DV), 'Wb': w(ks[4], D_MODEL, H), 'Wg': w(ks[5], D_MODEL, H * DV), 'Wo': w(ks[6], H * DV, D_MODEL), 'norm_w': jnp.ones((DV,), jnp.float32)}
    _L0_attn_in = _L0_attn_setup()

    def _L0_ffn_setup():
        import jax, jax.numpy as jnp
        import numpy as np
        DIM = 128
        DEPTH = 2
        HEADS = 8
        DIM_HEAD = 64
        WINDOW = 64
        INNER = HEADS * DIM_HEAD
        HID = int(DIM * 4 * 2 / 3)
        B, N = (2, 1024)
        QK_SCALE = 8.0

        def shift_token(t):
            t1, t2 = jnp.split(t, 2, axis=-1)
            t2 = jnp.pad(t2, ((0, 0), (1, 0), (0, 0)))[:, :-1]
            return jnp.concatenate([t1, t2], axis=-1)

        def l2norm(t):
            return t / jnp.clip(jnp.linalg.norm(t, axis=-1, keepdims=True), 1e-12)

        def rotate_half(x):
            x1, x2 = jnp.split(x, 2, axis=-1)
            return jnp.concatenate([-x2, x1], axis=-1)

        def rotary_xpos(q, k):
            n = q.shape[-2]
            half_idx = jnp.arange(0, DIM_HEAD, 2, dtype=jnp.float32)
            inv_freq = 1.0 / 10000.0 ** (half_idx / DIM_HEAD)
            t = jnp.arange(n, dtype=jnp.float32)
            freqs = t[:, None] * inv_freq[None, :]
            freqs = jnp.concatenate([freqs, freqs], axis=-1)
            base = (half_idx + 0.4 * DIM_HEAD) / (1.4 * DIM_HEAD)
            power = (t - n // 2) / float(WINDOW // 2)
            scale = base[None, :] ** power[:, None]
            scale = jnp.concatenate([scale, scale], axis=-1)
            cos, sin = (jnp.cos(freqs), jnp.sin(freqs))
            q = q * cos * scale + rotate_half(q) * sin * scale
            k = k * cos / scale + rotate_half(k) * sin / scale
            return (q, k)

        def local_attention(q, k, v):
            b, h, n, d = q.shape
            w = n // WINDOW
            bq = q.reshape(b, h, w, WINDOW, d) * QK_SCALE
            bk = k.reshape(b, h, w, WINDOW, d)
            bv = v.reshape(b, h, w, WINDOW, d)

            def look_around(t):
                p = jnp.pad(t, ((0, 0), (0, 0), (1, 0), (0, 0), (0, 0)))
                return jnp.concatenate([p[:, :, :w], p[:, :, 1:]], axis=3)
            bk, bv = (look_around(bk), look_around(bv))
            bt = jnp.arange(n).reshape(w, WINDOW)
            btp = jnp.pad(bt, ((1, 0), (0, 0)), constant_values=-1)
            btk = jnp.concatenate([btp[:w], btp[1:]], axis=1)
            sim = jnp.einsum('bhwid,bhwjd->bhwij', bq, bk)
            i = bt[:, :, None]
            j = btk[:, None, :]
            mask = (i < j) | (i > j + WINDOW) | (j == -1)
            sim = jnp.where(mask, -jnp.finfo(sim.dtype).max, sim)
            attn = jax.nn.softmax(sim, axis=-1)
            out = jnp.einsum('bhwij,bhwjd->bhwid', attn, bv)
            return out.reshape(b, h, n, d)

        def _layer(x, wqkv, qs, ksc, wo, lg, lb, w1, b1, w2, b2):
            b, n, _ = x.shape
            h = shift_token(x)
            qkv = h @ wqkv
            q, k, v = jnp.split(qkv, 3, axis=-1)
            to_heads = lambda t: t.reshape(b, n, HEADS, DIM_HEAD).transpose(0, 2, 1, 3)
            q, k, v = (to_heads(q), to_heads(k), to_heads(v))
            q = l2norm(q) * qs
            k = l2norm(k) * ksc
            q, k = rotary_xpos(q, k)
            o = local_attention(q, k, v)
            o = o.transpose(0, 2, 1, 3).reshape(b, n, INNER)
            x = x + o @ wo
            h = shift_token(x)
            mu = h.mean(-1, keepdims=True)
            var = h.var(-1, keepdims=True)
            h = (h - mu) / jnp.sqrt(var + 1e-05) * lg + lb
            h = h @ w1 + b1
            a, g = jnp.split(h, 2, axis=-1)
            h = a * jax.nn.gelu(g, approximate=False)
            x = x + h @ w2 + b2
            return x
        key = jax.random.key(seed)
        ks = jax.random.split(key, 6)
        return {'x': jax.random.normal(ks[0], (B, N, DIM), jnp.float32), 'wqkv': jax.random.normal(ks[1], (DEPTH, DIM, 3 * INNER), jnp.float32) * 0.02, 'q_scale': jnp.ones((DEPTH, DIM_HEAD), jnp.float32), 'k_scale': jnp.ones((DEPTH, DIM_HEAD), jnp.float32), 'wo': jax.random.normal(ks[2], (DEPTH, INNER, DIM), jnp.float32) * 0.02, 'ln_g': jnp.ones((DEPTH, DIM), jnp.float32), 'ln_b': jnp.zeros((DEPTH, DIM), jnp.float32), 'w1': jax.random.normal(ks[3], (DEPTH, DIM, 2 * HID), jnp.float32) * 0.02, 'b1': jnp.zeros((DEPTH, 2 * HID), jnp.float32), 'w2': jax.random.normal(ks[4], (DEPTH, HID, DIM), jnp.float32) * 0.02, 'b2': jnp.zeros((DEPTH, DIM), jnp.float32)}
    _L0_ffn_in = _L0_ffn_setup()

    def _L1_attn_setup():
        import jax, jax.numpy as jnp
        import numpy as np
        D_MODEL = 128
        N_HEADS = 16
        HEAD_DIM = D_MODEL // N_HEADS
        KV_LATENT = 32
        LN_EPS = 1e-05

        def apply_rope(x):
            b, h, t, d = x.shape
            half = d // 2
            pos = jnp.arange(t, dtype=x.dtype)[:, None]
            inv_freq = 1.0 / 10000.0 ** (jnp.arange(half, dtype=x.dtype) / half)
            angles = pos * inv_freq[None, :]
            sin = jnp.sin(angles)[None, None]
            cos = jnp.cos(angles)[None, None]
            x1, x2 = (x[..., :half], x[..., half:])
            return jnp.concatenate([x1 * cos - x2 * sin, x1 * sin + x2 * cos], axis=-1)
        key = jax.random.key(seed)
        ks = jax.random.split(key, 6)
        d, L = (D_MODEL, KV_LATENT)
        s = 1.0 / np.sqrt(d)
        sl = 1.0 / np.sqrt(L)
        return {'x': jax.random.normal(ks[0], (2, 256, d), dtype=jnp.float32), 'W_q': jax.random.uniform(ks[1], (d, d), jnp.float32, -s, s), 'W_dkv': jax.random.uniform(ks[2], (d, L), jnp.float32, -s, s), 'W_uk': jax.random.uniform(ks[3], (L, d), jnp.float32, -sl, sl), 'W_uv': jax.random.uniform(ks[4], (L, d), jnp.float32, -sl, sl), 'W_o': jax.random.uniform(ks[5], (d, d), jnp.float32, -s, s), 'ln_gamma': jnp.ones((L,), jnp.float32), 'ln_beta': jnp.zeros((L,), jnp.float32)}
    _L1_attn_in = _L1_attn_setup()

    def _L1_ffn_setup():
        import jax, jax.numpy as jnp
        import numpy as np
        DIM = 128
        MOE_INTER = 128
        SHARED_INTER = 128
        N_EXPERTS = 6
        TOP_K = 2
        ROUTE_SCALE = 1.0
        B, S = (8, 512)
        STD = 0.02 / np.sqrt(DIM)
        STD_I = 0.02 / np.sqrt(MOE_INTER)
        key = jax.random.key(seed)
        ks = jax.random.split(key, 10)
        inp = {'x': jax.random.normal(ks[0], (B, S, DIM), dtype=jnp.float32), 'gate_w': jax.random.normal(ks[1], (N_EXPERTS, DIM), dtype=jnp.float32) * STD, 'gate_b': jnp.zeros((N_EXPERTS,), dtype=jnp.float32), 'ew1': jax.random.normal(ks[2], (N_EXPERTS, MOE_INTER, DIM), dtype=jnp.float32) * STD, 'ew2': jax.random.normal(ks[3], (N_EXPERTS, DIM, MOE_INTER), dtype=jnp.float32) * STD_I, 'ew3': jax.random.normal(ks[4], (N_EXPERTS, MOE_INTER, DIM), dtype=jnp.float32) * STD, 'fc1': jax.random.normal(ks[5], (SHARED_INTER, DIM), dtype=jnp.float32) * STD, 'fc2': jax.random.normal(ks[6], (SHARED_INTER, DIM), dtype=jnp.float32) * STD, 'fc3': jax.random.normal(ks[7], (DIM, SHARED_INTER), dtype=jnp.float32) * STD_I}
        return inp
    _L1_ffn_in = _L1_ffn_setup()
    _d = {'L0_attn_x': _L0_attn_in['x'], 'L0_attn_Wq': _L0_attn_in['Wq'], 'L0_attn_Wk': _L0_attn_in['Wk'], 'L0_attn_Wv': _L0_attn_in['Wv'], 'L0_attn_Wb': _L0_attn_in['Wb'], 'L0_attn_Wg': _L0_attn_in['Wg'], 'L0_attn_Wo': _L0_attn_in['Wo'], 'L0_attn_norm_w': _L0_attn_in['norm_w'], 'L0_ffn_wqkv': _L0_ffn_in['wqkv'], 'L0_ffn_q_scale': _L0_ffn_in['q_scale'], 'L0_ffn_k_scale': _L0_ffn_in['k_scale'], 'L0_ffn_wo': _L0_ffn_in['wo'], 'L0_ffn_ln_g': _L0_ffn_in['ln_g'], 'L0_ffn_ln_b': _L0_ffn_in['ln_b'], 'L0_ffn_w1': _L0_ffn_in['w1'], 'L0_ffn_b1': _L0_ffn_in['b1'], 'L0_ffn_w2': _L0_ffn_in['w2'], 'L0_ffn_b2': _L0_ffn_in['b2'], 'L1_attn_W_q': _L1_attn_in['W_q'], 'L1_attn_W_dkv': _L1_attn_in['W_dkv'], 'L1_attn_W_uk': _L1_attn_in['W_uk'], 'L1_attn_W_uv': _L1_attn_in['W_uv'], 'L1_attn_W_o': _L1_attn_in['W_o'], 'L1_attn_ln_gamma': _L1_attn_in['ln_gamma'], 'L1_attn_ln_beta': _L1_attn_in['ln_beta'], 'L1_ffn_gate_w': _L1_ffn_in['gate_w'], 'L1_ffn_gate_b': _L1_ffn_in['gate_b'], 'L1_ffn_ew1': _L1_ffn_in['ew1'], 'L1_ffn_ew2': _L1_ffn_in['ew2'], 'L1_ffn_ew3': _L1_ffn_in['ew3'], 'L1_ffn_fc1': _L1_ffn_in['fc1'], 'L1_ffn_fc2': _L1_ffn_in['fc2'], 'L1_ffn_fc3': _L1_ffn_in['fc3']}
    _x0 = _d['L0_attn_x']
    _d['L0_attn_x'] = jax.random.normal(jax.random.fold_in(jax.random.key(seed), 1), (8, 512, 128), dtype=_x0.dtype)
    del _x0
    return _d

def reference(L0_attn_x, L0_attn_Wq, L0_attn_Wk, L0_attn_Wv, L0_attn_Wb, L0_attn_Wg, L0_attn_Wo, L0_attn_norm_w, L0_ffn_wqkv, L0_ffn_q_scale, L0_ffn_k_scale, L0_ffn_wo, L0_ffn_ln_g, L0_ffn_ln_b, L0_ffn_w1, L0_ffn_b1, L0_ffn_w2, L0_ffn_b2, L1_attn_W_q, L1_attn_W_dkv, L1_attn_W_uk, L1_attn_W_uv, L1_attn_W_o, L1_attn_ln_gamma, L1_attn_ln_beta, L1_ffn_gate_w, L1_ffn_gate_b, L1_ffn_ew1, L1_ffn_ew2, L1_ffn_ew3, L1_ffn_fc1, L1_ffn_fc2, L1_ffn_fc3):

    def _L0_attn_ref(x, Wq, Wk, Wv, Wb, Wg, Wo, norm_w):
        import jax, jax.numpy as jnp
        import numpy as np
        D_MODEL = 128
        H = 4
        DK = 128
        DV = 32
        EPS = 1e-05
        SCALE = DK ** (-0.5)

        def _delta_rule(q, k, v, beta):
            b = q.shape[0]
            qt = jnp.moveaxis(q, 1, 0)
            kt = jnp.moveaxis(k, 1, 0)
            vt = jnp.moveaxis(v, 1, 0)
            bt = jnp.moveaxis(beta, 1, 0)
            S0 = jnp.zeros((b, H, DK, DV), q.dtype)

            def step(S, inp):
                q_t, k_t, v_t, b_t = inp
                pred = jnp.einsum('bhk,bhkv->bhv', k_t, S)
                delta = (v_t - pred) * b_t[..., None]
                S = S + k_t[..., :, None] * delta[..., None, :]
                o_t = jnp.einsum('bhk,bhkv->bhv', q_t, S)
                return (S, o_t)
            _, o = jax.lax.scan(step, S0, (qt, kt, vt, bt))
            return jnp.moveaxis(o, 0, 1)
        b, n, _ = x.shape
        q = (x @ Wq).reshape(b, n, H, DK)
        k = (x @ Wk).reshape(b, n, H, DK)
        v = (x @ Wv).reshape(b, n, H, DV)
        beta = jax.nn.sigmoid(x @ Wb)
        k = k * jax.lax.rsqrt(jnp.sum(k * k, axis=-1, keepdims=True) + 1e-12)
        q = q * SCALE
        o = _delta_rule(q, k, v, beta)
        g = (x @ Wg).reshape(b, n, H, DV)
        o = o * jax.lax.rsqrt(jnp.mean(o * o, axis=-1, keepdims=True) + EPS) * norm_w
        o = o * (g * jax.nn.sigmoid(g))
        return o.reshape(b, n, H * DV) @ Wo

    def _L0_ffn_ref(x, wqkv, q_scale, k_scale, wo, ln_g, ln_b, w1, b1, w2, b2):
        import jax, jax.numpy as jnp
        import numpy as np
        DIM = 128
        DEPTH = 2
        HEADS = 8
        DIM_HEAD = 64
        WINDOW = 64
        INNER = HEADS * DIM_HEAD
        HID = int(DIM * 4 * 2 / 3)
        B, N = (2, 1024)
        QK_SCALE = 8.0

        def shift_token(t):
            t1, t2 = jnp.split(t, 2, axis=-1)
            t2 = jnp.pad(t2, ((0, 0), (1, 0), (0, 0)))[:, :-1]
            return jnp.concatenate([t1, t2], axis=-1)

        def l2norm(t):
            return t / jnp.clip(jnp.linalg.norm(t, axis=-1, keepdims=True), 1e-12)

        def rotate_half(x):
            x1, x2 = jnp.split(x, 2, axis=-1)
            return jnp.concatenate([-x2, x1], axis=-1)

        def rotary_xpos(q, k):
            n = q.shape[-2]
            half_idx = jnp.arange(0, DIM_HEAD, 2, dtype=jnp.float32)
            inv_freq = 1.0 / 10000.0 ** (half_idx / DIM_HEAD)
            t = jnp.arange(n, dtype=jnp.float32)
            freqs = t[:, None] * inv_freq[None, :]
            freqs = jnp.concatenate([freqs, freqs], axis=-1)
            base = (half_idx + 0.4 * DIM_HEAD) / (1.4 * DIM_HEAD)
            power = (t - n // 2) / float(WINDOW // 2)
            scale = base[None, :] ** power[:, None]
            scale = jnp.concatenate([scale, scale], axis=-1)
            cos, sin = (jnp.cos(freqs), jnp.sin(freqs))
            q = q * cos * scale + rotate_half(q) * sin * scale
            k = k * cos / scale + rotate_half(k) * sin / scale
            return (q, k)

        def local_attention(q, k, v):
            b, h, n, d = q.shape
            w = n // WINDOW
            bq = q.reshape(b, h, w, WINDOW, d) * QK_SCALE
            bk = k.reshape(b, h, w, WINDOW, d)
            bv = v.reshape(b, h, w, WINDOW, d)

            def look_around(t):
                p = jnp.pad(t, ((0, 0), (0, 0), (1, 0), (0, 0), (0, 0)))
                return jnp.concatenate([p[:, :, :w], p[:, :, 1:]], axis=3)
            bk, bv = (look_around(bk), look_around(bv))
            bt = jnp.arange(n).reshape(w, WINDOW)
            btp = jnp.pad(bt, ((1, 0), (0, 0)), constant_values=-1)
            btk = jnp.concatenate([btp[:w], btp[1:]], axis=1)
            sim = jnp.einsum('bhwid,bhwjd->bhwij', bq, bk)
            i = bt[:, :, None]
            j = btk[:, None, :]
            mask = (i < j) | (i > j + WINDOW) | (j == -1)
            sim = jnp.where(mask, -jnp.finfo(sim.dtype).max, sim)
            attn = jax.nn.softmax(sim, axis=-1)
            out = jnp.einsum('bhwij,bhwjd->bhwid', attn, bv)
            return out.reshape(b, h, n, d)

        def _layer(x, wqkv, qs, ksc, wo, lg, lb, w1, b1, w2, b2):
            b, n, _ = x.shape
            h = shift_token(x)
            qkv = h @ wqkv
            q, k, v = jnp.split(qkv, 3, axis=-1)
            to_heads = lambda t: t.reshape(b, n, HEADS, DIM_HEAD).transpose(0, 2, 1, 3)
            q, k, v = (to_heads(q), to_heads(k), to_heads(v))
            q = l2norm(q) * qs
            k = l2norm(k) * ksc
            q, k = rotary_xpos(q, k)
            o = local_attention(q, k, v)
            o = o.transpose(0, 2, 1, 3).reshape(b, n, INNER)
            x = x + o @ wo
            h = shift_token(x)
            mu = h.mean(-1, keepdims=True)
            var = h.var(-1, keepdims=True)
            h = (h - mu) / jnp.sqrt(var + 1e-05) * lg + lb
            h = h @ w1 + b1
            a, g = jnp.split(h, 2, axis=-1)
            h = a * jax.nn.gelu(g, approximate=False)
            x = x + h @ w2 + b2
            return x
        for l in range(DEPTH):
            x = _layer(x, wqkv[l], q_scale[l], k_scale[l], wo[l], ln_g[l], ln_b[l], w1[l], b1[l], w2[l], b2[l])
        return x

    def _L1_attn_ref(x, W_q, W_dkv, W_uk, W_uv, W_o, ln_gamma, ln_beta):
        import jax, jax.numpy as jnp
        import numpy as np
        D_MODEL = 128
        N_HEADS = 16
        HEAD_DIM = D_MODEL // N_HEADS
        KV_LATENT = 32
        LN_EPS = 1e-05

        def apply_rope(x):
            b, h, t, d = x.shape
            half = d // 2
            pos = jnp.arange(t, dtype=x.dtype)[:, None]
            inv_freq = 1.0 / 10000.0 ** (jnp.arange(half, dtype=x.dtype) / half)
            angles = pos * inv_freq[None, :]
            sin = jnp.sin(angles)[None, None]
            cos = jnp.cos(angles)[None, None]
            x1, x2 = (x[..., :half], x[..., half:])
            return jnp.concatenate([x1 * cos - x2 * sin, x1 * sin + x2 * cos], axis=-1)
        b, t, _ = x.shape
        q = (x @ W_q).reshape(b, t, N_HEADS, HEAD_DIM).transpose(0, 2, 1, 3)
        lat = x @ W_dkv
        mu = jnp.mean(lat, axis=-1, keepdims=True)
        var = jnp.mean(jnp.square(lat - mu), axis=-1, keepdims=True)
        lat = (lat - mu) * jax.lax.rsqrt(var + LN_EPS) * ln_gamma + ln_beta
        k = (lat @ W_uk).reshape(b, t, N_HEADS, HEAD_DIM).transpose(0, 2, 1, 3)
        v = (lat @ W_uv).reshape(b, t, N_HEADS, HEAD_DIM).transpose(0, 2, 1, 3)
        q = apply_rope(q)
        k = apply_rope(k)
        scores = jnp.einsum('bhqd,bhkd->bhqk', q, k) / jnp.sqrt(jnp.float32(HEAD_DIM))
        causal = jnp.tril(jnp.ones((t, t), dtype=bool))
        scores = jnp.where(causal[None, None], scores, -jnp.inf)
        attn = jax.nn.softmax(scores, axis=-1)
        out = jnp.einsum('bhqk,bhkd->bhqd', attn, v)
        out = out.transpose(0, 2, 1, 3).reshape(b, t, D_MODEL)
        return out @ W_o

    def _L1_ffn_ref(x, gate_w, gate_b, ew1, ew2, ew3, fc1, fc2, fc3):
        import jax, jax.numpy as jnp
        import numpy as np
        DIM = 128
        MOE_INTER = 128
        SHARED_INTER = 128
        N_EXPERTS = 6
        TOP_K = 2
        ROUTE_SCALE = 1.0
        B, S = (8, 512)
        STD = 0.02 / np.sqrt(DIM)
        STD_I = 0.02 / np.sqrt(MOE_INTER)
        orig_shape = x.shape
        xt = x.reshape(-1, DIM)
        logits = xt @ gate_w.T + gate_b
        probs = jax.nn.sigmoid(logits)
        w, idx = jax.lax.top_k(probs, TOP_K)
        w = w / (jnp.sum(w, axis=-1, keepdims=True) + 1e-08)
        w = w * ROUTE_SCALE
        ge = jnp.sum(jax.nn.one_hot(idx, N_EXPERTS, dtype=w.dtype) * w[..., None], axis=1)
        y = jnp.zeros_like(xt)
        for e in range(N_EXPERTS):
            h = jax.nn.silu(xt @ ew1[e].T) * (xt @ ew3[e].T)
            y = y + ge[:, e:e + 1] * (h @ ew2[e].T)
        z = jax.nn.silu(xt @ fc1.T) * (xt @ fc2.T) @ fc3.T
        return (y + z).reshape(orig_shape)
    x = L0_attn_x
    xn = _layernorm(x, axis=-1)
    x = x + _L0_attn_ref(xn, L0_attn_Wq, L0_attn_Wk, L0_attn_Wv, L0_attn_Wb, L0_attn_Wg, L0_attn_Wo, L0_attn_norm_w) + _L0_ffn_ref(xn, L0_ffn_wqkv, L0_ffn_q_scale, L0_ffn_k_scale, L0_ffn_wo, L0_ffn_ln_g, L0_ffn_ln_b, L0_ffn_w1, L0_ffn_b1, L0_ffn_w2, L0_ffn_b2)
    xn = _layernorm(x, axis=-1)
    x = x + _L1_attn_ref(xn, L1_attn_W_q, L1_attn_W_dkv, L1_attn_W_uk, L1_attn_W_uv, L1_attn_W_o, L1_attn_ln_gamma, L1_attn_ln_beta) + _L1_ffn_ref(xn, L1_ffn_gate_w, L1_ffn_gate_b, L1_ffn_ew1, L1_ffn_ew2, L1_ffn_ew3, L1_ffn_fc1, L1_ffn_fc2, L1_ffn_fc3)
    return x

_drawn_inputs = setup_inputs


def setup_inputs(seed=0):
    import zlib

    import numpy as np

    out = dict(_drawn_inputs(seed))
    spreads = {'L0_attn_norm_w': (1.0, 0.6),
     'L0_ffn_q_scale': (1.0, 0.6),
     'L0_ffn_k_scale': (1.0, 0.6),
     'L0_ffn_ln_g': (1.0, 0.6),
     'L0_ffn_ln_b': (0.0, 0.8),
     'L0_ffn_b1': (0.0, 0.8),
     'L0_ffn_b2': (0.0, 0.434),
     'L1_attn_ln_gamma': (1.0, 0.6),
     'L1_attn_ln_beta': (0.0, 2.0),
     'L1_ffn_gate_b': (0.0, 2.0)}
    factors = {'L0_ffn_wqkv': 3.745,
     'L0_ffn_wo': 3.728,
     'L0_ffn_w1': 6.189,
     'L0_ffn_w2': 6.101,
     'L1_attn_W_q': 18.468,
     'L1_attn_W_dkv': 2.713,
     'L1_attn_W_uk': 18.116,
     'L1_ffn_gate_w': 64.0,
     'L1_ffn_ew1': 64.0,
     'L1_ffn_ew2': 64.0,
     'L1_ffn_ew3': 64.0,
     'L1_ffn_fc1': 64.0,
     'L1_ffn_fc2': 64.0,
     'L1_ffn_fc3': 64.0,
     'L0_attn_Wq': 2.878,
     'L0_attn_Wk': 2.881,
     'L0_attn_Wv': 2.891,
     'L0_attn_Wb': 8.0,
     'L0_attn_Wg': 2.99,
     'L0_attn_Wo': 2.842}
    for name, (base, spread) in spreads.items():
        noise = np.random.default_rng([zlib.crc32(name.encode()), seed]).standard_normal(out[name].shape)
        drawn = base * np.exp(spread * noise) if base else spread * noise
        out[name] = jnp.asarray(drawn.astype(out[name].dtype))
    for name, factor in factors.items():
        out[name] = (out[name] * factor).astype(out[name].dtype)
    return out
```

```python
from contextlib import ExitStack

import numpy as np

import concourse.bass as bass
from concourse import mybir

ALU = mybir.AluOpType
ACT = mybir.ActivationFunctionType
AX = mybir.AxisListType.X
F32 = mybir.dt.float32
BF16 = mybir.dt.bfloat16
I32 = mybir.dt.int32

P = 128
BATCH, T, D = 8, 512, 128
NT = T // P
H0, DK, DV = 4, 128, 32
DEPTH, HF, DF, WIN = 2, 8, 64, 64
HID = D * 4 * 2 // 3
HM, DM, LAT = 16, 8, 32
NE = 6
LEVELS = 7
NEG = -1e30
EPS = 1e-5
NPAIR = HF // 2
VW = 32
GROUP = 4
NROW = NT * GROUP
LEAD = 7
PT_SLOTS = 6
HID_TILES = [(j * P, min(P, HID - j * P)) for j in range((HID + P - 1) // P)]



def weight_layout():
    w = [("wk", H0 * DK), ("wq", H0 * DK), ("wv", H0 * DV), ("wbg", H0 + H0 * DV), ("wo0", D)]
    for l in range(DEPTH):
        w += [(f"wqkv{l}", 3 * HF * DF), (f"wof{l}", 4 * D), (f"w1{l}", 2 * HID), (f"w2{l}", 3 * D), (f"cols{l}", 9)]
    w += [("Wq", D), ("Wqr", D), ("Wdkv", LAT), ("Wuk", D), ("Wukr", D), ("Wuv", D), ("Wo", D), ("latcols", 2)]
    w += [("gate", NE)]
    w += [(f"e{n}{i}", D) for i in range(NE + 1) for n in ("u", "w", "d")]
    return w


CONST_LAYOUT = [("ident", P), ("strict", P), ("upper", P),
                ("qcos", NT * DF), ("qsin", NT * DF), ("kcos", NT * DF), ("ksin", NT * DF),
                ("rcos", T), ("rsin", T), ("tri", NE * NE)]
BF_LAYOUT = [("identb", P), ("band", 192), ("causal", P), ("causalT", P),
             ("low", P), ("lowT", LEVELS * P)]


def offsets(layout):
    at, out = 0, {}
    for name, n in layout:
        out[name] = (at, n)
        at += n
    return out, at


def constants():
    f = np.float32
    i, j = np.arange(P)[:, None], np.arange(P)[None, :]
    c = {"ident": np.eye(P, dtype=f), "strict": (j < i).astype(f), "upper": -(i <= j).astype(f)}
    low = [-((i >> (k + 1) == j >> (k + 1)) & ((i >> k) & 1 == 1) & ((j >> k) & 1 == 0)).astype(f) for k in range(LEVELS)]
    half = np.arange(0, DF, 2, dtype=f)
    inv = (f(1) / f(10000) ** (half / f(DF))).astype(f)
    t = np.arange(T, dtype=f)
    ang = np.concatenate([t[:, None] * inv[None]] * 2, 1)
    base = ((half + f(0.4 * DF)) / f(1.4 * DF)).astype(f)
    scale = np.concatenate([base[None] ** ((t - T // 2) / f(WIN // 2))[:, None]] * 2, 1).astype(f)
    sign = np.where(np.arange(DF) < DF // 2, f(-1), f(1))[None]
    cos, sin = np.cos(ang), np.sin(ang) * sign
    tiles = lambda a: a.astype(f).reshape(NT, P, DF).transpose(1, 0, 2).reshape(P, NT * DF)
    c["qcos"], c["qsin"] = tiles(8 * cos * scale), tiles(8 * sin * scale)
    c["kcos"], c["ksin"] = tiles(cos / scale), tiles(sin / scale)
    hd = DM // 2
    inv = (f(1) / f(10000) ** (np.arange(hd, dtype=f) / f(hd))).astype(f)
    d = np.arange(D) % DM
    ang = inv[d % hd][:, None] * t[None]
    c["rcos"] = np.cos(ang).astype(f)
    c["rsin"] = (np.sin(ang) * np.where(d < hd, -1, 1)[:, None]).astype(f)
    e = np.arange(NE)
    c["tri"] = np.broadcast_to((e[None] < e[:, None]).astype(f).reshape(1, -1), (P, NE * NE))
    packed = np.concatenate([c[n].astype(f) for n, _ in CONST_LAYOUT], 1)
    key = np.arange(192)[None] - 64
    b = {"identb": np.eye(P), "band": np.where((key <= i) & (key >= i - WIN), 0, NEG),
         "causal": np.where(j <= i, 0, NEG), "causalT": np.where(i <= j, 0, NEG),
         "low": low[0], "lowT": np.concatenate([m.T for m in low], 1)}
    return np.ascontiguousarray(packed), np.concatenate([b[n].astype(f) for n, _ in BF_LAYOUT], 1)


def build(nc, x, weights, rows, consts, consts_bf, row_fill, parts_dram, out):
    W_AT, W_N = offsets(weight_layout())
    C_AT, C_N = offsets(CONST_LAYOUT)
    B_AT, B_N = offsets(BF_LAYOUT)
    R_AT, R_N = offsets([("norm_w", DV), ("qs", DEPTH * DF), ("ks", DEPTH * DF), ("gate_b", NE)])

    with ExitStack() as ctx:
        def sb(name, n, dt=F32):
            return ctx.enter_context(nc.sbuf_tensor(name, [P, n], dt))

        w_sb, c_sb, b_sb, r_sb = sb("w_sb", W_N), sb("c_sb", C_N), sb("b_sb", B_N, BF16), sb("r_sb", R_N)

        def W(name):
            a, n = W_AT[name]
            return w_sb[:, a:a + n]

        def C(name):
            a, n = C_AT[name]
            return c_sb[:, a:a + n]

        def B(name):
            a, n = B_AT[name]
            return b_sb[:, a:a + n]

        def R(name):
            a, n = R_AT[name]
            return r_sb[:, a:a + n]

        def v3(ap, a):
            return ap.rearrange("p (a b) -> p a b", a=a)

        def v4(ap, a, b):
            return ap.rearrange("p (a b c) -> p a b c", a=a, b=b)

        def spread(ap, n):
            return ap[:, :, None].to_broadcast([ap.shape[0], ap.shape[1], n])

        def repeat(ap, n):
            return ap[:, None, :].to_broadcast([ap.shape[0], n, ap.shape[1]])

        tab = {n: [sb(f"tab_{n}", NT * DF)[:, :], C(c)] for n, c in (("qc", "qcos"), ("qs", "qsin"), ("kc", "kcos"), ("ks", "ksin"))}
        norm_w = sb("norm_w_neg", H0 * DV)

        x_tm, norm_tm, xnT, r1T, r2T = sb("x_tm", T), sb("norm_tm", T), sb("xnT", T), sb("r1T", T), sb("r2T", T)
        hT, h2T = sb("hT", T), sb("h2T", T)
        qTz = sb("qTz", 2 * HF * P)
        p_sb, o_sb, gl, hm = sb("p_sb", 2 * T), sb("o_sb", 2 * T), sb("gl", 2 * T), sb("hm", 3 * T)
        oT0, latT = sb("oT0", T), sb("latT", T)
        NBG = H0 + H0 * DV
        stats, mv = sb("stats", NT * 6), sb("mv", NT * 2)
        rs_in, rs_tmp, rs_out = sb("rs_in", 2 * NT), sb("rs_tmp", 16), sb("rs_out", 16)
        kss, krs, beta = sb("kss", NT * H0), sb("krs", NT * H0), sb("beta", NT * H0)
        oss, ors = sb("oss", NT * H0), sb("ors", NT * H0)
        qk_ss, qk_rs = sb("qk_ss", 2 * 16), sb("qk_rs", 2 * 16)
        R_sb, U_sb, Sn = sb("R_sb", P), sb("U_sb", P), sb("Sn", H0 * DV)
        nmax, psums, prec = sb("nmax", NT * HF), sb("psums", NT * HF), sb("prec", NT * HF)
        nmx, mparts, mres = sb("nmx", NT * HM), sb("mparts", 3 * P, BF16), sb("mres", P)
        at_rec, gz, gp, gw_, ge = sb("at_rec", NT * GROUP), sb("gz", 24), sb("gp", 24), sb("gw_", 24), sb("ge", 24)
        gcmp, geq, grank, gsum = sb("gcmp", NT * 36), sb("geq", NT * 36), sb("grank", 24), sb("gsum", 2 * NT)
        PTW = NT * (NT + 1) // 2 * P
        layer0 = [("kn", NT * T), ("kT", NT * T), ("qT", NT * T), ("oTf", 2 * T), ("q_f", 2 * T), ("k_f", 2 * T), ("v_f", NT * T),
                  ("kTf", NPAIR * T), ("pT", 2 * T), ("rot", 2 * T), ("gs", T), ("th", NT * NBG), ("o_all", T), ("hnT", T),
                  ("Z", NT * T), ("Bm", T), ("L", 2 * T), ("X", 2 * T), ("Vm", 2 * T)]
        layer1 = [("Qst", HM * T // 2), ("Kst", HM * T // 2), ("qkf", 2 * T), ("res", 2 * T), ("parts", 3 * T), ("rope", 2 * T),
                  ("lat_tm", NT * LAT), ("he", 2 * T), ("vaug", NT * HM * VW), ("PTm", PT_SLOTS * PTW)]
        at0, n0 = offsets(layer0)
        at1, n1 = offsets(layer1)
        shared = sb("shared", max(n0, n1))
        kn, kT, qT, oTf, q_f, k_f, v_f, kTf, pT, rot, gs, th, o_all, hnT, Z, Bm, L, X, Vm = (
            shared[:, a:a + n] for a, n in at0.values())
        Qst, Kst, qkf, res, parts, rope_sb, lat_tm, he, vaug, PTm = (shared[:, a:a + n] for a, n in at1.values())
        Qst32, Kst32 = Qst, Kst
        Qst, Kst, parts = Qst.bitcast(BF16), Kst.bitcast(BF16), parts.bitcast(BF16)
        rc, rsn, atg = rope_sb[:, 0:T], rope_sb[:, T:2 * T], rope_sb
        PTm = [PTm[:, i * PTW:(i + 1) * PTW] for i in range(PT_SLOTS)]
        rot = [rot[:, 0:T], rot[:, T:2 * T]]
        the, se, x1_tm, xn2T, at_tm = o_sb, gl, r1T, xnT, r2T
        aT, acc, fin = hm[:, 0:T], hm[:, T:2 * T], hm[:, 2 * T:3 * T]

        bank = [ctx.enter_context(nc.psum_tensor(f"bank{i}", [P, 512], F32)) for i in range(8)]
        BANKS = {
            "normT": lambda n: (3, 4, 4, 4)[n], "k": lambda c: c % 3, "qT": lambda h: (NT + h) % 3,
            "bg": lambda c: (2 * NT + c) % 3, "kT": lambda c: 3 * NT % 3 + c % 3, "G": lambda c: c % 2,
            "V": lambda k, c: c % 2, "VX": lambda k, c: c % 2, "ZV": lambda k, c: 2,
            "B": lambda c: 0, "P": lambda c: 1, "U": lambda c: 2, "O": lambda c: 1, "dS": lambda c: 2, "oT0": lambda: 0,
            "fq": lambda l, c: 3, "fk": lambda l, c: 4, "fv": lambda l, c: 5, "fqT": lambda l, c: 3, "fkT": lambda l, c: 4,
            "fS": lambda l, i: 3 + i % 2, "fPT": lambda l, i: 5, "fO": lambda l, c: 6, "foT": lambda l, c: 5,
            "fwo": lambda l: 7, "h2tm": lambda l: 3, "fg": lambda l, j: (3, 5, 3)[j], "fa": lambda l, j: (4, 6, 4)[j],
            "fw2": lambda l: 7, "x1": lambda: 3,
            "lat": lambda: 5, "latT": lambda: 6, "mq": lambda i: 3 + i, "mv": lambda: 7, "mS": lambda h, t: 3 + t,
            "mrow": lambda g: 7, "mST": lambda h, t: t, "mPV": lambda g: 6, "matg": lambda g: 6, "aT": lambda: 7,
            "gate": lambda: 0, "eu": lambda e: 0, "ew": lambda e: 1, "ey": lambda e: 2, "fin": lambda: 3}

        def place(name, *i):
            return bank[BANKS[name](*i)]

        setup_loads = ctx.enter_context(nc.semaphore("setup_loads"))
        zeroed, tables_done = ctx.enter_context(nc.semaphore("zeroed")), ctx.enter_context(nc.semaphore("tables_done"))
        signals = []

        def semaphore(name):
            signals.append(ctx.enter_context(nc.semaphore(name)))
            return signals[-1]

        x_loaded = semaphore("x_loaded")
        norm_done = semaphore("norm_done")
        normT_psum = semaphore("normT_psum")
        xnT_copied = semaphore("xnT_copied")
        h_done = semaphore("h_done")
        r_done = semaphore("r_done")
        k_psum = semaphore("k_psum")
        k_copied = semaphore("k_copied")
        ksq_done = semaphore("ksq_done")
        kss_done = semaphore("kss_done")
        krs_done = semaphore("krs_done")
        kn_done = semaphore("kn_done")
        kT_psum = semaphore("kT_psum")
        kT_copied = semaphore("kT_copied")
        qT_psum = semaphore("qT_psum")
        qT_copied = semaphore("qT_copied")
        bg_psum = semaphore("bg_psum")
        th_done = semaphore("th_done")
        beta_done = semaphore("beta_done")
        gs_done = semaphore("gs_done")
        G_psum = semaphore("G_psum")
        L_done = semaphore("L_done")
        B_psum = semaphore("B_psum")
        Bm_done = semaphore("Bm_done")
        V_psum = semaphore("V_psum")
        Vm_done = semaphore("Vm_done")
        ZV_psum = semaphore("ZV_psum")
        VX_psum = semaphore("VX_psum")
        Z_done = semaphore("Z_done")
        X_done = semaphore("X_done")
        P_psum = semaphore("P_psum")
        R_done = semaphore("R_done")
        U_psum = semaphore("U_psum")
        U_copied = semaphore("U_copied")
        O_psum = semaphore("O_psum")
        o_copied = semaphore("o_copied")
        dS_psum = semaphore("dS_psum")
        S_done = semaphore("S_done")
        osq_done = semaphore("osq_done")
        ors_done = semaphore("ors_done")
        on_done = semaphore("on_done")
        og_done = semaphore("og_done")
        oT0_psum = semaphore("oT0_psum")
        oT0_copied = semaphore("oT0_copied")
        fq_psum = semaphore("fq_psum")
        fk_psum = semaphore("fk_psum")
        fv_psum = semaphore("fv_psum")
        fv_copied = semaphore("fv_copied")
        fsq_done = semaphore("fsq_done")
        fss_done = semaphore("fss_done")
        ft1_done = semaphore("ft1_done")
        frot_done = semaphore("frot_done")
        fsum_done = semaphore("fsum_done")
        frs_done = semaphore("frs_done")
        fn_done = semaphore("fn_done")
        fqT_psum = semaphore("fqT_psum")
        fkT_psum = semaphore("fkT_psum")
        fqT_lo = semaphore("fqT_lo")
        fqT_hi = semaphore("fqT_hi")
        fkT_copied = semaphore("fkT_copied")
        fS_psum = semaphore("fS_psum")
        fmax_done = semaphore("fmax_done")
        fexp_done = semaphore("fexp_done")
        fPT_psum = semaphore("fPT_psum")
        fPT_copied = semaphore("fPT_copied")
        fO_psum = semaphore("fO_psum")
        fo_done = semaphore("fo_done")
        foT_psum = semaphore("foT_psum")
        foT_copied = semaphore("foT_copied")
        fwo_psum = semaphore("fwo_psum")
        r1_done = semaphore("r1_done")
        h2_done = semaphore("h2_done")
        h2tm_psum = semaphore("h2tm_psum")
        hn_done = semaphore("hn_done")
        fa_psum = semaphore("fa_psum")
        fg_psum = semaphore("fg_psum")
        gelu_done = semaphore("gelu_done")
        hm_done = semaphore("hm_done")
        fw2_psum = semaphore("fw2_psum")
        x1_psum = semaphore("x1_psum")
        x1_done = semaphore("x1_done")
        xn2_copied = semaphore("xn2_copied")
        lat_psum = semaphore("lat_psum")
        lat_done = semaphore("lat_done")
        latT_psum = semaphore("latT_psum")
        latT_done = semaphore("latT_done")
        mq_psum = semaphore("mq_psum")
        rope_done = semaphore("rope_done")
        qkf_done = semaphore("qkf_done")
        split_done = semaphore("split_done")
        split2_done = semaphore("split2_done")
        parts_kept = semaphore("parts_kept")
        parts_sent = semaphore("parts_sent")
        rows_filled = semaphore("rows_filled")
        mv_psum = semaphore("mv_psum")
        vaug_done = semaphore("vaug_done")
        vaug_zeroed = semaphore("vaug_zeroed")
        mS_psum = semaphore("mS_psum")
        nmx_done = semaphore("nmx_done")
        mrow_psum = semaphore("mrow_psum")
        mrow_done = semaphore("mrow_done")
        mrow_sent = semaphore("mrow_sent")
        mST_psum = semaphore("mST_psum")
        mexp_done = semaphore("mexp_done")
        mPV_psum = semaphore("mPV_psum")
        atg_done = semaphore("atg_done")
        matg_psum = semaphore("matg_psum")
        at_done = semaphore("at_done")
        aT_psum = semaphore("aT_psum")
        aT_copied = semaphore("aT_copied")
        gate_psum = semaphore("gate_psum")
        gz_done = semaphore("gz_done")
        gexp_done = semaphore("gexp_done")
        ge_done = semaphore("ge_done")
        eu_psum = semaphore("eu_psum")
        ew_psum = semaphore("ew_psum")
        eth_done = semaphore("eth_done")
        es_done = semaphore("es_done")
        eh_done = semaphore("eh_done")
        ey_psum = semaphore("ey_psum")
        ey_done = semaphore("ey_done")
        fin_psum = semaphore("fin_psum")
        fin_done = semaphore("fin_done")
        out_stored = semaphore("out_stored")
        dve_chain = semaphore("dve_chain")
        numbers = sorted(s.num for s in signals)
        assert numbers == list(range(numbers[0], numbers[0] + len(numbers)))

        with nc.Block(no_gpsimd_drain=True) as block:
            @block.sync
            def _(sp):
                sp.dma_start(c_sb[:], consts).then_inc(setup_loads, 16)
                sp.dma_start(w_sb[:], weights).then_inc(setup_loads, 16)
                sp.dma_start(v3(x_tm[:], NT), x[0:1].rearrange("a (t p) d -> p (a t) d", p=P)).then_inc(setup_loads, 16)
                sp.wait_ge(setup_loads, 16 * 5)

            @block.scalar
            def _(act):
                act.dma_start(shared[:, 0:B_N], consts_bf).then_inc(setup_loads, 16)
                act.dma_start(r_sb[:], rows.to_broadcast([P, R_N])).then_inc(setup_loads, 16)

            @block.gpsimd
            def _(pool):
                for part in (qTz[:], p_sb[:], latT[:], hT[:, 0:1], h2T[:, 0:1]):
                    nc.gpsimd.memset(part, 0.0).then_inc(zeroed, 1)
                pool.wait_ge(zeroed, 5)

            @block.vector
            def _(dve):
                dve.wait_ge(setup_loads, 16 * 5)
                nc.vector.tensor_copy(b_sb[:], shared[:, 0:B_N]).then_inc(tables_done, 1)
                h = DF // 2
                for l in range(DEPTH):
                    for cos, sin, row, c_out, s_out in (("qcos", "qsin", "qs", "qc", "qs"), ("kcos", "ksin", "ks", "kc", "ks")):
                        g = R(row)[:, l * DF:(l + 1) * DF]
                        c_out, s_out = v3(tab[c_out][l], NT), v3(tab[s_out][l], NT)
                        tt, sines = nc.vector.tensor_tensor, v3(C(sin), NT)
                        tt(c_out, v3(C(cos), NT), repeat(g, NT), ALU.mult).then_inc(tables_done, 1)
                        tt(s_out[:, :, 0:h], sines[:, :, 0:h], repeat(g[:, h:], NT), ALU.mult).then_inc(tables_done, 1)
                        tt(s_out[:, :, h:], sines[:, :, h:], repeat(g[:, 0:h], NT), ALU.mult).then_inc(tables_done, 1)
                nc.vector.tensor_scalar(v3(norm_w[:], H0), repeat(R("norm_w"), H0), -0.5 * DK ** -0.5, None, ALU.mult)\
                    .then_inc(tables_done, 1)
                dve.wait_ge(tables_done, 6 * DEPTH + 2)

        def steps_delta():
            s = [("k", c) for c in range(NT)] + [("qT", h) for h in range(H0)] + [("krs",)]
            s += [("bg", c) for c in range(NT)] + [("kT", c) for c in range(NT)]
            for two in ((0, 1), (2, 3)):
                s += [("gram", c) for c in two]
                for k in range(LEVELS):
                    s += [("inv_v", k, c) for c in two]
                    if k:
                        s += [("inv_zx", k, c) for c in two]
            for c in range(NT):
                s += [("seq_b", c), ("seq_p", c), ("seq_u", c), ("seq_o", c)]
            return s + [("delta_norm",), ("oT0",)]

        def steps_ffn(l):
            s = []
            s += [("fqkv", l, 0), ("frs", l, 0), ("fqkv", l, 1), ("frs", l, 1)]
            n = NT * NPAIR
            for i in range(n + 3):
                if i < n:
                    if i % NPAIR == 0:
                        c = i // NPAIR
                        s += [("fT", l, c)] + ([("fqkv", l, c + 2), ("frs", l, c + 2)] if c + 2 < NT else [])
                    s += [("fS", l, i)]
                if 1 <= i <= n:
                    s += [("fPT", l, i - 1)]
                done = (i - 3) // NPAIR if i >= 3 and (i - 3) % NPAIR == NPAIR - 1 else None
                if done is not None:
                    s += [("foT", l, done)]
                if 2 <= i < n + 2:
                    s += [("fPV", l, i - 2)]
                if done is not None:
                    s += [("fwo", l, done)]
            return s + [("fres", l), ("fln", l), ("hnT", l)] + [("fw1", l, j) for j in range(3)] + [("fw2", l)]

        def steps_latent():
            s = []
            for h in range(HM + LEAD):
                if h < HM:
                    s += [("mS", h)]
                    if h % GROUP == GROUP - 1:
                        s += [("mrow", h // GROUP)]
                done = h - LEAD
                if done >= 0:
                    s += [("mST", done)]
                    if done % GROUP == 1 and done > GROUP:
                        s += [("mPV", done // GROUP - 1), ("matg", done // GROUP - 1)]
            return s + [("mPV", HM // GROUP - 1), ("matg", HM // GROUP - 1), ("aT",)]

        def steps_moe():
            return [("gate",)] + [s for e in range(NE + 1) for s in ([("e_up", e), ("e_down", e - 1)] if e else [("e_up", e)])]

        def merge(a, b):
            out, i, j = [], 0, 0
            while i < len(a) or j < len(b):
                if j == len(b) or (i < len(a) and i * len(b) <= j * len(a)):
                    out.append(a[i])
                    i += 1
                else:
                    out.append(b[j])
                    j += 1
            return out

        ffn = steps_ffn(0) + steps_ffn(1)
        schedule = [("ln0",), ("xnT",)] + merge(steps_delta(), ffn) + [("x1",), ("xn2T",)]
        latent, moe = steps_latent(), steps_moe()
        first = latent.index(("mST", 0))
        schedule += [("lat",), ("mq",), ("latT",), ("mk",), ("mv",)] + moe[:7] + merge(latent[:first], moe[7:]) + latent[first:] + [("final",)]

        def walk(parts):
            for name, *args in schedule:
                if name in parts:
                    parts[name](*args)

        def pair(l, i):
            return l * NT * NPAIR + i

        def at_level(k, c, levels, first=0):
            return c // 2 * 2 * levels + 2 * (k - first) + c % 2

        with nc.Fori(0, BATCH) as b:
            with nc.Block(no_gpsimd_drain=True) as block:
                @block.tensor
                def _(pe):
                    mm = nc.tensor.matmul
                    ident = C("ident")
                    def transposes(ps, src, n=4, width=P, last=None):
                        for i in range(n):
                            m = nc.tensor.transpose(ps[0:width, i * P:(i + 1) * P], src(i), ident)
                        return m

                    def xnT_():
                        ps = place("normT", 0)
                        pe.wait_ge(norm_done, 1)
                        transposes(ps, lambda i: v3(norm_tm[:], NT)[:, i]).then_inc(normT_psum, 1)

                    def k(c):
                        if c == 3:
                            pe.wait_ge(ksq_done, 1)
                        ps = place("k", c)
                        pe.wait_ge(xnT_copied, 1)
                        mm(ps[:], xnT[:, c * P:(c + 1) * P], W("wk"), start=True, stop=True).then_inc(k_psum, 1)

                    def qT_(h):
                        if h < 3:
                            pe.wait_ge(ksq_done, h + 2)
                        else:
                            pe.wait_ge(qT_copied, 1)
                        ps = place("qT", h)
                        mm(ps[:], W("wq")[:, h * DK:(h + 1) * DK], xnT[:], start=True, stop=True).then_inc(qT_psum, 1)

                    def bg(c):
                        if c < 3:
                            pe.wait_ge(qT_copied, c + 2)
                        else:
                            pe.wait_ge(gs_done, 1)
                        ps = place("bg", c)
                        mm(ps[:, 0:NBG], xnT[:, c * P:(c + 1) * P], W("wbg"), start=True, stop=True).then_inc(bg_psum, 1)

                    def kT_(c):
                        if c < 3:
                            pe.wait_ge(gs_done, c + 2)
                        else:
                            pe.wait_ge(kT_copied, 1)
                        ps = place("kT", c)
                        pe.wait_ge(kn_done, c + 1)
                        transposes(ps, lambda i: v4(kn[:], NT, H0)[:, c, i]).then_inc(kT_psum, 1)

                    def gram(c):
                        kc = v4(kT[:], NT, H0)[:, c]
                        ps = place("G", c)
                        pe.wait_ge(kT_copied, NT)
                        for h in range(H0):
                            m = mm(ps[:, h * P:(h + 1) * P], kc[:, h], kc[:, h], start=True, stop=True)
                        m.then_inc(G_psum, 1)

                    def seq_b(c):
                        kc = v4(kT[:], NT, H0)[:, c]
                        ps = place("B", c)
                        if c:
                            pe.wait_ge(Bm_done, c)
                        pe.wait_ge(qT_copied, H0)
                        for h in range(H0):
                            m = mm(ps[:, h * P:(h + 1) * P], kc[:, h], qT[:, h * T + c * P:h * T + (c + 1) * P], start=True, stop=True)
                        m.then_inc(B_psum, 1)

                    def inv_v(k, c):
                        n = at_level(k, c, LEVELS)
                        Lc, Zc = v4(L, 2, H0)[:, c % 2], v4(Z, NT, H0)[:, c]
                        ps = place("V", k, c)
                        if k == 0:
                            pe.wait_ge(L_done, c + 1)
                            m = transposes(ps, lambda i: Lc[:, i])
                        else:
                            pe.wait_ge(Z_done, n - 1)
                            if k >= 2:
                                pe.wait_ge(X_done, at_level(k, c, LEVELS - 1) - 1)
                            for h in range(H0):
                                m = mm(ps[:, h * P:(h + 1) * P], Lc[:, h], Zc[:, h], start=True, stop=True)
                        m.then_inc(V_psum, 1)

                    def inv_zx(k, c):
                        n, nx = at_level(k, c, LEVELS), at_level(k, c, LEVELS - 1)
                        Xc, Vc = v4(X, 2, H0)[:, c % 2], v4(Vm, 2, H0)[:, c % 2]
                        pe.wait_ge(Z_done, n)
                        ps = place("ZV", k, c)
                        pe.wait_ge(X_done, nx - 1)
                        pe.wait_ge(Vm_done, n + 1)
                        for h in range(H0):
                            m = mm(ps[:, h * P:(h + 1) * P], Xc[:, h], Vc[:, h], start=True, stop=True)
                        m.then_inc(ZV_psum, 1)
                        if k < LEVELS - 1:
                            ps = place("VX", k, c)
                            for h in range(H0):
                                m = mm(ps[:, h * P:(h + 1) * P], Vc[:, h], Xc[:, h], start=True, stop=True)
                            m.then_inc(VX_psum, 1)

                    def seq_p(c):
                        if c:
                            pe.wait_ge(o_copied, c)
                        ps = place("P", c)
                        m = mm(ps[:, 0:P], xnT[:, c * P:(c + 1) * P], W("wv"), start=True, stop=c == 0, skip_group_check=True)
                        if c:
                            pe.wait_ge(S_done, c)
                            for h in range(H0):
                                m = mm(ps[:, h * DV:(h + 1) * DV], v4(kT[:], NT, H0)[:, c, h], Sn[:, h * DV:(h + 1) * DV],
                                       start=False, stop=True, skip_group_check=True)
                        m.then_inc(P_psum, 1)

                    def seq_u(c):
                        if c == 0:
                            pe.wait_ge(Z_done, LEVELS * NT)
                        ps = place("U", c)
                        pe.wait_ge(R_done, c + 1)
                        pe.wait_ge(Z_done, at_level(LEVELS - 1, c, LEVELS) + 1)
                        for h in range(H0):
                            m = mm(ps[:, h * DV:(h + 1) * DV], v4(Z, NT, H0)[:, c, h], R_sb[:, h * DV:(h + 1) * DV], start=True, stop=True)
                        m.then_inc(U_psum, 1)

                    def seq_o(c):
                        pe.wait_ge(U_copied, c + 1)
                        pe.wait_ge(Bm_done, c + 1)
                        ps = place("O", c)
                        for h in range(H0):
                            u = U_sb[:, h * DV:(h + 1) * DV]
                            m = mm(ps[:, h * DV:(h + 1) * DV], v3(Bm, H0)[:, h], u, start=True, stop=c == 0)
                            if c:
                                m = mm(ps[:, h * DV:(h + 1) * DV], qT[:, h * T + c * P:h * T + (c + 1) * P],
                                       Sn[:, h * DV:(h + 1) * DV], start=False, stop=True)
                        m.then_inc(O_psum, 1)
                        if c < NT - 1:
                            ps = place("dS", c)
                            for h in range(H0):
                                m = mm(ps[:, h * DV:(h + 1) * DV], v4(kn[:], NT, H0)[:, c, h], U_sb[:, h * DV:(h + 1) * DV],
                                       start=True, stop=True)
                            m.then_inc(dS_psum, 1)

                    def oT0_():
                        ps = place("oT0")
                        pe.wait_ge(og_done, 1)
                        transposes(ps, lambda i: v3(o_all[:], NT)[:, i]).then_inc(oT0_psum, 1)

                    def fqkv(l, c):
                        n = l * NT + c + 1
                        src = hT[:, c * P:(c + 1) * P]
                        pe.wait_ge(h_done, l + 1)
                        w = W(f"wqkv{l}")
                        if c == 1:
                            pe.wait_ge(fsq_done, 2 * n - 3)
                            pe.wait_ge(frot_done, 2 * n - 3)
                        elif c >= 2:
                            pe.wait_ge(fqT_lo, n - 2)
                            pe.wait_ge(fqT_hi, n - 2)
                        mm(place("fq", l, c)[:], src, w[:, 0:T], start=True, stop=True).then_inc(fq_psum, 1)
                        if c == 1:
                            pe.wait_ge(fsq_done, 2 * n - 2)
                            pe.wait_ge(frot_done, 2 * n - 2)
                        elif c >= 2:
                            pe.wait_ge(fkT_copied, n - 2)
                        mm(place("fk", l, c)[:], src, w[:, T:2 * T], start=True, stop=True).then_inc(fk_psum, 1)
                        if c in (1, 2):
                            pe.wait_ge(fv_copied, n - 1)
                        elif c == 3:
                            pe.wait_ge(fPT_copied, pair(l, NPAIR - 2) + 1)
                        mm(place("fv", l, c)[:], src, w[:, 2 * T:3 * T], start=True, stop=True).then_inc(fv_psum, 1)

                    def fT(l, c):
                        n = l * NT + c + 1
                        pe.wait_ge(fn_done, 2 * n)
                        if c == 0:
                            pe.wait_ge(frot_done, 2 * n + 1)
                        else:
                            pe.wait_ge(fexp_done, 2 * pair(l, c * NPAIR - 2) + 2)
                        ps = place("fqT", l, c)
                        transposes(ps, lambda i: v4(q_f[:], 2, 4)[:, c % 2, i]).then_inc(fqT_psum, 1)
                        if c == 0:
                            pe.wait_ge(frot_done, 2 * n + 2)
                        else:
                            pe.wait_ge(fexp_done, 2 * pair(l, c * NPAIR - 1) + 2)
                        ps = place("fkT", l, c)
                        transposes(ps, lambda i: v4(k_f[:], 2, 4)[:, c % 2, i]).then_inc(fkT_psum, 1)

                    def fS(l, i):
                        c, g = divmod(i, NPAIR)
                        n = l * NT + c + 1
                        pe.wait_ge(fqT_lo, n)
                        pe.wait_ge(fqT_hi, n)
                        pe.wait_ge(fkT_copied, n)
                        if g >= 2:
                            pe.wait_ge(fexp_done, 2 * pair(l, i - 2) + 2)
                        elif c + 2 < NT:
                            pe.wait_ge(frot_done, 2 * (n + 2) - 1 + g)
                            pe.wait_ge(fsq_done, 2 * (n + 2) - 1 + g)
                        ps = v3(place("fS", l, i)[:], 2)
                        lo = 128 if c == 0 else 64
                        mm(ps[:, :, lo:256], B("identb"), repeat(B("band")[:, lo - 64:192], 2), start=True, stop=False,
                           skip_group_check=True)
                        keys = kTf[:, g * T + c * P - 128 + lo:g * T + (c + 1) * P]
                        for j in range(2):
                            q = v4(qTz[:], 2, HF)[:, c % 2, 2 * g + j]
                            m = mm(ps[:, j, lo:256], q, keys, start=False, stop=True, skip_group_check=True)
                        m.then_inc(fS_psum, 1)

                    def fPT(l, i):
                        c = i // NPAIR
                        n = pair(l, i) + 1
                        if i in (0, NPAIR - 1):
                            pe.wait_ge(fv_copied, l * NT + (3 if i == 0 else 4))
                        elif i % NPAIR == 2 and c:
                            pe.wait_ge(foT_copied, l * NT + c)
                        else:
                            pe.wait_ge(fPT_copied, n - 1)
                        ps = place("fPT", l, i)
                        pe.wait_ge(fexp_done, 2 * n)
                        p = v4(p_sb[:], 2, 4)[:, i % 2]
                        for j in ((1, 3) if c == 0 else range(4)):
                            m = nc.tensor.transpose(ps[:, j * P:(j + 1) * P], p[:, j], ident)
                        m.then_inc(fPT_psum, 1)

                    def fPV(l, i):
                        c, g = divmod(i, NPAIR)
                        ps = place("fO", l, c)
                        pe.wait_ge(fPT_copied, pair(l, i) + 1)
                        if g == 0:
                            pe.wait_ge(fv_copied, l * NT + c + 1)
                        pt = v4(pT[:], 2, 4)[:, i % 2]
                        for j in range(2):
                            h = 2 * g + j
                            o = ps[:, h * DF:(h + 1) * DF]
                            if c:
                                mm(o, pt[:, 2 * j], v_f[:, (c - 1) * T + h * DF:(c - 1) * T + (h + 1) * DF], start=True, stop=False)
                            m = mm(o, pt[:, 2 * j + 1], v_f[:, c * T + h * DF:c * T + (h + 1) * DF], start=c == 0, stop=True)
                        m.then_inc(fO_psum, 1)

                    def foT(l, c):
                        n = l * NT + c + 1
                        ps = place("foT", l, c)
                        pe.wait_ge(fPT_copied, pair(l, min(c * NPAIR + 5, NT * NPAIR - 1)) + 1)
                        pe.wait_ge(fo_done, n)
                        transposes(ps, lambda i: v4(o_sb[:], 2, 4)[:, c % 2, i]).then_inc(foT_psum, 1)

                    def fwo(l, c):
                        n = l * NT + c + 1
                        pe.wait_ge(foT_copied, n)
                        for j in range(4):
                            m = mm(place("fwo", l)[:, c * P:(c + 1) * P], W(f"wof{l}")[:, j * D:(j + 1) * D],
                                   v4(oTf, 2, 4)[:, c % 2, j], start=j == 0, stop=j == 3)
                        m.then_inc(fwo_psum, 1)

                    def fln(l):
                        ps = place("h2tm", l)
                        pe.wait_ge(h2_done, l + 1)
                        transposes(ps, lambda i: h2T[:, i * P:(i + 1) * P]).then_inc(h2tm_psum, 1)

                    def hnT_(l):
                        ps = place("normT", l + 1)
                        pe.wait_ge(norm_done, l + 2)
                        transposes(ps, lambda i: v3(norm_tm[:], NT)[:, i]).then_inc(normT_psum, 1)

                    def fw1(l, j):
                        at, m = HID_TILES[j]
                        n = 3 * l + j + 1
                        pe.wait_ge(hn_done, l + 1)
                        if j == 2:
                            pe.wait_ge(gelu_done, 3 * l + 1)
                            pe.wait_ge(hm_done, 3 * l + 1)
                        ps = place("fg", l, j)
                        mm(ps[0:m, :], W(f"w1{l}")[:, HID + at:HID + at + m], hnT[:], start=True, stop=True).then_inc(fg_psum, 1)
                        ps = place("fa", l, j)
                        mm(ps[0:m, :], W(f"w1{l}")[:, at:at + m], hnT[:], start=True, stop=True).then_inc(fa_psum, 1)

                    def fw2(l):
                        ps = place("fw2", l)
                        for j, (_, m) in enumerate(HID_TILES):
                            pe.wait_ge(hm_done, 3 * l + j + 1)
                            i = mm(ps[:], W(f"w2{l}")[0:m, j * D:(j + 1) * D], hm[0:m, j * T:(j + 1) * T], start=j == 0, stop=j == 2)
                        i.then_inc(fw2_psum, 1)

                    def x1():
                        ps = place("x1")
                        pe.wait_ge(r_done, DEPTH)
                        pe.wait_ge(oT0_copied, 1)
                        for c in range(NT):
                            o = ps[:, c * P:(c + 1) * P]
                            mm(o, oT0[:, c * P:(c + 1) * P], W("wo0"), start=True, stop=False)
                            m = mm(o, r2T[:, c * P:(c + 1) * P], ident, start=False, stop=True)
                        m.then_inc(x1_psum, 1)

                    def xn2T_():
                        ps = place("normT", 3)
                        pe.wait_ge(norm_done, 4)
                        transposes(ps, lambda i: v3(norm_tm[:], NT)[:, i]).then_inc(normT_psum, 1)

                    def lat():
                        ps = place("lat")
                        pe.wait_ge(xn2_copied, 1)
                        for c in range(NT):
                            m = mm(ps[:, c * LAT:(c + 1) * LAT], xn2T[:, c * P:(c + 1) * P], W("Wdkv"), start=True, stop=True)
                        m.then_inc(lat_psum, 1)

                    def latT_():
                        ps = place("latT")
                        pe.wait_ge(lat_done, 1)
                        transposes(ps, lambda i: v3(lat_tm[:], NT)[:, i], width=LAT).then_inc(latT_psum, 1)

                    def project(first, weights, src):
                        for i, w in enumerate(weights):
                            ps = place("mq", first + i)
                            mm(ps[:], W(w), src, start=True, stop=True).then_inc(mq_psum, 1)

                    def mq():
                        project(0, ("Wq", "Wqr"), xn2T[:])

                    def mk():
                        pe.wait_ge(latT_done, 1)
                        project(2, ("Wuk", "Wukr"), latT[:])

                    def mv_():
                        ps = place("mv")
                        for c in range(NT):
                            m = mm(ps[:, c * P:(c + 1) * P], latT[:, c * P:(c + 1) * P], W("Wuv"), start=True, stop=True)
                        m.then_inc(mv_psum, 1)

                    def mS(h):
                        if h == 0:
                            pe.wait_ge(parts_sent, 12 * 16)
                            pe.wait_ge(rows_filled, 32)
                        for t, tiles in enumerate(((0, 2), (1,), (3,))):
                            if h:
                                pe.wait_ge(nmx_done, 4 * (h - 1) + (2, 3, 4)[t])
                            ps = place("mS", h, t)
                            at = 0
                            for c in tiles:
                                n = (c + 1) * P
                                mm(ps[:, at + c * P:at + n], B("identb"), B("causal"), start=True, stop=False, skip_group_check=True)
                                m = mm(ps[:, at:at + n], Qst[:, h * T + c * P:h * T + (c + 1) * P], Kst[:, h * T:h * T + n],
                                       start=False, stop=True, skip_group_check=True)
                                at += n
                            m.then_inc(mS_psum, 1)

                    def mrow(g):
                        pe.wait_ge(nmx_done, NT * GROUP * (g + 1))
                        if g:
                            pe.wait_ge(mrow_done, g)
                        else:
                            pe.wait_ge(vaug_done, 1)
                        nc.tensor.transpose(place("mrow", g)[0:NROW, 0:P], nmx[:, g * NROW:(g + 1) * NROW], ident)\
                            .then_inc(mrow_psum, 1)

                    def mST(h):
                        if h % GROUP == 0:
                            pe.wait_ge(mrow_sent, 48 * (h // GROUP + 1))
                        if h == 0:
                            pe.wait_ge(es_done, NE + 1)
                            pe.wait_ge(eh_done, NE + 1)
                            pe.wait_ge(ey_done, NE)
                        for t, tiles in enumerate(((0,), (1, 3), (2,))):
                            if h:
                                pe.wait_ge(mexp_done, 3 * (h - 1) + t + 1)
                            ps = place("mST", h, t)
                            at = 0
                            for j in tiles:
                                n = T - j * P
                                mm(ps[:, at:at + P], B("identb"), B("causalT"), start=True, stop=False, skip_group_check=True)
                                m = mm(ps[:, at:at + n], Kst[:, h * T + j * P:h * T + (j + 1) * P], Qst[:, h * T + j * P:(h + 1) * T],
                                       start=False, stop=True, skip_group_check=True)
                                at += n
                            m.then_inc(mST_psum, 1)

                    def mPV(g):
                        if g:
                            pe.wait_ge(at_done, g)
                        ps = place("mPV", g)
                        pe.wait_ge(mexp_done, 3 * GROUP * (g + 1))
                        pe.wait_ge(vaug_done, 1)
                        start = {0: 0, 1: T, 3: 2 * T - P, 2: 2 * T}
                        for j in range(NT):
                            n = T - j * P
                            for i in range(GROUP):
                                h = GROUP * g + i
                                m = mm(ps[VW * i:VW * (i + 1), j * P:T], v3(vaug[:], NT * HM)[:, j * HM + h],
                                       PTm[h % PT_SLOTS][:, start[j]:start[j] + n], start=j == 0, stop=j == NT - 1,
                                       skip_group_check=True)
                        m.then_inc(mPV_psum, 1)

                    def matg(g):
                        ps = place("matg", g)
                        pe.wait_ge(atg_done, g + 1)
                        transposes(ps, lambda i: atg[:, (g % 2) * T + i * P:(g % 2) * T + (i + 1) * P]).then_inc(matg_psum, 1)

                    def aT_():
                        ps = place("aT")
                        pe.wait_ge(at_done, HM // GROUP)
                        transposes(ps, lambda i: v3(at_tm[:], NT)[:, i]).then_inc(aT_psum, 1)

                    def gate():
                        ps = place("gate")
                        pe.wait_ge(xn2_copied, 1)
                        for c in range(NT):
                            m = mm(ps[:, c * NE:(c + 1) * NE], xn2T[:, c * P:(c + 1) * P], W("gate"), start=True, stop=True)
                        m.then_inc(gate_psum, 1)

                    def e_up(e):
                        if e:
                            pe.wait_ge(es_done, e)
                        else:
                            pe.wait_ge(gz_done, 1)
                        ps = place("eu", e)
                        mm(ps[:], W(f"eu{e}"), xn2T[:], start=True, stop=True).then_inc(eu_psum, 1)
                        if e:
                            pe.wait_ge(eh_done, e)
                        ps = place("ew", e)
                        mm(ps[:], W(f"ew{e}"), xn2T[:], start=True, stop=True).then_inc(ew_psum, 1)

                    def e_down(e):
                        if e:
                            pe.wait_ge(ey_done, e)
                        ps = place("ey", e)
                        pe.wait_ge(eh_done, e + 1)
                        for c in range(NT):
                            m = mm(ps[:, c * P:(c + 1) * P], he[:, (e % 2) * T + c * P:(e % 2) * T + (c + 1) * P], W(f"ed{e}"),
                                   start=True, stop=True)
                        m.then_inc(ey_psum, 1)

                    def final():
                        ps = place("fin")
                        pe.wait_ge(eh_done, NE + 1)
                        pe.wait_ge(aT_copied, 1)
                        for c in range(NT):
                            o = ps[:, c * P:(c + 1) * P]
                            s = NE % 2 * T + c * P
                            mm(o, he[:, s:s + P], W(f"ed{NE}"), start=True, stop=False)
                            m = mm(o, aT[:, c * P:(c + 1) * P], W("Wo"), start=False, stop=True)
                        m.then_inc(fin_psum, 1)

                    walk({"xnT": xnT_, "k": k, "qT": qT_, "bg": bg, "kT": kT_, "gram": gram, "inv_v": inv_v, "inv_zx": inv_zx,
                          "seq_b": seq_b, "seq_p": seq_p, "seq_u": seq_u, "seq_o": seq_o, "oT0": oT0_, "fqkv": fqkv, "fT": fT, "fS": fS,
                          "fPT": fPT, "fPV": fPV, "foT": foT, "fwo": fwo, "fln": fln, "hnT": hnT_, "fw1": fw1, "fw2": fw2,
                          "x1": x1, "xn2T": xn2T_, "lat": lat, "latT": latT_, "mq": mq, "mk": mk, "mv": mv_, "mS": mS,
                          "mrow": mrow, "mST": mST, "mPV": mPV, "matg": matg, "aT": aT_, "gate": gate, "e_up": e_up,
                          "e_down": e_down, "final": final})

                @block.scalar
                def _(act):
                    af = nc.scalar.activation


                    def copy_out(dst, key, full, n, done):
                        act.wait_ge(full, n)
                        af(dst, place(*key)[:], ACT.Copy).then_inc(done, 1)

                    def k(c):
                        copy_out(kn[:, c * T:(c + 1) * T], ("k", c), k_psum, c + 1, k_copied)
                        af(kT[:, c * T:(c + 1) * T], place("k", c)[:], ACT.Square).then_inc(ksq_done, 1)

                    def bg(c):
                        act.wait_ge(bg_psum, c + 1)
                        af(th[:, c * NBG:(c + 1) * NBG], place("bg", c)[:, 0:NBG], ACT.Tanh, scale=0.5).then_inc(th_done, 1)

                    def seq_u(c):
                        act.wait_ge(U_psum, c + 1)
                        if c >= 2:
                            act.wait_ge(dS_psum, c)
                        elif c == 1:
                            act.wait_ge(dS_psum, 1)
                        af(U_sb[:], place("U", c)[:, 0:P], ACT.Copy).then_inc(U_copied, 1)

                    def seq_o(c):
                        act.wait_ge(O_psum, c + 1)
                        af(o_all[:, c * P:(c + 1) * P], place("O", c)[:, 0:P], ACT.Copy).then_inc(o_copied, 1)

                    def delta_norm():
                        act.wait_ge(o_copied, NT)
                        af(kn[:, 0:T], o_all[:], ACT.Square).then_inc(osq_done, 1)

                    def fqkv(l, c):
                        n = l * NT + c
                        act.wait_ge(fv_psum, n + 1)
                        if l:
                            act.wait_ge(fO_psum, NT * NPAIR)
                        af(v_f[:, c * T:(c + 1) * T], place("fv", l, c)[:], ACT.Copy).then_inc(fv_copied, 1)
                        for i, name in enumerate(("fq", "fk")):
                            m = 2 * n + i
                            if m >= 2:
                                act.wait_ge(fsum_done, m - 1)
                            af(rot[m % 2][:], place(name, l, c)[:], ACT.Square).then_inc(fsq_done, 1)

                    def fT(l, c):
                        n = l * NT + c
                        act.wait_ge(fqT_psum, n + 1)
                        if n >= 2:
                            act.wait_ge(fS_psum, (n - 1) * NPAIR)
                        half = slice(0, DF)
                        af(v4(qTz[:], 2, HF)[half, c % 2, 0:HF:2], v3(place("fqT", l, c)[:], NPAIR)[half], ACT.Copy).then_inc(fqT_lo, 1)
                        act.wait_ge(fkT_psum, n + 1)
                        if l:
                            act.wait_ge(fS_psum, NT * NPAIR)
                        af(v4(kTf[:], NPAIR, NT)[:, :, c], v3(place("fkT", l, c)[:], NPAIR), ACT.Copy).then_inc(fkT_copied, 1)

                    def fS(l, i):
                        c, g = divmod(i, NPAIR)
                        n = pair(l, i)
                        act.wait_ge(fmax_done, n + 1)
                        if n >= 2:
                            act.wait_ge(fPT_psum, n - 1)
                        lo = 128 if c == 0 else 64
                        for j in range(2):
                            h = c * HF + 2 * g + j
                            af(v4(p_sb[:], 2, 2)[:, i % 2, j, lo:256], v3(place("fS", l, i)[:], 2)[:, j, lo:256], ACT.Exp,
                               bias=nmax[:, h:h + 1], accum_out=psums[:, h:h + 1]).then_inc(fexp_done, 1)

                    def fPT(l, i):
                        n = pair(l, i)
                        act.wait_ge(fPT_psum, n + 1)
                        if n >= 2:
                            act.wait_ge(fO_psum, n - 1)
                        ps, dst = v4(place("fPT", l, i)[:], 2, 2), v4(pT[:, (i % 2) * T:(i % 2 + 1) * T], 2, 2)
                        if i // NPAIR == 0:
                            ps, dst = ps[:, :, 1], dst[:, :, 1]
                        af(dst, ps, ACT.Copy).then_inc(fPT_copied, 1)

                    def foT(l, c):
                        n = l * NT + c
                        act.wait_ge(foT_psum, n + 1)
                        if n >= 2:
                            act.wait_ge(fwo_psum, n - 1)
                        af(oTf[:, c % 2 * T:(c % 2 + 1) * T], place("foT", l, c)[:], ACT.Copy).then_inc(foT_copied, 1)

                    def fw1(l, j):
                        _, m = HID_TILES[j]
                        n = 3 * l + j
                        act.wait_ge(fg_psum, n + 1)
                        if n >= 2:
                            act.wait_ge(hm_done, n - 1)
                        af(gl[0:m, (n % 2) * T:(n % 2 + 1) * T], place("fg", l, j)[0:m, :], ACT.Gelu,
                           bias=W(f"cols{l}")[0:m, 3 + j:4 + j]).then_inc(gelu_done, 1)

                    def split(i):
                        act.wait_ge(qkf_done, i + 1)
                        af(parts[:, 3 * i * T:(3 * i + 1) * T], qkf[:, i * T:(i + 1) * T], ACT.Copy).then_inc(split_done, 1)
                        act.wait_ge(split2_done, 2 * i + 1)
                        af(parts[:, (3 * i + 1) * T:(3 * i + 2) * T], res[:, i * T:(i + 1) * T], ACT.Copy).then_inc(split_done, 1)

                    def mv_():
                        act.wait_ge(mv_psum, 1)
                        act.wait_ge(vaug_zeroed, 2)
                        af(v3(vaug[:], NT * HM)[:, :, 0:DM], v3(place("mv")[:], NT * HM), ACT.Copy).then_inc(vaug_done, 1)

                    def mST(h):
                        if h >= PT_SLOTS:
                            act.wait_ge(mPV_psum, (h - PT_SLOTS) // GROUP + 1)
                        for t, (at, n) in enumerate(((0, T), (T, T), (2 * T, 2 * P))):
                            act.wait_ge(mST_psum, 3 * h + t + 1)
                            af(PTm[h % PT_SLOTS][:, at:at + n], place("mST", h, t)[:, 0:n], ACT.Exp).then_inc(mexp_done, 1)

                    def mPV(g):
                        if g >= 2:
                            act.wait_ge(matg_psum, g - 1)
                        act.wait_ge(mPV_psum, g + 1)
                        af(atg[:, (g % 2) * T:(g % 2 + 1) * T], place("mPV", g)[:], ACT.Copy).then_inc(atg_done, 1)

                    def gate():
                        act.wait_ge(gz_done, 1)
                        af(gp[:], gz[:], ACT.Exp, scale=-1.0).then_inc(gexp_done, 1)

                    def e_up(e):
                        act.wait_ge(eu_psum, e + 1)
                        if e >= 2:
                            act.wait_ge(es_done, e - 1)
                        af(the[:, (e % 2) * T:(e % 2 + 1) * T], place("eu", e)[:], ACT.Tanh, scale=0.5).then_inc(eth_done, 1)

                    walk({"xnT": lambda: copy_out(xnT[:], ("normT", 0), normT_psum, 1, xnT_copied), "k": k,
                          "qT": lambda h: copy_out(qT[:, h * T:(h + 1) * T], ("qT", h), qT_psum, h + 1, qT_copied), "bg": bg,
                          "kT": lambda c: copy_out(kT[:, c * T:(c + 1) * T], ("kT", c), kT_psum, c + 1, kT_copied),
                          "seq_u": seq_u, "seq_o": seq_o, "delta_norm": delta_norm,
                          "oT0": lambda: copy_out(oT0[:], ("oT0",), oT0_psum, 1, oT0_copied), "fqkv": fqkv, "fT": fT,
                          "fS": fS, "fPT": fPT, "foT": foT, "fw1": fw1,
                          "xn2T": lambda: copy_out(xn2T[:], ("normT", 3), normT_psum, 4, xn2_copied),
                          "mq": lambda: split(0), "mk": lambda: split(1), "mv": mv_, "mST": mST, "mPV": mPV,
                          "aT": lambda: copy_out(aT[:], ("aT",), aT_psum, 1, aT_copied), "gate": gate, "e_up": e_up})

                @block.vector
                def _(dve):
                    tt, ts, stt = nc.vector.tensor_tensor, nc.vector.tensor_scalar, nc.vector.scalar_tensor_tensor
                    chain = [0]


                    def link(ins):
                        chain[0] += 1
                        ins.then_inc(dve_chain, 1)
                        dve.wait_ge(dve_chain, chain[0])

                    def rsqrt(dst, src, n, done):
                        y, t = rs_out[:, 0:n], rs_tmp[:, 0:n]
                        link(ts(t.bitcast(I32), src.bitcast(I32), 1, None, ALU.logical_shift_right))
                        link(ts(y.bitcast(I32), t.bitcast(I32), -1.0, float(0x5f3759df), ALU.mult, ALU.add))
                        for i in range(3):
                            link(tt(t, y, y, ALU.mult))
                            link(stt(t, t, -0.5, src, ALU.mult, ALU.mult))
                            last = stt(y if i < 2 else dst, t, 1.5, y, ALU.add, ALU.mult)
                            if i < 2 or done is None:
                                link(last)
                            else:
                                last.then_inc(done, 1)

                    def layernorm(dst, src, width, done):
                        for c in range(NT):
                            link(nc.vector.bn_stats(v3(stats[:], NT)[:, c], src[:, c])) if c == NT - 1 else nc.vector.bn_stats(
                                v3(stats[:], NT)[:, c], src[:, c])
                        for c in range(NT):
                            m = nc.vector.bn_aggr(v3(mv[:], NT)[:, c], v3(stats[:], NT)[:, c])
                        link(m)
                        link(ts(rs_in[:, 0:NT], v3(mv[:], NT)[:, :, 1], EPS, None, ALU.add))
                        rsqrt(rs_in[:, NT:2 * NT], rs_in[:, 0:NT], NT, None)
                        for c in range(NT):
                            m = ts(dst[:, c], src[:, c], v3(mv[:], NT)[:, c, 0:1], rs_in[:, NT + c:NT + c + 1], ALU.subtract, ALU.mult)
                        m.then_inc(done, 1)

                    def ln0():
                        layernorm(v3(norm_tm[:], NT), v3(x_tm[:], NT), D, norm_done)

                    def shifted(dst, src):
                        nc.vector.tensor_copy(dst[0:64, :], src[0:64, :])
                        return nc.vector.tensor_copy(dst[64:P, 1:T], src[64:P, 0:T - 1])

                    def xnT_():
                        dve.wait_ge(xnT_copied, 1)
                        shifted(hT, xnT).then_inc(h_done, 1)

                    def k(c):
                        dve.wait_ge(ksq_done, c + 1)
                        nc.vector.tensor_reduce(kss[:, c * H0:(c + 1) * H0], v3(kT[:, c * T:(c + 1) * T], H0), AX, ALU.add).then_inc(kss_done, 1)

                    def krs_():
                        dve.wait_ge(kss_done, NT)
                        link(ts(kss[:], kss[:], 1e-12, None, ALU.add))
                        rsqrt(krs[:], kss[:], NT * H0, krs_done)

                    def bg(c):
                        t = th[:, c * NBG:(c + 1) * NBG]
                        dve.wait_ge(th_done, c + 1)
                        ts(beta[:, c * H0:(c + 1) * H0], t[:, 0:H0], 0.5, 0.5, ALU.mult, ALU.add).then_inc(beta_done, 1)
                        stt(gs[:, c * P:(c + 1) * P], t[:, H0:NBG], 1.0, place("bg", c)[:, H0:NBG], ALU.add, ALU.mult).then_inc(gs_done, 1)

                    def gram(c):
                        dve.wait_ge(G_psum, c + 1)
                        dve.wait_ge(beta_done, c + 1)
                        for h in range(H0):
                            m = stt(v4(L, 2, H0)[:, c % 2, h], v3(place("G", c)[:], H0)[:, h], beta[:, c * H0 + h:c * H0 + h + 1],
                                    C("strict"), ALU.mult, ALU.mult)
                        m.then_inc(L_done, 1)

                    def seq_b(c):
                        dve.wait_ge(B_psum, c + 1)
                        if c:
                            dve.wait_ge(O_psum, c)
                        tt(v3(Bm, H0), v3(place("B", c)[:], H0), repeat(C("upper"), H0), ALU.mult).then_inc(Bm_done, 1)

                    def inv_v(k, c):
                        n = at_level(k, c, LEVELS)
                        dve.wait_ge(V_psum, n + 1)
                        Vc, Xc, Zc = v4(Vm, 2, H0)[:, c % 2], v4(X, 2, H0)[:, c % 2], v4(Z, NT, H0)[:, c]
                        tt(Vc, v3(place("V", k, c)[:], H0), repeat(B("lowT")[:, k * P:(k + 1) * P], H0), ALU.mult).then_inc(Vm_done, 1)
                        if k == 0:
                            dve.wait_ge(Vm_done, n + 1)
                            tt(Zc, Vc, repeat(C("ident"), H0), ALU.add).then_inc(Z_done, 1)
                            link(tt(Xc, v4(L, 2, H0)[:, c % 2], repeat(B("low"), H0), ALU.mult))
                            tt(Xc, Xc, repeat(C("ident"), H0), ALU.add).then_inc(X_done, 1)

                    def inv_zx(k, c):
                        Zc, Xc = v4(Z, NT, H0)[:, c], v4(X, 2, H0)[:, c % 2]
                        dve.wait_ge(ZV_psum, at_level(k, c, LEVELS - 1, 1) + 1)
                        dve.wait_ge(Z_done, at_level(k - 1, c, LEVELS) + 1)
                        tt(Zc, Zc, v3(place("ZV", k, c)[:], H0), ALU.add).then_inc(Z_done, 1)
                        if k < LEVELS - 1:
                            dve.wait_ge(VX_psum, at_level(k, c, LEVELS - 2, 1) + 1)
                            dve.wait_ge(X_done, at_level(k - 1, c, LEVELS - 1) + 1)
                            tt(Xc, Xc, v3(place("VX", k, c)[:], H0), ALU.add).then_inc(X_done, 1)

                    def seq_p(c):
                        dve.wait_ge(P_psum, c + 1)
                        if c:
                            dve.wait_ge(U_psum, c)
                        tt(v3(R_sb[:], H0), v3(place("P", c)[:, 0:P], H0), spread(beta[:, c * H0:(c + 1) * H0], DV), ALU.mult)\
                            .then_inc(R_done, 1)

                    def seq_o(c):
                        if c < NT - 1:
                            dve.wait_ge(dS_psum, c + 1)
                            ps = place("dS", c)[:, 0:P]
                            if c:
                                dve.wait_ge(S_done, c)
                                tt(Sn[:], Sn[:], ps, ALU.subtract).then_inc(S_done, 1)
                            else:
                                ts(Sn[:], ps, -1.0, None, ALU.mult).then_inc(S_done, 1)

                    def delta_norm():
                        dve.wait_ge(osq_done, 1)
                        link(nc.vector.tensor_reduce(oss[:], v3(kn[:, 0:T], NT * H0), AX, ALU.add))
                        link(ts(oss[:], oss[:], 1.0 / (DK * DV), EPS, ALU.mult, ALU.add))
                        rsqrt(ors[:], oss[:], NT * H0, ors_done)

                    def fqkv(l, c):
                        n = l * NT + c
                        for i, (full_bank, full, turned, dst, tc, tsn) in enumerate((
                                (place("fq", l, c), fq_psum, fqT_psum, q_f, "qc", "qs"), (place("fk", l, c), fk_psum, fkT_psum, k_f, "kc", "ks"))):
                            m = 2 * n + i
                            at = c * DF
                            dve.wait_ge(fsq_done, m + 1)
                            nc.vector.tensor_reduce(qk_ss[:, c % 2 * 16 + 8 * i:c % 2 * 16 + 8 * i + 8], v3(rot[m % 2][:], HF), AX, ALU.add)\
                                .then_inc(fss_done, 1)
                            dve.wait_ge(full, n + 1)
                            if n >= 2:
                                dve.wait_ge(turned, n - 1)
                            ps = v3(full_bank[:], HF)
                            tt(v3(dst[:, c % 2 * T:(c % 2 + 1) * T], HF), ps, repeat(tab[tc][l][:, at:at + DF], HF), ALU.mult).then_inc(ft1_done, 1)
                            dve.wait_ge(fss_done, m + 1)
                            r = v3(rot[m % 2][:], HF)
                            hd = DF // 2
                            tt(r[:, :, 0:hd], ps[:, :, hd:DF], repeat(tab[tsn][l][:, at:at + hd], HF), ALU.mult)
                            tt(r[:, :, hd:DF], ps[:, :, 0:hd], repeat(tab[tsn][l][:, at + hd:at + DF], HF), ALU.mult).then_inc(frot_done, 1)

                    def frs(l, c):
                        n = l * NT + c
                        if n >= 2:
                            dve.wait_ge(fn_done, 2 * (n - 1))
                        dve.wait_ge(fss_done, 2 * n + 2)
                        v = qk_ss[:, c % 2 * 16:c % 2 * 16 + 16]
                        link(ts(v, v, 1e-24, None, ALU.max))
                        rsqrt(qk_rs[:, c % 2 * 16:c % 2 * 16 + 16], v, 16, frs_done)

                    def fT(l, c):
                        n = l * NT + c
                        dve.wait_ge(fqT_psum, n + 1)
                        if n >= 2:
                            dve.wait_ge(fS_psum, (n - 1) * NPAIR)
                        half = slice(DF, P)
                        nc.vector.tensor_copy(v4(qTz[:], 2, HF)[half, c % 2, 1:HF:2], v3(place("fqT", l, c)[:], NPAIR)[half])\
                            .then_inc(fqT_hi, 1)

                    def fS(l, i):
                        c, g = divmod(i, NPAIR)
                        n = pair(l, i)
                        lo = 128 if c == 0 else 64
                        dve.wait_ge(fS_psum, n + 1)
                        if l:
                            dve.wait_ge(fexp_done, 2 * NT * NPAIR)
                        nc.vector.tensor_reduce(nmax[:, c * HF + 2 * g:c * HF + 2 * g + 2], v3(place("fS", l, i)[:], 2)[:, :, lo:256],
                                                AX, ALU.max, negate=True).then_inc(fmax_done, 1)

                    def fPV(l, i):
                        c, g = divmod(i, NPAIR)
                        if g < NPAIR - 1:
                            return
                        n = l * NT + c
                        dve.wait_ge(fO_psum, pair(l, i) + 1)
                        dve.wait_ge(fexp_done, 2 * pair(l, i) + 2)
                        r = prec[:, c * HF:(c + 1) * HF]
                        link(nc.vector.reciprocal(r, psums[:, c * HF:(c + 1) * HF]))
                        if n >= 2:
                            dve.wait_ge(foT_psum, n - 1)
                        tt(v3(o_sb[:, (c % 2) * T:(c % 2 + 1) * T], HF), v3(place("fO", l, c)[:], HF), spread(r, DF), ALU.mult)\
                            .then_inc(fo_done, 1)

                    def fres(l):
                        dve.wait_ge(fwo_psum, NT * (l + 1))
                        old = xnT if l == 0 else r2T
                        dve.wait_ge(xnT_copied, 1) if l == 0 else dve.wait_ge(r_done, 1)
                        tt(r1T[:], place("fwo", l)[:], old[:], ALU.add).then_inc(r1_done, 1)
                        dve.wait_ge(r1_done, l + 1)
                        if l:
                            dve.wait_ge(h2tm_psum, l)
                        shifted(h2T, r1T).then_inc(h2_done, 1)

                    def fln(l):
                        dve.wait_ge(h2tm_psum, l + 1)
                        dve.wait_ge(normT_psum, l + 1)
                        layernorm(v3(norm_tm[:], NT), v3(place("h2tm", l)[:], NT), D, norm_done)

                    def hnT_(l):
                        dve.wait_ge(normT_psum, l + 2)
                        if l:
                            dve.wait_ge(fa_psum, 3)
                        cols = W(f"cols{l}")
                        ts(hnT[:], place("normT", l + 1)[:], cols[:, 7:8], cols[:, 8:9], ALU.mult, ALU.add).then_inc(hn_done, 1)

                    def fw1(l, j):
                        _, m = HID_TILES[j]
                        n = 3 * l + j
                        dve.wait_ge(gelu_done, n + 1)
                        dve.wait_ge(fa_psum, n + 1)
                        if l:
                            dve.wait_ge(fw2_psum, 1)
                        stt(hm[0:m, j * T:(j + 1) * T], place("fa", l, j)[0:m, :], W(f"cols{l}")[0:m, j:j + 1],
                            gl[0:m, (n % 2) * T:(n % 2 + 1) * T], ALU.add, ALU.mult).then_inc(hm_done, 1)

                    def fw2(l):
                        dve.wait_ge(fw2_psum, l + 1)
                        stt(r2T[:], place("fw2", l)[:], W(f"cols{l}")[:, 6:7], r1T[:], ALU.add, ALU.add).then_inc(r_done, 1)
                        if l == 0:
                            dve.wait_ge(r_done, 1)
                            shifted(hT, r2T).then_inc(h_done, 1)

                    def x1():
                        dve.wait_ge(x1_psum, 1)
                        dve.wait_ge(normT_psum, 3)
                        tt(x1_tm[:], place("x1")[:], x_tm[:], ALU.add).then_inc(x1_done, 1)
                        dve.wait_ge(x1_done, 1)
                        layernorm(v3(norm_tm[:], NT), v3(x1_tm[:], NT), D, norm_done)

                    def lat():
                        dve.wait_ge(lat_psum, 1)
                        layernorm(v3(lat_tm[:], NT), v3(place("lat")[:, 0:NT * LAT], NT), LAT, lat_done)

                    def latT_():
                        dve.wait_ge(latT_psum, 1)
                        cols = W("latcols")
                        ts(latT[0:LAT, :], place("latT")[0:LAT, :], cols[0:LAT, 0:1], cols[0:LAT, 1:2], ALU.mult, ALU.add)\
                            .then_inc(latT_done, 1)

                    def rope(i, scale):
                        f = qkf[:, i * T:(i + 1) * T]
                        dve.wait_ge(mq_psum, 2 * i + 1)
                        stt(rc[:], place("mq", 2 * i)[:], scale, C("rcos"), ALU.mult, ALU.mult).then_inc(rope_done, 1)
                        dve.wait_ge(mq_psum, 2 * i + 2)
                        stt(rsn[:], place("mq", 2 * i + 1)[:], scale, C("rsin"), ALU.mult, ALU.mult).then_inc(rope_done, 1)
                        dve.wait_ge(rope_done, 2 * i + 2)
                        tt(f, rc[:], rsn[:], ALU.add).then_inc(qkf_done, 1)
                        p = [parts[:, (3 * i + n) * T:(3 * i + n + 1) * T] for n in range(3)]
                        r = res[:, i * T:(i + 1) * T]
                        dve.wait_ge(split_done, 2 * i + 1)
                        tt(r, f, p[0], ALU.subtract).then_inc(split2_done, 1)
                        dve.wait_ge(split_done, 2 * i + 2)
                        tt(p[2], r, p[1], ALU.subtract).then_inc(split2_done, 1)

                    def mS(h):
                        for t, c, at in ((0, 0, 0), (0, 2, P), (1, 1, 0), (2, 3, 0)):
                            dve.wait_ge(mS_psum, 3 * h + t + 1)
                            nc.vector.tensor_reduce(nmx[:, h * NT + c:h * NT + c + 1], place("mS", h, t)[:, at:at + (c + 1) * P],
                                                    AX, ALU.max, negate=True).then_inc(nmx_done, 1)

                    def mrow(g):
                        dve.wait_ge(mrow_psum, g + 1)
                        if g:
                            dve.wait_ge(mrow_sent, 48 * g)
                        p = [mparts[0:NROW, n * P:(n + 1) * P] for n in range(3)]
                        ps, left = place("mrow", g)[0:NROW, 0:P], mres[0:NROW, :]
                        link(nc.vector.tensor_copy(p[0], ps))
                        link(tt(left, ps, p[0], ALU.subtract))
                        link(nc.vector.tensor_copy(p[1], left))
                        tt(p[2], left, p[1], ALU.subtract).then_inc(mrow_done, 1)

                    def matg(g):
                        dve.wait_ge(matg_psum, g + 1)
                        ps = v3(place("matg", g)[:], NT * GROUP)
                        r = at_rec[:, 0:NT * GROUP]
                        link(nc.vector.reciprocal(r, ps[:, :, DM]))
                        o = v3(at_tm[:], NT)[:, :, g * GROUP * DM:(g + 1) * GROUP * DM].rearrange("p c (h d) -> p c h d", h=GROUP)
                        for c in range(NT):
                            m = tt(o[:, c], ps[:, c * GROUP:(c + 1) * GROUP, 0:DM], spread(r[:, c * GROUP:(c + 1) * GROUP], DM), ALU.mult)
                        m.then_inc(at_done, 1)

                    def gate():
                        dve.wait_ge(gate_psum, 1)
                        tt(v3(gz[:], NT), v3(place("gate")[:, 0:NT * NE], NT), repeat(R("gate_b"), NT), ALU.add).then_inc(gz_done, 1)
                        dve.wait_ge(gexp_done, 1)
                        link(ts(gw_[:], gp[:], 1.0, None, ALU.add))
                        link(nc.vector.reciprocal(gp[:], gw_[:]))
                        for c in range(NT):
                            p = gp[:, c * NE:(c + 1) * NE]
                            other, own = repeat(p, NE), spread(p, NE)
                            tt(v3(gcmp[:, c * 36:(c + 1) * 36], NE), other, own, ALU.is_gt)
                            m = tt(v3(geq[:, c * 36:(c + 1) * 36], NE), other, own, ALU.is_equal)
                        link(m)
                        link(tt(v3(geq[:], NT), v3(geq[:], NT), repeat(C("tri"), NT), ALU.mult))
                        link(tt(gcmp[:], gcmp[:], geq[:], ALU.add))
                        link(nc.vector.tensor_reduce(grank[:], v3(gcmp[:], NT * NE), AX, ALU.add))
                        link(stt(gw_[:], grank[:], 1.5, gp[:], ALU.is_lt, ALU.mult))
                        link(nc.vector.tensor_reduce(gsum[:, 0:NT], v3(gw_[:], NT), AX, ALU.add))
                        link(ts(gsum[:, 0:NT], gsum[:, 0:NT], 1e-8, None, ALU.add))
                        link(nc.vector.reciprocal(gsum[:, NT:2 * NT], gsum[:, 0:NT]))
                        tt(v3(ge[:], NT), v3(gw_[:], NT), spread(gsum[:, NT:2 * NT], NE), ALU.mult).then_inc(ge_done, 1)

                    def e_up(e):
                        slot = slice((e % 2) * T, (e % 2 + 1) * T)
                        dve.wait_ge(eth_done, e + 1)
                        stt(se[:, slot], the[:, slot], 1.0, place("eu", e)[:], ALU.add, ALU.mult).then_inc(es_done, 1)
                        dve.wait_ge(es_done, e + 1)
                        dve.wait_ge(ew_psum, e + 1)
                        if e >= 2:
                            dve.wait_ge(ey_psum, e - 1)
                        stt(he[:, slot], se[:, slot], 0.5, place("ew", e)[:], ALU.mult, ALU.mult).then_inc(eh_done, 1)

                    def e_down(e):
                        dve.wait_ge(ey_psum, e + 1)
                        dve.wait_ge(ge_done, 1)
                        if e:
                            dve.wait_ge(ey_done, e)
                        for c in range(NT):
                            s = ge[:, c * NE + e:c * NE + e + 1]
                            o, y = acc[:, c * P:(c + 1) * P], place("ey", e)[:, c * P:(c + 1) * P]
                            m = stt(o, y, s, o, ALU.mult, ALU.add) if e else ts(o, y, s, None, ALU.mult)
                        m.then_inc(ey_done, 1)

                    def final():
                        dve.wait_ge(ey_done, NE)
                        link(tt(acc[:], acc[:], x1_tm[:], ALU.add))
                        dve.wait_ge(fin_psum, 1)
                        tt(fin[:], place("fin")[:], acc[:], ALU.add).then_inc(fin_done, 1)

                    walk({"ln0": ln0, "xnT": xnT_, "k": k, "krs": krs_, "bg": bg, "gram": gram, "inv_v": inv_v, "inv_zx": inv_zx,
                          "seq_b": seq_b, "seq_p": seq_p, "seq_o": seq_o, "delta_norm": delta_norm, "fqkv": fqkv, "frs": frs, "fT": fT, "fS": fS,
                          "fPV": fPV, "fres": fres, "fln": fln, "hnT": hnT_, "fw1": fw1, "fw2": fw2, "x1": x1, "lat": lat,
                          "latT": latT_, "mq": lambda: rope(0, DM ** -0.5), "mk": lambda: rope(1, 1.0),
                          "mS": mS, "mrow": mrow, "matg": matg, "gate": gate, "e_up": e_up, "e_down": e_down, "final": final})

                @block.gpsimd
                def _(pool):
                    tt = nc.gpsimd.tensor_tensor


                    def kT_(c):
                        pool.wait_ge(krs_done, 1)
                        pool.wait_ge(k_copied, c + 1)
                        tt(v4(kn[:], NT, H0)[:, c], v4(kn[:], NT, H0)[:, c], spread(krs[:, c * H0:(c + 1) * H0], DK), ALU.mult)\
                            .then_inc(kn_done, 1)

                    def delta_norm():
                        pool.wait_ge(ors_done, 1)
                        pool.wait_ge(o_copied, NT)
                        o = v3(o_all[:], NT * H0)
                        pool.wait_ge(osq_done, 1)
                        tt(o, o, spread(ors[:], DV), ALU.mult).then_inc(on_done, 1)
                        pool.wait_ge(on_done, 1)
                        tt(v3(o_all[:], NT), v3(o_all[:], NT), repeat(norm_w[:], NT), ALU.mult).then_inc(on_done, 1)
                        pool.wait_ge(on_done, 2)
                        pool.wait_ge(gs_done, NT)
                        tt(o_all[:], o_all[:], gs[:], ALU.mult).then_inc(og_done, 1)

                    def fqkv(l, c):
                        for i, dst in enumerate((q_f, k_f)):
                            m = 2 * (l * NT + c) + i
                            pool.wait_ge(ft1_done, m + 1)
                            pool.wait_ge(frot_done, m + 1)
                            d = dst[:, c % 2 * T:(c % 2 + 1) * T]
                            tt(d, d, rot[m % 2][:], ALU.add).then_inc(fsum_done, 1)

                    def fT(l, c):
                        pool.wait_ge(frs_done, l * NT + c + 1)
                        for i, dst in enumerate((q_f, k_f)):
                            m = 2 * (l * NT + c) + i
                            pool.wait_ge(fsum_done, m + 1)
                            d = v3(dst[:, c % 2 * T:(c % 2 + 1) * T], HF)
                            tt(d, d, spread(qk_rs[:, c % 2 * 16 + 8 * i:c % 2 * 16 + 8 * i + 8], DF), ALU.mult).then_inc(fn_done, 1)

                    def x1():
                        pool.wait_ge(x1_psum, 1)
                        nc.gpsimd.memset(vaug, 0.0).then_inc(vaug_zeroed, 1)
                        pool.wait_ge(vaug_zeroed, 1)
                        nc.gpsimd.memset(v3(vaug, NT * HM)[:, :, DM:DM + 1], 1.0).then_inc(vaug_zeroed, 1)

                    walk({"kT": kT_, "delta_norm": delta_norm, "fqkv": fqkv, "fT": fT, "x1": x1})

                @block.sync
                def _(sp):

                    def x1():
                        sp.wait_ge(x1_done, 1)
                        sp.dma_start(v3(x_tm[:], NT), x[bass.ds(b + 1, 1)].rearrange("a (t p) d -> p (a t) d", p=P)).then_inc(x_loaded, 16)
                        for i, dst in enumerate((Qst32, Kst32)):
                            sp.dma_start(dst[9 * DM:P, :], row_fill[i]).then_inc(rows_filled, 16)

                    def send(i):
                        for n in range(3):
                            sp.wait_ge(split_done, 2 * i + 1 + (n > 0))
                            sp.wait_ge(split2_done, 2 * i + 1 + (n > 1))
                            to = parts_dram[i, n * DM:(n + 1) * DM].rearrange("d (h t) -> h d t", h=HM)
                            sp.dma_start(to, parts[:, (3 * i + n) * T:(3 * i + n + 1) * T]).then_inc(parts_kept, 16)
                        sp.wait_ge(parts_kept, 48 * (i + 1))
                        rows = 3 * DM
                        for s in range(3):
                            if i == 1:
                                sp.dma_start(Kst[s * rows:(s + 1) * rows, :], parts_dram[1]).then_inc(parts_sent, 16)
                            else:
                                for n in range(3):
                                    at = (3 * n + s) * DM
                                    sp.dma_start(Qst[at:at + DM, :], parts_dram[0, n * DM:(n + 1) * DM]).then_inc(parts_sent, 16)

                    def mrow(g):
                        sp.wait_ge(mrow_done, g + 1)
                        for i in range(3):
                            dst = Qst[9 * DM + i:9 * DM + i + 1, g * GROUP * T:(g + 1) * GROUP * T].rearrange("a (r t) -> a r t", t=P)
                            sp.dma_start(dst, mparts[0:NROW, i * P:(i + 1) * P]).then_inc(mrow_sent, 16)

                    def final():
                        sp.wait_ge(fin_done, 1)
                        sp.dma_start(out[bass.ds(b, 1)].rearrange("a (t p) d -> p (a t) d", p=P), v3(fin[:], NT)).then_inc(out_stored, 16)
                        sp.wait_ge(out_stored, 16)
                        sp.wait_ge(x_loaded, 16)

                    walk({"x1": x1, "mq": lambda: send(0), "mk": lambda: send(1), "mrow": mrow, "final": final})

            nc.sync.sem_clear(range(numbers[0], numbers[-1] + 1))
            nc.all_engine_barrier()



def pack(inp):
    f = np.float32
    a = {k: np.asarray(v) for k, v in inp.items()}

    def rows128(m):
        out = np.zeros((P, m.shape[1]), f)
        out[:m.shape[0]] = m
        return out

    def tiles(m):
        n = -(-m.shape[0] // P)
        return np.concatenate([rows128(m[j * P:(j + 1) * P]) for j in range(n)], 1)

    w = {"wk": a["L0_attn_Wk"], "wq": a["L0_attn_Wq"], "wv": a["L0_attn_Wv"],
         "wbg": np.concatenate([a["L0_attn_Wb"], a["L0_attn_Wg"]], 1), "wo0": a["L0_attn_Wo"]}
    for l in range(DEPTH):
        w[f"wqkv{l}"] = a["L0_ffn_wqkv"][l]
        w[f"wof{l}"] = tiles(a["L0_ffn_wo"][l])
        w[f"w1{l}"] = a["L0_ffn_w1"][l]
        w[f"w2{l}"] = tiles(a["L0_ffn_w2"][l])
        b1 = a["L0_ffn_b1"][l]
        w[f"cols{l}"] = np.concatenate([tiles(b1[:HID, None]), tiles(b1[HID:, None]), a["L0_ffn_b2"][l][:, None],
                                        a["L0_ffn_ln_g"][l][:, None], a["L0_ffn_ln_b"][l][:, None]], 1)
    turned = np.arange(D).reshape(HM, 2, DM // 2)[:, ::-1].reshape(-1)
    w["Wq"], w["Wqr"] = a["L1_attn_W_q"], a["L1_attn_W_q"][:, turned]
    w["Wdkv"] = a["L1_attn_W_dkv"]
    w["Wuk"], w["Wukr"], w["Wuv"] = rows128(a["L1_attn_W_uk"]), rows128(a["L1_attn_W_uk"][:, turned]), rows128(a["L1_attn_W_uv"])
    w["Wo"] = a["L1_attn_W_o"]
    w["latcols"] = rows128(np.stack([a["L1_attn_ln_gamma"], a["L1_attn_ln_beta"]], 1))
    w["gate"] = a["L1_ffn_gate_w"].T
    for e in range(NE):
        w[f"eu{e}"], w[f"ew{e}"], w[f"ed{e}"] = a["L1_ffn_ew1"][e].T, a["L1_ffn_ew3"][e].T, a["L1_ffn_ew2"][e].T
    w[f"eu{NE}"], w[f"ew{NE}"], w[f"ed{NE}"] = a["L1_ffn_fc1"].T, a["L1_ffn_fc2"].T, a["L1_ffn_fc3"].T
    packed = np.ascontiguousarray(np.concatenate([w[n] for n, _ in weight_layout()], 1))
    rows = np.concatenate([a["L0_attn_norm_w"], a["L0_ffn_q_scale"].reshape(-1), a["L0_ffn_k_scale"].reshape(-1),
                           a["L1_ffn_gate_b"]])[None]
    return packed, np.ascontiguousarray(rows)


def kernel(**inputs):
    import concourse.bacc as bacc
    from concourse.bass_utils import run_bass_kernel_spmd

    packed, rows = pack(inputs)
    consts, consts_bf = constants()
    row_fill = np.zeros((2, P - 9 * DM, HM * T // 2), np.uint32)
    row_fill[1, 0:3] = 0x3F803F80
    row_fill = row_fill.view(np.float32)
    padded = np.concatenate([inputs["L0_attn_x"], np.zeros((1, T, D), np.float32)])
    arrays = {"x": padded, "weights": packed, "rows": rows, "consts": consts,
              "consts_bf": consts_bf, "row_fill": row_fill}
    nc = bacc.Bacc("TRN2", target_bir_lowering=False, num_devices=1)
    args = [nc.dram_tensor(n, a.shape, mybir.dt.from_np(a.dtype), kind="ExternalInput").ap() for n, a in arrays.items()]
    out = nc.dram_tensor("out", (BATCH, T, D), F32, kind="ExternalOutput").ap()
    parts_dram = nc.dram_tensor("parts_dram", (2, 3 * DM, HM * T), BF16, kind="Internal").ap()
    build(nc, *args, parts_dram, out)
    r = run_bass_kernel_spmd(nc, [arrays], core_ids=[0])
    return r.results[0]["out"]
```

```python
from contextlib import ExitStack

import numpy as np

import concourse.bass as bass
from concourse import mybir

ALU = mybir.AluOpType
ACT = mybir.ActivationFunctionType
AX = mybir.AxisListType.X
F32 = mybir.dt.float32
BF16 = mybir.dt.bfloat16
I32 = mybir.dt.int32

P = 128
BATCH, T, D = 8, 512, 128
NT = T // P
H0, DK, DV = 4, 128, 32
DEPTH, HF, DF, WIN = 2, 8, 64, 64
HID = D * 4 * 2 // 3
HM, DM, LAT = 16, 8, 32
NE = 6
BLK = 16
NBLK = NT * H0 * P // BLK
LEVELS = 4
HEAD_ROOM = P * P + P
BLOCK_STEP = (P + 1) * BLK
NEG = -1e30
EPS = 1e-5
NPAIR = HF // 2
VW = 32
GROUP = 4
NROW = NT * GROUP
LEAD = 7
PT_SLOTS = 6
DELTA_AFTER = "302330001000010101003010000010000010100002000011010001100000010001000010001010000210000125000020210111100000001010100000100010001001000100110010000000000000000010100100210001"
EXPERTS_AFTER = "002161400000000"
HID_TILES = [(j * P, min(P, HID - j * P)) for j in range((HID + P - 1) // P)]



def weight_layout():
    w = [("wk", H0 * DK), ("wq", H0 * DK), ("wv", H0 * DV), ("wbg", H0 + H0 * DV), ("wqkv0", 3 * HF * DF), ("wo0", D)]
    for l in range(DEPTH):
        w += [("wqkv1", 3 * HF * DF)] if l else []
        w += [(f"wof{l}", 4 * D), (f"w1{l}", 2 * HID), (f"w2{l}", 3 * D), (f"cols{l}", 9)]
    w += [("Wq", D), ("Wqr", D), ("Wdkv", LAT), ("Wuk", D), ("Wukr", D), ("Wuv", D), ("Wo", D), ("latcols", 2)]
    w += [("gate", NE)]
    w += [(f"e{n}{i}", D) for i in range(NE + 1) for n in ("u", "w", "d")]
    return w


CONST_LAYOUT = [("ident", P), ("strict", P), ("upper", P),
                ("qcos", NT * DF), ("qsin", NT * DF), ("kcos", NT * DF), ("ksin", NT * DF),
                ("tri", NE * NE), ("rcos", T), ("rsin", T)]
BF_LAYOUT = [("identb", P), ("band", 192), ("causal", P), ("causalT", P),
             ("lowT", (LEVELS - 1) * P)]


def offsets(layout):
    at, out = 0, {}
    for name, n in layout:
        out[name] = (at, n)
        at += n
    return out, at


def constants():
    f = np.float32
    i, j = np.arange(P)[:, None], np.arange(P)[None, :]
    c = {"ident": np.eye(P, dtype=f), "strict": (j < i).astype(f), "upper": -(i <= j).astype(f)}
    low = [-((i >> (k + 1) == j >> (k + 1)) & ((i >> k) & 1 == 1) & ((j >> k) & 1 == 0)).astype(f) for k in range(4, 7)]
    half = np.arange(0, DF, 2, dtype=f)
    inv = (f(1) / f(10000) ** (half / f(DF))).astype(f)
    t = np.arange(T, dtype=f)
    ang = np.concatenate([t[:, None] * inv[None]] * 2, 1)
    base = ((half + f(0.4 * DF)) / f(1.4 * DF)).astype(f)
    scale = np.concatenate([base[None] ** ((t - T // 2) / f(WIN // 2))[:, None]] * 2, 1).astype(f)
    sign = np.where(np.arange(DF) < DF // 2, f(-1), f(1))[None]
    cos, sin = np.cos(ang), np.sin(ang) * sign
    tiles = lambda a: a.astype(f).reshape(NT, P, DF).transpose(1, 0, 2).reshape(P, NT * DF)
    c["qcos"], c["qsin"] = tiles(8 * cos * scale), tiles(8 * sin * scale)
    c["kcos"], c["ksin"] = tiles(cos / scale), tiles(sin / scale)
    hd = DM // 2
    inv = (f(1) / f(10000) ** (np.arange(hd, dtype=f) / f(hd))).astype(f)
    d = np.arange(D) % DM
    ang = inv[d % hd][:, None] * t[None]
    c["rcos"] = np.cos(ang).astype(f)
    c["rsin"] = (np.sin(ang) * np.where(d < hd, -1, 1)[:, None]).astype(f)
    e = np.arange(NE)
    c["tri"] = np.broadcast_to((e[None] < e[:, None]).astype(f).reshape(1, -1), (P, NE * NE))
    packed = np.concatenate([c[n].astype(f) for n, _ in CONST_LAYOUT], 1)
    key = np.arange(192)[None] - 64
    b = {"identb": np.eye(P), "band": np.where((key <= i) & (key >= i - WIN), 0, NEG),
         "causal": np.where(j <= i, 0, NEG), "causalT": np.where(i <= j, 0, NEG),
         "lowT": np.concatenate([m.T for m in low], 1)}
    return np.ascontiguousarray(packed), np.concatenate([b[n].astype(f) for n, _ in BF_LAYOUT], 1)


def build(nc, x, weights, rows, consts, consts_bf, row_fill, parts_dram, L_dram, X_dram, out):
    W_AT, W_N = offsets(weight_layout())
    C_AT, C_N = offsets(CONST_LAYOUT)
    B_AT, B_N = offsets(BF_LAYOUT)
    R_AT, R_N = offsets([("norm_w", DV), ("qs", DEPTH * DF), ("ks", DEPTH * DF), ("gate_b", NE)])

    with ExitStack() as ctx:
        def sb(name, n, dt=F32):
            return ctx.enter_context(nc.sbuf_tensor(name, [P, n], dt))

        w_sb, c_sb, b_sb, r_sb = sb("w_sb", W_N), sb("c_sb", C_N), sb("b_sb", B_N, BF16), sb("r_sb", R_N)

        def W(name):
            a, n = W_AT[name]
            return w_sb[:, a:a + n]

        def C(name):
            a, n = C_AT[name]
            return c_sb[:, a:a + n]

        def B(name):
            a, n = B_AT[name]
            return b_sb[:, a:a + n]

        def R(name):
            a, n = R_AT[name]
            return r_sb[:, a:a + n]

        def v3(ap, a):
            return ap.rearrange("p (a b) -> p a b", a=a)

        def v4(ap, a, b):
            return ap.rearrange("p (a b c) -> p a b c", a=a, b=b)

        def spread(ap, n):
            return ap[:, :, None].to_broadcast([ap.shape[0], ap.shape[1], n])

        def repeat(ap, n):
            return ap[:, None, :].to_broadcast([ap.shape[0], n, ap.shape[1]])

        tab = {n: [sb(f"tab_{n}", NT * DF)[:, :], C(c)] for n, c in (("qc", "qcos"), ("qs", "qsin"), ("kc", "kcos"), ("ks", "ksin"))}
        norm_w = sb("norm_w_neg", H0 * DV)

        x_tm, norm_tm, xnT, r1T, r2T = sb("x_tm", T), sb("norm_tm", T), sb("xnT", T), sb("r1T", T), sb("r2T", T)
        hT, h2T = sb("hT", T), sb("h2T", T)
        qTz = sb("qTz", 2 * HF * P)
        p_sb, o_sb, gl, hm = sb("p_sb", 2 * T), sb("o_sb", 2 * T), sb("gl", 2 * T), sb("hm", 3 * T)
        oT0, latT = sb("oT0", T), sb("latT", T)
        NBG = H0 + H0 * DV
        stats, mv = sb("stats", NT * 6), sb("mv", NT * 2)
        rs_in, rs_tmp, rs_out = sb("rs_in", 2 * NT), sb("rs_tmp", 16), sb("rs_out", 16)
        kss, krs, beta = sb("kss", NT * H0), sb("krs", NT * H0), sb("beta", NT * H0)
        oss, ors = sb("oss", NT * H0), sb("ors", NT * H0)
        qk_ss, qk_rs = sb("qk_ss", 2 * 16), sb("qk_rs", 2 * 16)
        R_sb, U_sb, Sn = sb("R_sb", P), sb("U_sb", P), sb("Sn", H0 * DV)
        nmax, psums, prec = sb("nmax", NT * HF), sb("psums", NT * HF), sb("prec", NT * HF)
        nmx, mparts, mres = sb("nmx", NT * HM), sb("mparts", 3 * P, BF16), sb("mres", P)
        at_rec, gz, gp, gw_, ge = sb("at_rec", NT * GROUP), sb("gz", 24), sb("gp", 24), sb("gw_", 24), sb("ge", 24)
        gcmp, geq, grank, gsum = sb("gcmp", NT * 36), sb("geq", NT * 36), sb("grank", 24), sb("gsum", 2 * NT)
        PTW = NT * (NT + 1) // 2 * P
        layer0 = [("kn", NT * T), ("kT", NT * T), ("qT", NT * T), ("oTf", 2 * T), ("q_f", 2 * T), ("k_f", 2 * T), ("v_f", NT * T),
                  ("kTf", NPAIR * T), ("pT", 2 * T), ("rot", 2 * T), ("gs", T), ("th", NT * NBG), ("o_all", T), ("hnT", T),
                  ("Z", NT * T), ("Bm", T), ("L", 2 * T), ("X", 2 * T), ("Vm", 2 * T),
                  ("blk", 3 * BLK * BLK)]
        layer1 = [("Qst", HM * T // 2), ("Kst", HM * T // 2), ("qkf", 2 * T), ("res", 2 * T), ("parts", 3 * T), ("rope", 2 * T),
                  ("lat_tm", NT * LAT), ("he", 2 * T), ("vaug", NT * HM * VW), ("PTm", PT_SLOTS * PTW)]
        at0, n0 = offsets(layer0)
        at1, n1 = offsets(layer1)
        shared = sb("shared", max(n0, n1))
        kn, kT, qT, oTf, q_f, k_f, v_f, kTf, pT, rot, gs, th, o_all, hnT, Z, Bm, L, X, Vm, blk = (
            shared[:, a:a + n] for a, n in at0.values())
        Qst, Kst, qkf, res, parts, rope_sb, lat_tm, he, vaug, PTm = (shared[:, a:a + n] for a, n in at1.values())
        Qst32, Kst32 = Qst, Kst
        Qst, Kst, parts = Qst.bitcast(BF16), Kst.bitcast(BF16), parts.bitcast(BF16)
        rc, rsn, atg = rope_sb[:, 0:T], rope_sb[:, T:2 * T], rope_sb
        PTm = [PTm[:, i * PTW:(i + 1) * PTW] for i in range(PT_SLOTS)]
        rot = [rot[:, 0:T], rot[:, T:2 * T]]
        Lb, Xb, prod = blk[:, 0:BLK * BLK], blk[:, BLK * BLK:2 * BLK * BLK], blk[:, 2 * BLK * BLK:]

        def in_dram(m, c):
            return m.rearrange("(g r) -> g r", r=HEAD_ROOM)[c * H0:(c + 1) * H0, 0:P * P].rearrange("h (p t) -> p h t", p=P)

        def diagonal(m):
            return m.rearrange("(b r) -> b r", r=BLOCK_STEP)[:, 0:BLK * P].rearrange("b (i t) -> b i t", t=P)[:, :, 0:BLK]

        the, se, x1_tm, xn2T, at_tm = o_sb, gl, r1T, xnT, r2T
        aT, acc, fin = hm[:, 0:T], hm[:, T:2 * T], hm[:, 2 * T:3 * T]

        bank = [ctx.enter_context(nc.psum_tensor(f"bank{i}", [P, 512], F32)) for i in range(8)]
        BANKS = {
            "head": lambda: 4, "normT": lambda n: 4, "k": lambda c: c % 3, "bg": lambda c: (NT + c) % 3,
            "kT": lambda c: (2 * NT + c) % 3, "G": lambda c: (3 * NT + c) % 3, "qT": lambda h: (4 * NT + h) % 3,
            "V": lambda k, c: c % 2, "VX": lambda k, c: c % 2, "ZV": lambda k, c: 2,
            "B": lambda c: 0, "P": lambda c: 1, "U": lambda c: 2, "O": lambda c: 1, "dS": lambda c: 2, "oT0": lambda: 0,
            "fq": lambda l, c: 3, "fk": lambda l, c: 4, "fv": lambda l, c: 5, "fqT": lambda l, c: 3, "fkT": lambda l, c: 4,
            "fS": lambda l, i: 3 + i % 2, "fPT": lambda l, i: 5, "fO": lambda l, c: 6, 
            "fwo": lambda l: 7, "h2tm": lambda l: 3, "fg": lambda l, j: (3, 5, 3)[j], "fa": lambda l, j: (4, 6, 4)[j],
            "fw2": lambda l: 7, "x1": lambda: 3,
            "lat": lambda: 5, "latT": lambda: 7, "mq": lambda i: (3, 4, 5, 3)[i], "mv": lambda: 7, "mS": lambda h, t: 3 + t,
            "mrow": lambda g: 7, "mST": lambda h, t: t, "mPV": lambda g: 6, "matg": lambda g: 6, "aT": lambda: 7,
            "gate": lambda: 0, "eu": lambda e: (0, 6)[e % 2], "ew": lambda e: 1, "ey": lambda e: 2, "fin": lambda: 3}

        def place(name, *i):
            return bank[BANKS[name](*i)]

        zeros = hm[:, 0:T]
        X_zeroed = ctx.enter_context(nc.semaphore("X_zeroed"))
        late_loads = ctx.enter_context(nc.semaphore("late_loads"))
        setup_loads = ctx.enter_context(nc.semaphore("setup_loads"))
        zeroed, tables_done = ctx.enter_context(nc.semaphore("zeroed")), ctx.enter_context(nc.semaphore("tables_done"))
        signals = []

        def semaphore(name):
            signals.append(ctx.enter_context(nc.semaphore(name)))
            return signals[-1]

        x_loaded = semaphore("x_loaded")
        head_norm_done = semaphore("head_norm_done")
        head_psum = semaphore("head_psum")
        head_copied = semaphore("head_copied")
        norm_done = semaphore("norm_done")
        normT_psum = semaphore("normT_psum")
        h_done = semaphore("h_done")
        r_done = semaphore("r_done")
        k_psum = semaphore("k_psum")
        k_copied = semaphore("k_copied")
        ksq_done = semaphore("ksq_done")
        kss_done = semaphore("kss_done")
        krs_done = semaphore("krs_done")
        kn_done = semaphore("kn_done")
        kT_psum = semaphore("kT_psum")
        kT_copied = semaphore("kT_copied")
        qT_psum = semaphore("qT_psum")
        qT_copied = semaphore("qT_copied")
        bg_psum = semaphore("bg_psum")
        th_done = semaphore("th_done")
        beta_done = semaphore("beta_done")
        gs_done = semaphore("gs_done")
        G_psum = semaphore("G_psum")
        L_done = semaphore("L_done")
        B_psum = semaphore("B_psum")
        Bm_done = semaphore("Bm_done")
        V_psum = semaphore("V_psum")
        Vm_done = semaphore("Vm_done")
        ZV_psum = semaphore("ZV_psum")
        VX_psum = semaphore("VX_psum")
        L_kept = [semaphore("L_kept_even"), semaphore("L_kept_odd")]
        Lb_loaded = semaphore("Lb_loaded")
        Xb_done = semaphore("Xb_done")
        Xb_kept = semaphore("Xb_kept")
        L_loaded = [semaphore("L_loaded_even"), semaphore("L_loaded_odd")]
        X_loaded = [semaphore("X_loaded_even"), semaphore("X_loaded_odd")]
        Z_done = semaphore("Z_done")
        X_done = semaphore("X_done")
        P_psum = semaphore("P_psum")
        R_done = semaphore("R_done")
        U_psum = semaphore("U_psum")
        U_copied = semaphore("U_copied")
        O_psum = semaphore("O_psum")
        o_copied = semaphore("o_copied")
        dS_psum = semaphore("dS_psum")
        S_done = semaphore("S_done")
        osq_done = semaphore("osq_done")
        ors_done = semaphore("ors_done")
        on_done = semaphore("on_done")
        og_done = semaphore("og_done")
        oT0_psum = semaphore("oT0_psum")
        oT0_copied = semaphore("oT0_copied")
        fq_psum = semaphore("fq_psum")
        fk_psum = semaphore("fk_psum")
        fv_psum = semaphore("fv_psum")
        fv_copied = semaphore("fv_copied")
        fsq_done = semaphore("fsq_done")
        fss_done = semaphore("fss_done")
        ft1_done = semaphore("ft1_done")
        frot_done = semaphore("frot_done")
        fsum_done = semaphore("fsum_done")
        frs_done = semaphore("frs_done")
        fn_done = semaphore("fn_done")
        fqT_psum = semaphore("fqT_psum")
        fkT_psum = semaphore("fkT_psum")
        fqT_lo = semaphore("fqT_lo")
        fqT_hi = semaphore("fqT_hi")
        fkT_copied = semaphore("fkT_copied")
        fS_psum = semaphore("fS_psum")
        fmax_done = semaphore("fmax_done")
        fexp_done = semaphore("fexp_done")
        fPT_psum = semaphore("fPT_psum")
        fPT_copied = semaphore("fPT_copied")
        fO_psum = semaphore("fO_psum")
        fnorm_done = semaphore("fnorm_done")
        fprec_done = semaphore("fprec_done")
        foT_copied = semaphore("foT_copied")
        fwo_psum = semaphore("fwo_psum")
        r1_done = semaphore("r1_done")
        h2_done = semaphore("h2_done")
        h2tm_psum = semaphore("h2tm_psum")
        hn_done = semaphore("hn_done")
        fa_psum = semaphore("fa_psum")
        fg_psum = semaphore("fg_psum")
        gelu_done = semaphore("gelu_done")
        hm_done = semaphore("hm_done")
        fw2_psum = semaphore("fw2_psum")
        x1_psum = semaphore("x1_psum")
        x1_done = semaphore("x1_done")
        xn2_copied = semaphore("xn2_copied")
        lat_psum = semaphore("lat_psum")
        lat_done = semaphore("lat_done")
        latT_psum = semaphore("latT_psum")
        latT_done = semaphore("latT_done")
        mq_psum = semaphore("mq_psum")
        rope_done = semaphore("rope_done")
        qkf_done = semaphore("qkf_done")
        split_done = semaphore("split_done")
        split2_done = semaphore("split2_done")
        parts_kept = semaphore("parts_kept")
        parts_sent = semaphore("parts_sent")
        rows_filled = semaphore("rows_filled")
        mv_psum = semaphore("mv_psum")
        vaug_done = semaphore("vaug_done")
        vaug_zeroed = semaphore("vaug_zeroed")
        mS_psum = semaphore("mS_psum")
        nmx_done = semaphore("nmx_done")
        mrow_psum = semaphore("mrow_psum")
        mrow_done = semaphore("mrow_done")
        mrow_sent = semaphore("mrow_sent")
        mST_psum = semaphore("mST_psum")
        mexp_done = semaphore("mexp_done")
        mPV_psum = semaphore("mPV_psum")
        atg_done = semaphore("atg_done")
        matg_psum = semaphore("matg_psum")
        at_done = semaphore("at_done")
        aT_psum = semaphore("aT_psum")
        aT_copied = semaphore("aT_copied")
        gate_psum = semaphore("gate_psum")
        gz_done = semaphore("gz_done")
        gexp_done = semaphore("gexp_done")
        ge_done = semaphore("ge_done")
        eu_psum = semaphore("eu_psum")
        ew_psum = semaphore("ew_psum")
        eth_done = semaphore("eth_done")
        es_done = semaphore("es_done")
        eh_done = semaphore("eh_done")
        ey_psum = semaphore("ey_psum")
        ey_done = semaphore("ey_done")
        fin_psum = semaphore("fin_psum")
        fin_done = semaphore("fin_done")
        out_stored = semaphore("out_stored")
        dve_chain = semaphore("dve_chain")
        numbers = sorted(s.num for s in signals)
        assert numbers == list(range(numbers[0], numbers[0] + len(numbers)))

        chain = [0]
        tt, ts, stt = nc.vector.tensor_tensor, nc.vector.tensor_scalar, nc.vector.scalar_tensor_tensor

        def link(ins):
            chain[0] += 1
            ins.then_inc(dve_chain, 1)
            nc.vector.wait_ge(dve_chain, chain[0])

        def rsqrt(dst, src, n, done):
            y, t = rs_out[:, 0:n], rs_tmp[:, 0:n]
            link(ts(y.bitcast(I32), src.bitcast(I32), -0.5, float(0x5f3759df), ALU.mult, ALU.add))
            for i in range(3):
                link(tt(t, y, y, ALU.mult))
                link(stt(t, t, -0.5, src, ALU.mult, ALU.mult))
                last = stt(y if i < 2 else dst, t, 1.5, y, ALU.add, ALU.mult)
                if i < 2 or done is None:
                    link(last)
                else:
                    last.then_inc(done, 1)

        def layernorm(dst, src, width, done):
            for c in range(NT):
                link(nc.vector.bn_stats(v3(stats[:], NT)[:, c], src[:, c])) if c == NT - 1 else nc.vector.bn_stats(
                    v3(stats[:], NT)[:, c], src[:, c])
            for c in range(NT):
                m = nc.vector.bn_aggr(v3(mv[:], NT)[:, c], v3(stats[:], NT)[:, c])
            link(m)
            link(ts(rs_in[:, 0:NT], v3(mv[:], NT)[:, :, 1], EPS, None, ALU.add))
            rsqrt(rs_in[:, NT:2 * NT], rs_in[:, 0:NT], NT, None)
            for c in range(NT):
                m = ts(dst[:, c], src[:, c], v3(mv[:], NT)[:, c, 0:1], rs_in[:, NT + c:NT + c + 1], ALU.subtract, ALU.mult)
            m.then_inc(done, 1)

        def head_norm():
            layernorm(v3(norm_tm[:], NT), v3(x_tm[:], NT), D, head_norm_done)

        def head_transpose():
            nc.tensor.wait_ge(head_norm_done, 1)
            for i in range(NT):
                m = nc.tensor.transpose(place("head")[:, i * P:(i + 1) * P], v3(norm_tm[:], NT)[:, i], C("ident"))
            m.then_inc(head_psum, 1)

        def head_copy():
            nc.vector.wait_ge(head_psum, 1)
            nc.vector.tensor_copy(xnT[:], place("head")[:])
            nc.vector.tensor_copy(hT[0:64, :], place("head")[0:64, :])
            nc.vector.tensor_copy(hT[64:P, 1:T], place("head")[64:P, 0:T - 1]).then_inc(head_copied, 1)
            nc.vector.wait_ge(head_copied, 1)

        early_w, early_c = W_AT["wo0"][0], C_AT["rcos"][0]
        with nc.Block(no_gpsimd_drain=True) as block:
            @block.tensor
            def _(pe):
                pe.wait_ge(setup_loads, 16 * 5)
                head_transpose()

            @block.sync
            def _(sp):
                sp.dma_start(v3(x_tm[:], NT), x[0:1].rearrange("a (t p) d -> p (a t) d", p=P)).then_inc(setup_loads, 16)
                sp.dma_start(c_sb[:, 0:early_c], consts[:, 0:early_c]).then_inc(setup_loads, 16)
                sp.dma_start(w_sb[:, 0:early_w], weights[:, 0:early_w]).then_inc(setup_loads, 16)
                sp.dma_start(w_sb[:, early_w:], weights[:, early_w:]).then_inc(late_loads, 16)
                sp.dma_start(c_sb[:, early_c:], consts[:, early_c:]).then_inc(late_loads, 16)
                sp.wait_ge(setup_loads, 16 * 5)

            @block.scalar
            def _(act):
                act.dma_start(shared[:, 0:B_N], consts_bf).then_inc(setup_loads, 16)
                act.dma_start(r_sb[:], rows.to_broadcast([P, R_N])).then_inc(setup_loads, 16)

            @block.gpsimd
            def _(pool):
                for part in (zeros, qTz[:], p_sb[:], latT[:], hT[:, 0:1], h2T[:, 0:1]):
                    nc.gpsimd.memset(part, 0.0).then_inc(zeroed, 1)
                pool.wait_ge(zeroed, 6)
                for c in range(NT):
                    pool.dma_start(in_dram(X_dram, c), v3(zeros, H0)).then_inc(X_zeroed, 16)

            @block.vector
            def _(dve):
                dve.wait_ge(setup_loads, 16 * 5)
                head_norm()
                nc.vector.tensor_copy(b_sb[:], shared[:, 0:B_N]).then_inc(tables_done, 1)
                h = DF // 2
                for l in range(DEPTH):
                    for cos, sin, row, c_out, s_out in (("qcos", "qsin", "qs", "qc", "qs"), ("kcos", "ksin", "ks", "kc", "ks")):
                        g = R(row)[:, l * DF:(l + 1) * DF]
                        c_out, s_out = v3(tab[c_out][l], NT), v3(tab[s_out][l], NT)
                        tt, sines = nc.vector.tensor_tensor, v3(C(sin), NT)
                        tt(c_out, v3(C(cos), NT), repeat(g, NT), ALU.mult).then_inc(tables_done, 1)
                        tt(s_out[:, :, 0:h], sines[:, :, 0:h], repeat(g[:, h:], NT), ALU.mult).then_inc(tables_done, 1)
                        tt(s_out[:, :, h:], sines[:, :, h:], repeat(g[:, 0:h], NT), ALU.mult).then_inc(tables_done, 1)
                nc.vector.tensor_scalar(v3(norm_w[:], H0), repeat(R("norm_w"), H0), -0.5 * DK ** -0.5, None, ALU.mult)\
                    .then_inc(tables_done, 1)
                dve.wait_ge(tables_done, 6 * DEPTH + 2)
                dve.wait_ge(zeroed, 6)
                head_copy()

        nc.sync.sem_clear(range(numbers[0], numbers[-1] + 1))
        nc.all_engine_barrier()

        def steps_delta():
            s = [("k", c) for c in range(NT)] + [("krs",)] + [("bg", c) for c in range(NT)]
            s += [("kT", c) for c in range(NT)] + [("gram", c) for c in range(NT)]
            s += [("qT", h) for h in range(H0)] + [("solve",)]
            for two in ((0, 1), (2, 3)):
                s += [("inv_load", c) for c in two]
                for k in range(LEVELS):
                    s += [("inv_v", k, c) for c in two]
                    if k:
                        s += [("inv_zx", k, c) for c in two]
                for c in two:
                    s += [("seq_b", c), ("seq_p", c), ("seq_u", c), ("seq_o", c)]
            return s + [("delta_norm",), ("oT0",)]

        def steps_ffn(l):
            s = []
            s += [("fqkv", l, 0), ("frs", l, 0), ("fqkv", l, 1), ("frs", l, 1)]
            n = NT * NPAIR
            for i in range(n + 4):
                if i < n:
                    if i % NPAIR == 0:
                        c = i // NPAIR
                        s += [("fT", l, c)] + ([("fqkv", l, c + 2), ("frs", l, c + 2)] if c + 2 < NT else [])
                    s += [("fS", l, i)]
                if 1 <= i <= n:
                    s += [("fnorm", l, i - 1)]
                if 2 <= i < n + 2:
                    s += [("fPT", l, i - 2)]
                if i >= 7 and i % NPAIR == 3:
                    s += [("fwo", l, (i - 7) // NPAIR)]
                if 3 <= i < n + 3:
                    s += [("fPV", l, i - 3)]
            return s + [("fres", l), ("fln", l), ("hnT", l)] + [("fw1", l, j) for j in range(3)] + [("fw2", l)]

        def steps_latent():
            s = []
            for h in range(HM + LEAD):
                if h < HM:
                    s += [("mS", h)]
                    if h % GROUP == GROUP - 1:
                        s += [("mrow", h // GROUP)]
                done = h - LEAD
                if done >= 0:
                    s += [("mST", done)] + ([("head_norm",)] if done == 8 else [("head_T",)] if done == 12 else [])
                    if done % GROUP == 1 and done > GROUP:
                        s += [("mPV", done // GROUP - 1), ("matg", done // GROUP - 1)]
            return s + [("mPV", HM // GROUP - 1), ("matg", HM // GROUP - 1), ("aT",)]

        def steps_moe():
            return [("gate",)] + [s for e in range(NE + 1) for s in ([("e_up", e), ("e_down", e - 1)] if e else [("e_up", e)])]

        def fill(main, other, counts):
            assert len(counts) == len(main) and sum(map(int, counts)) == len(other)
            out, other = [], list(other)
            for step, n in zip(main, counts):
                out.append(step)
                for _ in range(int(n)):
                    out.append(other.pop(0))
            return out

        latent = steps_latent()
        first = latent.index(("mST", 0))
        schedule = fill(steps_ffn(0) + steps_ffn(1), steps_delta(), DELTA_AFTER) + [("x1",), ("xn2T",)]
        schedule += fill([("lat",), ("mq",), ("latT",), ("mk",), ("mv",)] + latent[:first], steps_moe(), EXPERTS_AFTER) + latent[first:] + [("final",)]

        def walk(parts):
            for name, *args in schedule:
                if name in parts:
                    parts[name](*args)

        def pair(l, i):
            return l * NT * NPAIR + i

        def at_level(k, c, levels, first=0):
            return c // 2 * 2 * levels + 2 * (k - first) + c % 2

        with nc.Fori(0, BATCH) as b:
            with nc.Block(no_gpsimd_drain=True) as block:
                @block.tensor
                def _(pe):
                    mm = nc.tensor.matmul
                    ident = C("ident")
                    def transposes(ps, src, n=4, width=P, last=None):
                        for i in range(n):
                            m = nc.tensor.transpose(ps[0:width, i * P:(i + 1) * P], src(i), ident)
                        return m

                    def k(c):
                        if c == 3:
                            pe.wait_ge(ksq_done, 1)
                        ps = place("k", c)
                        mm(ps[:], xnT[:, c * P:(c + 1) * P], W("wk"), start=True, stop=True).then_inc(k_psum, 1)

                    def qT_(h):
                        if h < 3:
                            pe.wait_ge(L_done, h + 2)
                        else:
                            pe.wait_ge(qT_copied, 1)
                        ps = place("qT", h)
                        mm(ps[:], W("wq")[:, h * DK:(h + 1) * DK], xnT[:], start=True, stop=True).then_inc(qT_psum, 1)

                    def bg(c):
                        if c < 3:
                            pe.wait_ge(ksq_done, c + 2)
                        else:
                            pe.wait_ge(gs_done, 1)
                        ps = place("bg", c)
                        mm(ps[:, 0:NBG], xnT[:, c * P:(c + 1) * P], W("wbg"), start=True, stop=True).then_inc(bg_psum, 1)

                    def kT_(c):
                        if c < 3:
                            pe.wait_ge(gs_done, c + 2)
                        else:
                            pe.wait_ge(kT_copied, 1)
                        ps = place("kT", c)
                        pe.wait_ge(kn_done, c + 1)
                        transposes(ps, lambda i: v4(kn[:], NT, H0)[:, c, i]).then_inc(kT_psum, 1)

                    def gram(c):
                        kc = v4(kT[:], NT, H0)[:, c]
                        ps = place("G", c)
                        pe.wait_ge(kT_copied, min(c + 2, NT))
                        if c == 3:
                            pe.wait_ge(L_done, 1)
                        for h in range(H0):
                            m = mm(ps[:, h * P:(h + 1) * P], kc[:, h], kc[:, h], start=True, stop=True)
                        m.then_inc(G_psum, 1)

                    def seq_b(c):
                        kc = v4(kT[:], NT, H0)[:, c]
                        ps = place("B", c)
                        if c:
                            pe.wait_ge(Bm_done, c)
                        pe.wait_ge(qT_copied, H0)
                        for h in range(H0):
                            m = mm(ps[:, h * P:(h + 1) * P], kc[:, h], qT[:, h * T + c * P:h * T + (c + 1) * P], start=True, stop=True)
                        m.then_inc(B_psum, 1)

                    def inv_v(k, c):
                        n = at_level(k, c, LEVELS)
                        Lc, Xc, Zc = v4(L, 2, H0)[:, c % 2], v4(X, 2, H0)[:, c % 2], v4(Z, NT, H0)[:, c]
                        ps = place("V", k, c)
                        if k == 0:
                            pe.wait_ge(X_loaded[c % 2], 16 * (c // 2 + 1))
                            if c < 2:
                                pe.wait_ge(qT_copied, 3 + c)
                            elif c == 2:
                                pe.wait_ge(Bm_done, 2)
                            else:
                                pe.wait_ge(o_copied, 2)
                            m = transposes(ps, lambda i: Xc[:, i])
                        else:
                            if k == 1:
                                pe.wait_ge(L_loaded[c % 2], 16 * (c // 2 + 1))
                            else:
                                pe.wait_ge(X_done, at_level(k, c, LEVELS - 2, 1) - 1)
                            pe.wait_ge(Z_done, n - 1)
                            for h in range(H0):
                                m = mm(ps[:, h * P:(h + 1) * P], Lc[:, h], Zc[:, h], start=True, stop=True)
                        m.then_inc(V_psum, 1)

                    def inv_zx(k, c):
                        n = at_level(k, c, LEVELS)
                        Xc, Vc = v4(X, 2, H0)[:, c % 2], v4(Vm, 2, H0)[:, c % 2]
                        pe.wait_ge(Z_done, n)
                        if k == 1 and c == 2:
                            pe.wait_ge(S_done, 2)
                        ps = place("ZV", k, c)
                        pe.wait_ge(Vm_done, at_level(k, c, LEVELS - 1, 1) + 1)
                        for h in range(H0):
                            m = mm(ps[:, h * P:(h + 1) * P], Xc[:, h], Vc[:, h], start=True, stop=True)
                        m.then_inc(ZV_psum, 1)
                        if k < LEVELS - 1:
                            ps = place("VX", k, c)
                            for h in range(H0):
                                m = mm(ps[:, h * P:(h + 1) * P], Vc[:, h], Xc[:, h], start=True, stop=True)
                            m.then_inc(VX_psum, 1)

                    def seq_p(c):
                        if c:
                            pe.wait_ge(o_copied, c)
                        ps = place("P", c)
                        m = mm(ps[:, 0:P], xnT[:, c * P:(c + 1) * P], W("wv"), start=True, stop=c == 0, skip_group_check=True)
                        if c:
                            pe.wait_ge(S_done, c)
                            for h in range(H0):
                                m = mm(ps[:, h * DV:(h + 1) * DV], v4(kT[:], NT, H0)[:, c, h], Sn[:, h * DV:(h + 1) * DV],
                                       start=False, stop=True, skip_group_check=True)
                        m.then_inc(P_psum, 1)

                    def seq_u(c):
                        if c % 2 == 0:
                            pe.wait_ge(Z_done, LEVELS * (c + 2))
                        ps = place("U", c)
                        pe.wait_ge(R_done, c + 1)
                        pe.wait_ge(Z_done, at_level(LEVELS - 1, c, LEVELS) + 1)
                        for h in range(H0):
                            m = mm(ps[:, h * DV:(h + 1) * DV], v4(Z, NT, H0)[:, c, h], R_sb[:, h * DV:(h + 1) * DV], start=True, stop=True)
                        m.then_inc(U_psum, 1)

                    def seq_o(c):
                        pe.wait_ge(U_copied, c + 1)
                        pe.wait_ge(Bm_done, c + 1)
                        ps = place("O", c)
                        for h in range(H0):
                            u = U_sb[:, h * DV:(h + 1) * DV]
                            m = mm(ps[:, h * DV:(h + 1) * DV], v3(Bm, H0)[:, h], u, start=True, stop=c == 0)
                            if c:
                                m = mm(ps[:, h * DV:(h + 1) * DV], qT[:, h * T + c * P:h * T + (c + 1) * P],
                                       Sn[:, h * DV:(h + 1) * DV], start=False, stop=True)
                        m.then_inc(O_psum, 1)
                        if c < NT - 1:
                            ps = place("dS", c)
                            for h in range(H0):
                                m = mm(ps[:, h * DV:(h + 1) * DV], v4(kn[:], NT, H0)[:, c, h], U_sb[:, h * DV:(h + 1) * DV],
                                       start=True, stop=True)
                            m.then_inc(dS_psum, 1)

                    def oT0_():
                        ps = place("oT0")
                        pe.wait_ge(og_done, 1)
                        transposes(ps, lambda i: v3(o_all[:], NT)[:, i]).then_inc(oT0_psum, 1)

                    def fqkv(l, c):
                        n = l * NT + c + 1
                        src = hT[:, c * P:(c + 1) * P]
                        if l:
                            pe.wait_ge(h_done, 1)
                        w = W(f"wqkv{l}")
                        if c == 1:
                            pe.wait_ge(fsq_done, 2 * n - 3)
                            pe.wait_ge(frot_done, 2 * n - 3)
                        elif c >= 2:
                            pe.wait_ge(fqT_lo, n - 2)
                            pe.wait_ge(fqT_hi, n - 2)
                        mm(place("fq", l, c)[:], src, w[:, 0:T], start=True, stop=True).then_inc(fq_psum, 1)
                        if c == 1:
                            pe.wait_ge(fsq_done, 2 * n - 2)
                            pe.wait_ge(frot_done, 2 * n - 2)
                        elif c >= 2:
                            pe.wait_ge(fkT_copied, n - 2)
                        mm(place("fk", l, c)[:], src, w[:, T:2 * T], start=True, stop=True).then_inc(fk_psum, 1)
                        if c in (1, 2):
                            pe.wait_ge(fv_copied, n - 1)
                        elif c == 3:
                            pe.wait_ge(fPT_copied, pair(l, 1) + 1)
                        mm(place("fv", l, c)[:], src, w[:, 2 * T:3 * T], start=True, stop=True).then_inc(fv_psum, 1)

                    def fT(l, c):
                        n = l * NT + c + 1
                        pe.wait_ge(fn_done, 2 * n)
                        if c == 0:
                            pe.wait_ge(frot_done, 2 * n + 1)
                        else:
                            pe.wait_ge(fexp_done, 2 * pair(l, c * NPAIR - 2) + 2)
                        ps = place("fqT", l, c)
                        transposes(ps, lambda i: v4(q_f[:], 2, 4)[:, c % 2, i]).then_inc(fqT_psum, 1)
                        if c == 0:
                            pe.wait_ge(frot_done, 2 * n + 2)
                        else:
                            pe.wait_ge(fexp_done, 2 * pair(l, c * NPAIR - 1) + 2)
                        ps = place("fkT", l, c)
                        transposes(ps, lambda i: v4(k_f[:], 2, 4)[:, c % 2, i]).then_inc(fkT_psum, 1)

                    def fS(l, i):
                        c, g = divmod(i, NPAIR)
                        n = l * NT + c + 1
                        pe.wait_ge(fqT_lo, n)
                        pe.wait_ge(fqT_hi, n)
                        pe.wait_ge(fkT_copied, n)
                        if g >= 2:
                            pe.wait_ge(fexp_done, 2 * pair(l, i - 2) + 2)
                        elif c + 2 < NT:
                            pe.wait_ge(frot_done, 2 * (n + 2) - 1 + g)
                            pe.wait_ge(fsq_done, 2 * (n + 2) - 1 + g)
                        ps = v3(place("fS", l, i)[:], 2)
                        lo = 128 if c == 0 else 64
                        mm(ps[:, :, lo:256], B("identb"), repeat(B("band")[:, lo - 64:192], 2), start=True, stop=False,
                           skip_group_check=True)
                        keys = kTf[:, g * T + c * P - 128 + lo:g * T + (c + 1) * P]
                        for j in range(2):
                            q = v4(qTz[:], 2, HF)[:, c % 2, 2 * g + j]
                            m = mm(ps[:, j, lo:256], q, keys, start=False, stop=True, skip_group_check=True)
                        m.then_inc(fS_psum, 1)

                    def fPT(l, i):
                        c = i // NPAIR
                        n = pair(l, i) + 1
                        if i in (0, 2):
                            pe.wait_ge(fv_copied, l * NT + (3 if i == 0 else 4))
                        else:
                            pe.wait_ge(fPT_copied, n - 1)
                        ps = place("fPT", l, i)
                        pe.wait_ge(fnorm_done, n)
                        p = v4(p_sb[:], 2, 4)[:, i % 2]
                        for j in ((1, 3) if c == 0 else range(4)):
                            m = nc.tensor.transpose(ps[:, j * P:(j + 1) * P], p[:, j], ident)
                        m.then_inc(fPT_psum, 1)

                    def fPV(l, i):
                        c, g = divmod(i, NPAIR)
                        ps = place("fO", l, c)
                        pe.wait_ge(fPT_copied, pair(l, i) + 1)
                        if g == 0:
                            pe.wait_ge(fv_copied, l * NT + c + 1)
                        pt = v4(pT[:], 2, 4)[:, i % 2]
                        for k in ((0, 1) if c else (1,)):
                            for j in range(2):
                                v = (c - 1 + k) * T + (2 * g + j) * DF
                                m = mm(ps[j * DF:(j + 1) * DF, g * P:(g + 1) * P], v_f[:, v:v + DF], pt[:, 2 * j + k],
                                       start=k == (0 if c else 1), stop=k == 1, skip_group_check=True)
                        m.then_inc(fO_psum, 1)

                    def fwo(l, c):
                        n = l * NT + c + 1
                        if n == 1:
                            pe.wait_ge(late_loads, 32)
                        pe.wait_ge(foT_copied, n)
                        for j in range(4):
                            m = mm(place("fwo", l)[:, c * P:(c + 1) * P], W(f"wof{l}")[:, j * D:(j + 1) * D],
                                   v4(oTf, 2, 4)[:, c % 2, j], start=j == 0, stop=j == 3)
                        m.then_inc(fwo_psum, 1)

                    def fln(l):
                        ps = place("h2tm", l)
                        pe.wait_ge(h2_done, l + 1)
                        transposes(ps, lambda i: h2T[:, i * P:(i + 1) * P]).then_inc(h2tm_psum, 1)

                    def hnT_(l):
                        ps = place("normT", l)
                        pe.wait_ge(norm_done, l + 1)
                        transposes(ps, lambda i: v3(norm_tm[:], NT)[:, i]).then_inc(normT_psum, 1)

                    def fw1(l, j):
                        at, m = HID_TILES[j]
                        n = 3 * l + j + 1
                        pe.wait_ge(hn_done, l + 1)
                        if j == 2:
                            pe.wait_ge(gelu_done, 3 * l + 1)
                            pe.wait_ge(hm_done, 3 * l + 1)
                        ps = place("fg", l, j)
                        mm(ps[0:m, :], W(f"w1{l}")[:, HID + at:HID + at + m], hnT[:], start=True, stop=True).then_inc(fg_psum, 1)
                        ps = place("fa", l, j)
                        mm(ps[0:m, :], W(f"w1{l}")[:, at:at + m], hnT[:], start=True, stop=True).then_inc(fa_psum, 1)

                    def fw2(l):
                        ps = place("fw2", l)
                        for j, (_, m) in enumerate(HID_TILES):
                            pe.wait_ge(hm_done, 3 * l + j + 1)
                            i = mm(ps[:], W(f"w2{l}")[0:m, j * D:(j + 1) * D], hm[0:m, j * T:(j + 1) * T], start=j == 0, stop=j == 2)
                        i.then_inc(fw2_psum, 1)

                    def x1():
                        ps = place("x1")
                        pe.wait_ge(r_done, DEPTH)
                        pe.wait_ge(oT0_copied, 1)
                        for c in range(NT):
                            o = ps[:, c * P:(c + 1) * P]
                            mm(o, oT0[:, c * P:(c + 1) * P], W("wo0"), start=True, stop=False)
                            m = mm(o, r2T[:, c * P:(c + 1) * P], ident, start=False, stop=True)
                        m.then_inc(x1_psum, 1)

                    def xn2T_():
                        ps = place("normT", 2)
                        pe.wait_ge(norm_done, 3)
                        transposes(ps, lambda i: v3(norm_tm[:], NT)[:, i]).then_inc(normT_psum, 1)

                    def lat():
                        ps = place("lat")
                        pe.wait_ge(xn2_copied, 1)
                        for c in range(NT):
                            m = mm(ps[:, c * LAT:(c + 1) * LAT], xn2T[:, c * P:(c + 1) * P], W("Wdkv"), start=True, stop=True)
                        m.then_inc(lat_psum, 1)

                    def latT_():
                        ps = place("latT")
                        pe.wait_ge(lat_done, 1)
                        transposes(ps, lambda i: v3(lat_tm[:], NT)[:, i], width=LAT).then_inc(latT_psum, 1)

                    def project(first, weights, src):
                        for i, w in enumerate(weights):
                            if first + i == 3:
                                pe.wait_ge(rope_done, 1)
                            ps = place("mq", first + i)
                            mm(ps[:], W(w), src, start=True, stop=True).then_inc(mq_psum, 1)

                    def mq():
                        project(0, ("Wq", "Wqr"), xn2T[:])

                    def mk():
                        pe.wait_ge(latT_done, 1)
                        project(2, ("Wuk", "Wukr"), latT[:])

                    def mv_():
                        ps = place("mv")
                        for c in range(NT):
                            m = mm(ps[:, c * P:(c + 1) * P], latT[:, c * P:(c + 1) * P], W("Wuv"), start=True, stop=True)
                        m.then_inc(mv_psum, 1)

                    def mS(h):
                        if h == 0:
                            pe.wait_ge(parts_sent, 12 * 16)
                            pe.wait_ge(rows_filled, 32)
                        for t, tiles in enumerate(((0, 2), (1,), (3,))):
                            if h:
                                pe.wait_ge(nmx_done, 4 * (h - 1) + (2, 3, 4)[t])
                            ps = place("mS", h, t)
                            at = 0
                            for c in tiles:
                                n = (c + 1) * P
                                mm(ps[:, at + c * P:at + n], B("identb"), B("causal"), start=True, stop=False, skip_group_check=True)
                                m = mm(ps[:, at:at + n], Qst[:, h * T + c * P:h * T + (c + 1) * P], Kst[:, h * T:h * T + n],
                                       start=False, stop=True, skip_group_check=True)
                                at += n
                            m.then_inc(mS_psum, 1)

                    def mrow(g):
                        pe.wait_ge(nmx_done, NT * GROUP * (g + 1))
                        if g:
                            pe.wait_ge(mrow_done, g)
                        else:
                            pe.wait_ge(vaug_done, 1)
                        nc.tensor.transpose(place("mrow", g)[0:NROW, 0:P], nmx[:, g * NROW:(g + 1) * NROW], ident)\
                            .then_inc(mrow_psum, 1)

                    def mST(h):
                        if h % GROUP == 0:
                            pe.wait_ge(mrow_sent, 48 * (h // GROUP + 1))
                        if h == 0:
                            pe.wait_ge(es_done, NE + 1)
                            pe.wait_ge(eh_done, NE + 1)
                            pe.wait_ge(ey_done, NE)
                        for t, tiles in enumerate(((0,), (1, 3), (2,))):
                            if h:
                                pe.wait_ge(mexp_done, 3 * (h - 1) + t + 1)
                            ps = place("mST", h, t)
                            at = 0
                            for j in tiles:
                                n = T - j * P
                                mm(ps[:, at:at + P], B("identb"), B("causalT"), start=True, stop=False, skip_group_check=True)
                                m = mm(ps[:, at:at + n], Kst[:, h * T + j * P:h * T + (j + 1) * P], Qst[:, h * T + j * P:(h + 1) * T],
                                       start=False, stop=True, skip_group_check=True)
                                at += n
                            m.then_inc(mST_psum, 1)

                    def mPV(g):
                        if g:
                            pe.wait_ge(at_done, g)
                        ps = place("mPV", g)
                        pe.wait_ge(mexp_done, 3 * GROUP * (g + 1))
                        pe.wait_ge(vaug_done, 1)
                        start = {0: 0, 1: T, 3: 2 * T - P, 2: 2 * T}
                        for j in range(NT):
                            n = T - j * P
                            for i in range(GROUP):
                                h = GROUP * g + i
                                m = mm(ps[VW * i:VW * (i + 1), j * P:T], v3(vaug[:], NT * HM)[:, j * HM + h],
                                       PTm[h % PT_SLOTS][:, start[j]:start[j] + n], start=j == 0, stop=j == NT - 1,
                                       skip_group_check=True)
                        m.then_inc(mPV_psum, 1)

                    def matg(g):
                        ps = place("matg", g)
                        pe.wait_ge(atg_done, g + 1)
                        transposes(ps, lambda i: atg[:, (g % 2) * T + i * P:(g % 2) * T + (i + 1) * P]).then_inc(matg_psum, 1)

                    def aT_():
                        ps = place("aT")
                        pe.wait_ge(at_done, HM // GROUP)
                        transposes(ps, lambda i: v3(at_tm[:], NT)[:, i]).then_inc(aT_psum, 1)

                    def gate():
                        ps = place("gate")
                        pe.wait_ge(xn2_copied, 1)
                        for c in range(NT):
                            m = mm(ps[:, c * NE:(c + 1) * NE], xn2T[:, c * P:(c + 1) * P], W("gate"), start=True, stop=True)
                        m.then_inc(gate_psum, 1)

                    def e_up(e):
                        if e >= 2:
                            pe.wait_ge(es_done, e - 1)
                        elif e == 0:
                            pe.wait_ge(gz_done, 1)
                        ps = place("eu", e)
                        mm(ps[:], W(f"eu{e}"), xn2T[:], start=True, stop=True).then_inc(eu_psum, 1)
                        if e:
                            pe.wait_ge(eh_done, e)
                        ps = place("ew", e)
                        mm(ps[:], W(f"ew{e}"), xn2T[:], start=True, stop=True).then_inc(ew_psum, 1)

                    def e_down(e):
                        if e:
                            pe.wait_ge(ey_done, e)
                        ps = place("ey", e)
                        pe.wait_ge(eh_done, e + 1)
                        for c in range(NT):
                            m = mm(ps[:, c * P:(c + 1) * P], he[:, (e % 2) * T + c * P:(e % 2) * T + (c + 1) * P], W(f"ed{e}"),
                                   start=True, stop=True)
                        m.then_inc(ey_psum, 1)

                    def final():
                        ps = place("fin")
                        pe.wait_ge(eh_done, NE + 1)
                        pe.wait_ge(aT_copied, 1)
                        for c in range(NT):
                            o = ps[:, c * P:(c + 1) * P]
                            s = NE % 2 * T + c * P
                            mm(o, he[:, s:s + P], W(f"ed{NE}"), start=True, stop=False)
                            m = mm(o, aT[:, c * P:(c + 1) * P], W("Wo"), start=False, stop=True)
                        m.then_inc(fin_psum, 1)

                    walk({"k": k, "qT": qT_, "bg": bg, "kT": kT_, "gram": gram, "inv_v": inv_v, "inv_zx": inv_zx,
                          "seq_b": seq_b, "seq_p": seq_p, "seq_u": seq_u, "seq_o": seq_o, "oT0": oT0_, "fqkv": fqkv, "fT": fT, "fS": fS,
                          "fPT": fPT, "fPV": fPV, "fwo": fwo, "fln": fln, "hnT": hnT_, "fw1": fw1, "fw2": fw2,
                          "x1": x1, "xn2T": xn2T_, "lat": lat, "latT": latT_, "mq": mq, "mk": mk, "mv": mv_, "mS": mS,
                          "mrow": mrow, "head_T": head_transpose, "mST": mST, "mPV": mPV, "matg": matg, "aT": aT_, "gate": gate, "e_up": e_up,
                          "e_down": e_down, "final": final})

                @block.scalar
                def _(act):
                    af = nc.scalar.activation


                    def copy_out(dst, key, full, n, done):
                        act.wait_ge(full, n)
                        af(dst, place(*key)[:], ACT.Copy).then_inc(done, 1)

                    def k(c):
                        copy_out(kn[:, c * T:(c + 1) * T], ("k", c), k_psum, c + 1, k_copied)
                        af(kT[:, c * T:(c + 1) * T], place("k", c)[:], ACT.Square).then_inc(ksq_done, 1)

                    def bg(c):
                        act.wait_ge(bg_psum, c + 1)
                        af(th[:, c * NBG:(c + 1) * NBG], place("bg", c)[:, 0:NBG], ACT.Tanh, scale=0.5).then_inc(th_done, 1)

                    def seq_u(c):
                        act.wait_ge(U_psum, c + 1)
                        if c >= 2:
                            act.wait_ge(dS_psum, c)
                        elif c == 1:
                            act.wait_ge(dS_psum, 1)
                        af(U_sb[:], place("U", c)[:, 0:P], ACT.Copy).then_inc(U_copied, 1)

                    def seq_o(c):
                        act.wait_ge(O_psum, c + 1)
                        af(o_all[:, c * P:(c + 1) * P], place("O", c)[:, 0:P], ACT.Copy).then_inc(o_copied, 1)

                    def delta_norm():
                        act.wait_ge(o_copied, NT)
                        af(kn[:, 0:T], o_all[:], ACT.Square).then_inc(osq_done, 1)

                    def fqkv(l, c):
                        n = l * NT + c
                        act.wait_ge(fv_psum, n + 1)
                        if l:
                            act.wait_ge(fO_psum, NT * NPAIR)
                        af(v_f[:, c * T:(c + 1) * T], place("fv", l, c)[:], ACT.Copy).then_inc(fv_copied, 1)
                        for i, name in enumerate(("fq", "fk")):
                            m = 2 * n + i
                            if m >= 2:
                                act.wait_ge(fsum_done, m - 1)
                            af(rot[m % 2][:], place(name, l, c)[:], ACT.Square).then_inc(fsq_done, 1)

                    def fT(l, c):
                        n = l * NT + c
                        act.wait_ge(fqT_psum, n + 1)
                        if n >= 2:
                            act.wait_ge(fS_psum, (n - 1) * NPAIR)
                        half = slice(0, DF)
                        af(v4(qTz[:], 2, HF)[half, c % 2, 0:HF:2], v3(place("fqT", l, c)[:], NPAIR)[half], ACT.Copy).then_inc(fqT_lo, 1)
                        act.wait_ge(fkT_psum, n + 1)
                        if l:
                            act.wait_ge(fS_psum, NT * NPAIR)
                        af(v4(kTf[:], NPAIR, NT)[:, :, c], v3(place("fkT", l, c)[:], NPAIR), ACT.Copy).then_inc(fkT_copied, 1)

                    def fS(l, i):
                        c, g = divmod(i, NPAIR)
                        n = pair(l, i)
                        act.wait_ge(fmax_done, n + 1)
                        if n >= 2:
                            act.wait_ge(fPT_psum, n - 1)
                        lo = 128 if c == 0 else 64
                        for j in range(2):
                            h = c * HF + 2 * g + j
                            af(v4(p_sb[:], 2, 2)[:, i % 2, j, lo:256], v3(place("fS", l, i)[:], 2)[:, j, lo:256], ACT.Exp,
                               bias=nmax[:, h:h + 1], accum_out=psums[:, h:h + 1]).then_inc(fexp_done, 1)

                    def fPT(l, i):
                        n = pair(l, i)
                        act.wait_ge(fPT_psum, n + 1)
                        if n >= 2:
                            act.wait_ge(fO_psum, n - 1)
                        ps, dst = v4(place("fPT", l, i)[:], 2, 2), v4(pT[:, (i % 2) * T:(i % 2 + 1) * T], 2, 2)
                        if i // NPAIR == 0:
                            ps, dst = ps[:, :, 1], dst[:, :, 1]
                        af(dst, ps, ACT.Copy).then_inc(fPT_copied, 1)

                    def fPV(l, i):
                        c, g = divmod(i, NPAIR)
                        if g < NPAIR - 1:
                            return
                        n = l * NT + c
                        act.wait_ge(fO_psum, pair(l, i) + 1)
                        if n >= 2:
                            act.wait_ge(fwo_psum, n - 1)
                        af(oTf[:, c % 2 * T:(c % 2 + 1) * T], place("fO", l, c)[:], ACT.Copy).then_inc(foT_copied, 1)

                    def fw1(l, j):
                        _, m = HID_TILES[j]
                        n = 3 * l + j
                        act.wait_ge(late_loads, 32)
                        act.wait_ge(fg_psum, n + 1)
                        if n >= 2:
                            act.wait_ge(hm_done, n - 1)
                        af(gl[0:m, (n % 2) * T:(n % 2 + 1) * T], place("fg", l, j)[0:m, :], ACT.Gelu,
                           bias=W(f"cols{l}")[0:m, 3 + j:4 + j]).then_inc(gelu_done, 1)

                    def split(i):
                        act.wait_ge(qkf_done, i + 1)
                        af(parts[:, 3 * i * T:(3 * i + 1) * T], qkf[:, i * T:(i + 1) * T], ACT.Copy).then_inc(split_done, 1)
                        act.wait_ge(split2_done, 2 * i + 1)
                        af(parts[:, (3 * i + 1) * T:(3 * i + 2) * T], res[:, i * T:(i + 1) * T], ACT.Copy).then_inc(split_done, 1)

                    def mv_():
                        act.wait_ge(mv_psum, 1)
                        act.wait_ge(vaug_zeroed, 2)
                        af(v3(vaug[:], NT * HM)[:, :, 0:DM], v3(place("mv")[:], NT * HM), ACT.Copy).then_inc(vaug_done, 1)

                    def mST(h):
                        if h >= PT_SLOTS:
                            act.wait_ge(mPV_psum, (h - PT_SLOTS) // GROUP + 1)
                        for t, (at, n) in enumerate(((0, T), (T, T), (2 * T, 2 * P))):
                            act.wait_ge(mST_psum, 3 * h + t + 1)
                            af(PTm[h % PT_SLOTS][:, at:at + n], place("mST", h, t)[:, 0:n], ACT.Exp).then_inc(mexp_done, 1)

                    def mPV(g):
                        if g >= 2:
                            act.wait_ge(matg_psum, g - 1)
                        act.wait_ge(mPV_psum, g + 1)
                        af(atg[:, (g % 2) * T:(g % 2 + 1) * T], place("mPV", g)[:], ACT.Copy).then_inc(atg_done, 1)

                    def gate():
                        act.wait_ge(gz_done, 1)
                        af(gp[:], gz[:], ACT.Exp, scale=-1.0).then_inc(gexp_done, 1)

                    def e_up(e):
                        act.wait_ge(eu_psum, e + 1)
                        if e >= 2:
                            act.wait_ge(es_done, e - 1)
                        af(the[:, (e % 2) * T:(e % 2 + 1) * T], place("eu", e)[:], ACT.Tanh, scale=0.5).then_inc(eth_done, 1)

                    walk({"k": k,
                          "qT": lambda h: copy_out(qT[:, h * T:(h + 1) * T], ("qT", h), qT_psum, h + 1, qT_copied), "bg": bg,
                          "kT": lambda c: copy_out(kT[:, c * T:(c + 1) * T], ("kT", c), kT_psum, c + 1, kT_copied),
                          "seq_u": seq_u, "seq_o": seq_o, "delta_norm": delta_norm,
                          "oT0": lambda: copy_out(oT0[:], ("oT0",), oT0_psum, 1, oT0_copied), "fqkv": fqkv, "fT": fT,
                          "fS": fS, "fPT": fPT, "fPV": fPV, "fw1": fw1,
                          "xn2T": lambda: copy_out(xn2T[:], ("normT", 2), normT_psum, 3, xn2_copied),
                          "mq": lambda: split(0), "mk": lambda: split(1), "mv": mv_, "mST": mST, "mPV": mPV,
                          "aT": lambda: copy_out(aT[:], ("aT",), aT_psum, 1, aT_copied), "gate": gate, "e_up": e_up})

                @block.vector
                def _(dve):
                    tt, ts, stt = nc.vector.tensor_tensor, nc.vector.tensor_scalar, nc.vector.scalar_tensor_tensor


                    chain[0] = 0

                    def shifted(dst, src):
                        nc.vector.tensor_copy(dst[0:64, :], src[0:64, :])
                        return nc.vector.tensor_copy(dst[64:P, 1:T], src[64:P, 0:T - 1])

                    def k(c):
                        dve.wait_ge(ksq_done, c + 1)
                        nc.vector.tensor_reduce(kss[:, c * H0:(c + 1) * H0], v3(kT[:, c * T:(c + 1) * T], H0), AX, ALU.add).then_inc(kss_done, 1)

                    def krs_():
                        dve.wait_ge(kss_done, NT)
                        link(ts(kss[:], kss[:], 1e-12, None, ALU.add))
                        rsqrt(krs[:], kss[:], NT * H0, krs_done)

                    def bg(c):
                        t = th[:, c * NBG:(c + 1) * NBG]
                        dve.wait_ge(th_done, c + 1)
                        ts(beta[:, c * H0:(c + 1) * H0], t[:, 0:H0], 0.5, 0.5, ALU.mult, ALU.add).then_inc(beta_done, 1)
                        stt(gs[:, c * P:(c + 1) * P], t[:, H0:NBG], 1.0, place("bg", c)[:, H0:NBG], ALU.add, ALU.mult).then_inc(gs_done, 1)

                    def gram(c):
                        dve.wait_ge(G_psum, c + 1)
                        dve.wait_ge(beta_done, c + 1)
                        if c >= 2:
                            dve.wait_ge(L_kept[c % 2], 16)
                        for h in range(H0):
                            m = stt(v4(L, 2, H0)[:, c % 2, h], v3(place("G", c)[:], H0)[:, h], beta[:, c * H0 + h:c * H0 + h + 1],
                                    C("strict"), ALU.mult, ALU.mult)
                        m.then_inc(L_done, 1)

                    def seq_b(c):
                        dve.wait_ge(B_psum, c + 1)
                        if c:
                            dve.wait_ge(O_psum, c)
                        tt(v3(Bm, H0), v3(place("B", c)[:], H0), repeat(C("upper"), H0), ALU.mult).then_inc(Bm_done, 1)

                    def solve():
                        dve.wait_ge(Lb_loaded, 16)
                        l, x = v3(Lb, BLK), v3(Xb, BLK)
                        link(nc.vector.memset(Xb, 0.0))
                        link(nc.vector.memset(Xb[:, 0:BLK * BLK:BLK + 1], 1.0))
                        for i in range(1, BLK):
                            t = v3(prod[:, 0:i * i], i)
                            link(tt(t, repeat(l[:, i, 0:i], i), x[:, 0:i, 0:i].rearrange("p j n -> p n j"), ALU.mult))
                            m = nc.vector.tensor_reduce(x[:, i, 0:i], t, AX, ALU.add, negate=True)
                            link(m) if i < BLK - 1 else m.then_inc(Xb_done, 1)

                    def inv_v(k, c):
                        n = at_level(k, c, LEVELS)
                        dve.wait_ge(V_psum, n + 1)
                        Vc, Zc = v4(Vm, 2, H0)[:, c % 2], v4(Z, NT, H0)[:, c]
                        if k:
                            mask = repeat(B("lowT")[:, (k - 1) * P:k * P], H0)
                            tt(Vc, v3(place("V", k, c)[:], H0), mask, ALU.mult).then_inc(Vm_done, 1)
                        else:
                            nc.vector.tensor_copy(Zc, v3(place("V", k, c)[:], H0)).then_inc(Z_done, 1)

                    def inv_zx(k, c):
                        Zc, Xc = v4(Z, NT, H0)[:, c], v4(X, 2, H0)[:, c % 2]
                        dve.wait_ge(ZV_psum, at_level(k, c, LEVELS - 1, 1) + 1)
                        dve.wait_ge(Z_done, at_level(k - 1, c, LEVELS) + 1)
                        tt(Zc, Zc, v3(place("ZV", k, c)[:], H0), ALU.add).then_inc(Z_done, 1)
                        if k < LEVELS - 1:
                            dve.wait_ge(VX_psum, at_level(k, c, LEVELS - 2, 1) + 1)
                            if k > 1:
                                dve.wait_ge(X_done, at_level(k - 1, c, LEVELS - 2, 1) + 1)
                            tt(Xc, Xc, v3(place("VX", k, c)[:], H0), ALU.add).then_inc(X_done, 1)

                    def seq_p(c):
                        dve.wait_ge(P_psum, c + 1)
                        if c:
                            dve.wait_ge(U_psum, c)
                        tt(v3(R_sb[:], H0), v3(place("P", c)[:, 0:P], H0), spread(beta[:, c * H0:(c + 1) * H0], DV), ALU.mult)\
                            .then_inc(R_done, 1)

                    def seq_o(c):
                        if c < NT - 1:
                            dve.wait_ge(dS_psum, c + 1)
                            ps = place("dS", c)[:, 0:P]
                            if c:
                                dve.wait_ge(S_done, c)
                                tt(Sn[:], Sn[:], ps, ALU.subtract).then_inc(S_done, 1)
                            else:
                                ts(Sn[:], ps, -1.0, None, ALU.mult).then_inc(S_done, 1)

                    def delta_norm():
                        dve.wait_ge(osq_done, 1)
                        link(nc.vector.tensor_reduce(oss[:], v3(kn[:, 0:T], NT * H0), AX, ALU.add))
                        link(ts(oss[:], oss[:], 1.0 / (DK * DV), EPS, ALU.mult, ALU.add))
                        rsqrt(ors[:], oss[:], NT * H0, ors_done)

                    def fqkv(l, c):
                        n = l * NT + c
                        for i, (full_bank, full, turned, dst, tc, tsn) in enumerate((
                                (place("fq", l, c), fq_psum, fqT_psum, q_f, "qc", "qs"), (place("fk", l, c), fk_psum, fkT_psum, k_f, "kc", "ks"))):
                            m = 2 * n + i
                            at = c * DF
                            dve.wait_ge(fsq_done, m + 1)
                            nc.vector.tensor_reduce(qk_ss[:, c % 2 * 16 + 8 * i:c % 2 * 16 + 8 * i + 8], v3(rot[m % 2][:], HF), AX, ALU.add)\
                                .then_inc(fss_done, 1)
                            dve.wait_ge(full, n + 1)
                            if n >= 2:
                                dve.wait_ge(turned, n - 1)
                            ps = v3(full_bank[:], HF)
                            tt(v3(dst[:, c % 2 * T:(c % 2 + 1) * T], HF), ps, repeat(tab[tc][l][:, at:at + DF], HF), ALU.mult).then_inc(ft1_done, 1)
                            dve.wait_ge(fss_done, m + 1)
                            r = v3(rot[m % 2][:], HF)
                            hd = DF // 2
                            tt(r[:, :, 0:hd], ps[:, :, hd:DF], repeat(tab[tsn][l][:, at:at + hd], HF), ALU.mult)
                            tt(r[:, :, hd:DF], ps[:, :, 0:hd], repeat(tab[tsn][l][:, at + hd:at + DF], HF), ALU.mult).then_inc(frot_done, 1)

                    def frs(l, c):
                        n = l * NT + c
                        if n >= 2:
                            dve.wait_ge(fn_done, 2 * (n - 1))
                        dve.wait_ge(fss_done, 2 * n + 2)
                        v = qk_ss[:, c % 2 * 16:c % 2 * 16 + 16]
                        link(ts(v, v, 1e-24, None, ALU.max))
                        rsqrt(qk_rs[:, c % 2 * 16:c % 2 * 16 + 16], v, 16, frs_done)

                    def fT(l, c):
                        n = l * NT + c
                        dve.wait_ge(fqT_psum, n + 1)
                        if n >= 2:
                            dve.wait_ge(fS_psum, (n - 1) * NPAIR)
                        half = slice(DF, P)
                        nc.vector.tensor_copy(v4(qTz[:], 2, HF)[half, c % 2, 1:HF:2], v3(place("fqT", l, c)[:], NPAIR)[half])\
                            .then_inc(fqT_hi, 1)

                    def fS(l, i):
                        c, g = divmod(i, NPAIR)
                        n = pair(l, i)
                        lo = 128 if c == 0 else 64
                        dve.wait_ge(fS_psum, n + 1)
                        if l:
                            dve.wait_ge(fexp_done, 2 * NT * NPAIR)
                        nc.vector.tensor_reduce(nmax[:, c * HF + 2 * g:c * HF + 2 * g + 2], v3(place("fS", l, i)[:], 2)[:, :, lo:256],
                                                AX, ALU.max, negate=True).then_inc(fmax_done, 1)

                    def fnorm(l, i):
                        n = pair(l, i)
                        at = 2 * i
                        dve.wait_ge(fexp_done, 2 * n + 2)
                        nc.vector.reciprocal(prec[:, at:at + 2], psums[:, at:at + 2]).then_inc(fprec_done, 1)

                    def fres(l):
                        dve.wait_ge(fwo_psum, NT * (l + 1))
                        old = xnT if l == 0 else r2T
                        if l:
                            dve.wait_ge(r_done, 1)
                        tt(r1T[:], place("fwo", l)[:], old[:], ALU.add).then_inc(r1_done, 1)
                        dve.wait_ge(r1_done, l + 1)
                        if l:
                            dve.wait_ge(h2tm_psum, l)
                        shifted(h2T, r1T).then_inc(h2_done, 1)

                    def fln(l):
                        dve.wait_ge(h2tm_psum, l + 1)
                        if l:
                            dve.wait_ge(normT_psum, 1)
                        layernorm(v3(norm_tm[:], NT), v3(place("h2tm", l)[:], NT), D, norm_done)

                    def hnT_(l):
                        dve.wait_ge(normT_psum, l + 1)
                        if l:
                            dve.wait_ge(fa_psum, 3)
                        cols = W(f"cols{l}")
                        dve.wait_ge(late_loads, 32)
                        ts(hnT[:], place("normT", l)[:], cols[:, 7:8], cols[:, 8:9], ALU.mult, ALU.add).then_inc(hn_done, 1)

                    def fw1(l, j):
                        _, m = HID_TILES[j]
                        n = 3 * l + j
                        if n == 0:
                            dve.wait_ge(X_zeroed, 16 * NT)
                        dve.wait_ge(gelu_done, n + 1)
                        dve.wait_ge(fa_psum, n + 1)
                        if l:
                            dve.wait_ge(fw2_psum, 1)
                        stt(hm[0:m, j * T:(j + 1) * T], place("fa", l, j)[0:m, :], W(f"cols{l}")[0:m, j:j + 1],
                            gl[0:m, (n % 2) * T:(n % 2 + 1) * T], ALU.add, ALU.mult).then_inc(hm_done, 1)

                    def fw2(l):
                        dve.wait_ge(fw2_psum, l + 1)
                        stt(r2T[:], place("fw2", l)[:], W(f"cols{l}")[:, 6:7], r1T[:], ALU.add, ALU.add).then_inc(r_done, 1)
                        if l == 0:
                            dve.wait_ge(r_done, 1)
                            shifted(hT, r2T).then_inc(h_done, 1)

                    def x1():
                        dve.wait_ge(x1_psum, 1)
                        dve.wait_ge(normT_psum, 2)
                        tt(x1_tm[:], place("x1")[:], x_tm[:], ALU.add).then_inc(x1_done, 1)
                        dve.wait_ge(x1_done, 1)
                        layernorm(v3(norm_tm[:], NT), v3(x1_tm[:], NT), D, norm_done)

                    def lat():
                        dve.wait_ge(lat_psum, 1)
                        layernorm(v3(lat_tm[:], NT), v3(place("lat")[:, 0:NT * LAT], NT), LAT, lat_done)

                    def latT_():
                        dve.wait_ge(latT_psum, 1)
                        cols = W("latcols")
                        ts(latT[0:LAT, :], place("latT")[0:LAT, :], cols[0:LAT, 0:1], cols[0:LAT, 1:2], ALU.mult, ALU.add)\
                            .then_inc(latT_done, 1)

                    def rope(i, scale):
                        f = qkf[:, i * T:(i + 1) * T]
                        dve.wait_ge(mq_psum, 2 * i + 1)
                        stt(rc[:], place("mq", 2 * i)[:], scale, C("rcos"), ALU.mult, ALU.mult).then_inc(rope_done, 1)
                        dve.wait_ge(mq_psum, 2 * i + 2)
                        stt(rsn[:], place("mq", 2 * i + 1)[:], scale, C("rsin"), ALU.mult, ALU.mult).then_inc(rope_done, 1)
                        dve.wait_ge(rope_done, 2 * i + 2)
                        tt(f, rc[:], rsn[:], ALU.add).then_inc(qkf_done, 1)
                        p = [parts[:, (3 * i + n) * T:(3 * i + n + 1) * T] for n in range(3)]
                        r = res[:, i * T:(i + 1) * T]
                        dve.wait_ge(split_done, 2 * i + 1)
                        tt(r, f, p[0], ALU.subtract).then_inc(split2_done, 1)
                        dve.wait_ge(split_done, 2 * i + 2)
                        tt(p[2], r, p[1], ALU.subtract).then_inc(split2_done, 1)

                    def mS(h):
                        for t, c, at in ((0, 0, 0), (0, 2, P), (1, 1, 0), (2, 3, 0)):
                            dve.wait_ge(mS_psum, 3 * h + t + 1)
                            nc.vector.tensor_reduce(nmx[:, h * NT + c:h * NT + c + 1], place("mS", h, t)[:, at:at + (c + 1) * P],
                                                    AX, ALU.max, negate=True).then_inc(nmx_done, 1)

                    def mrow(g):
                        dve.wait_ge(mrow_psum, g + 1)
                        if g:
                            dve.wait_ge(mrow_sent, 48 * g)
                        p = [mparts[0:NROW, n * P:(n + 1) * P] for n in range(3)]
                        ps, left = place("mrow", g)[0:NROW, 0:P], mres[0:NROW, :]
                        link(nc.vector.tensor_copy(p[0], ps))
                        link(tt(left, ps, p[0], ALU.subtract))
                        link(nc.vector.tensor_copy(p[1], left))
                        tt(p[2], left, p[1], ALU.subtract).then_inc(mrow_done, 1)

                    def next_norm():
                        dve.wait_ge(x_loaded, 16)
                        dve.wait_ge(normT_psum, 3)
                        head_norm()

                    def next_copy():
                        dve.wait_ge(ew_psum, NE + 1)
                        head_copy()

                    def matg(g):
                        dve.wait_ge(matg_psum, g + 1)
                        ps = v3(place("matg", g)[:], NT * GROUP)
                        r = at_rec[:, 0:NT * GROUP]
                        link(nc.vector.reciprocal(r, ps[:, :, DM]))
                        o = v3(at_tm[:], NT)[:, :, g * GROUP * DM:(g + 1) * GROUP * DM].rearrange("p c (h d) -> p c h d", h=GROUP)
                        for c in range(NT):
                            m = tt(o[:, c], ps[:, c * GROUP:(c + 1) * GROUP, 0:DM], spread(r[:, c * GROUP:(c + 1) * GROUP], DM), ALU.mult)
                        m.then_inc(at_done, 1)

                    def gate():
                        dve.wait_ge(gate_psum, 1)
                        tt(v3(gz[:], NT), v3(place("gate")[:, 0:NT * NE], NT), repeat(R("gate_b"), NT), ALU.add).then_inc(gz_done, 1)
                        dve.wait_ge(gexp_done, 1)
                        link(ts(gw_[:], gp[:], 1.0, None, ALU.add))
                        link(nc.vector.reciprocal(gp[:], gw_[:]))
                        for c in range(NT):
                            p = gp[:, c * NE:(c + 1) * NE]
                            other, own = repeat(p, NE), spread(p, NE)
                            tt(v3(gcmp[:, c * 36:(c + 1) * 36], NE), other, own, ALU.is_gt)
                            m = tt(v3(geq[:, c * 36:(c + 1) * 36], NE), other, own, ALU.is_equal)
                        link(m)
                        link(tt(v3(geq[:], NT), v3(geq[:], NT), repeat(C("tri"), NT), ALU.mult))
                        link(tt(gcmp[:], gcmp[:], geq[:], ALU.add))
                        link(nc.vector.tensor_reduce(grank[:], v3(gcmp[:], NT * NE), AX, ALU.add))
                        link(stt(gw_[:], grank[:], 1.5, gp[:], ALU.is_lt, ALU.mult))
                        link(nc.vector.tensor_reduce(gsum[:, 0:NT], v3(gw_[:], NT), AX, ALU.add))
                        link(ts(gsum[:, 0:NT], gsum[:, 0:NT], 1e-8, None, ALU.add))
                        link(nc.vector.reciprocal(gsum[:, NT:2 * NT], gsum[:, 0:NT]))
                        tt(v3(ge[:], NT), v3(gw_[:], NT), spread(gsum[:, NT:2 * NT], NE), ALU.mult).then_inc(ge_done, 1)

                    def e_up(e):
                        slot = slice((e % 2) * T, (e % 2 + 1) * T)
                        dve.wait_ge(eth_done, e + 1)
                        stt(se[:, slot], the[:, slot], 1.0, place("eu", e)[:], ALU.add, ALU.mult).then_inc(es_done, 1)
                        dve.wait_ge(es_done, e + 1)
                        dve.wait_ge(ew_psum, e + 1)
                        if e >= 2:
                            dve.wait_ge(ey_psum, e - 1)
                        stt(he[:, slot], se[:, slot], 0.5, place("ew", e)[:], ALU.mult, ALU.mult).then_inc(eh_done, 1)

                    def e_down(e):
                        dve.wait_ge(ey_psum, e + 1)
                        dve.wait_ge(ge_done, 1)
                        if e:
                            dve.wait_ge(ey_done, e)
                        for c in range(NT):
                            s = ge[:, c * NE + e:c * NE + e + 1]
                            o, y = acc[:, c * P:(c + 1) * P], place("ey", e)[:, c * P:(c + 1) * P]
                            m = stt(o, y, s, o, ALU.mult, ALU.add) if e else ts(o, y, s, None, ALU.mult)
                        m.then_inc(ey_done, 1)

                    def final():
                        dve.wait_ge(ey_done, NE)
                        link(tt(acc[:], acc[:], x1_tm[:], ALU.add))
                        dve.wait_ge(fin_psum, 1)
                        tt(fin[:], place("fin")[:], acc[:], ALU.add).then_inc(fin_done, 1)

                    walk({"k": k, "krs": krs_, "bg": bg, "gram": gram, "solve": solve, "inv_v": inv_v,
                          "inv_zx": inv_zx, "seq_b": seq_b, "seq_p": seq_p, "seq_o": seq_o, "delta_norm": delta_norm, "fqkv": fqkv, "frs": frs, "fT": fT, "fS": fS,
                          "fnorm": fnorm, "fres": fres, "fln": fln, "hnT": hnT_, "fw1": fw1, "fw2": fw2, "x1": x1, "lat": lat,
                          "latT": latT_, "mq": lambda: rope(0, DM ** -0.5), "mk": lambda: rope(1, 1.0),
                          "mS": mS, "mrow": mrow, "head_norm": next_norm, "head_T": next_copy, "matg": matg,
                          "gate": gate, "e_up": e_up, "e_down": e_down, "final": final})

                @block.gpsimd
                def _(pool):
                    tt = nc.gpsimd.tensor_tensor


                    def kT_(c):
                        pool.wait_ge(krs_done, 1)
                        pool.wait_ge(k_copied, c + 1)
                        tt(v4(kn[:], NT, H0)[:, c], v4(kn[:], NT, H0)[:, c], spread(krs[:, c * H0:(c + 1) * H0], DK), ALU.mult)\
                            .then_inc(kn_done, 1)

                    def delta_norm():
                        pool.wait_ge(ors_done, 1)
                        pool.wait_ge(o_copied, NT)
                        o = v3(o_all[:], NT * H0)
                        pool.wait_ge(osq_done, 1)
                        tt(o, o, spread(ors[:], DV), ALU.mult).then_inc(on_done, 1)
                        pool.wait_ge(on_done, 1)
                        tt(v3(o_all[:], NT), v3(o_all[:], NT), repeat(norm_w[:], NT), ALU.mult).then_inc(on_done, 1)
                        pool.wait_ge(on_done, 2)
                        pool.wait_ge(gs_done, NT)
                        tt(o_all[:], o_all[:], gs[:], ALU.mult).then_inc(og_done, 1)

                    def fqkv(l, c):
                        for i, dst in enumerate((q_f, k_f)):
                            m = 2 * (l * NT + c) + i
                            pool.wait_ge(ft1_done, m + 1)
                            pool.wait_ge(frot_done, m + 1)
                            d = dst[:, c % 2 * T:(c % 2 + 1) * T]
                            tt(d, d, rot[m % 2][:], ALU.add).then_inc(fsum_done, 1)

                    def fT(l, c):
                        pool.wait_ge(frs_done, l * NT + c + 1)
                        for i, dst in enumerate((q_f, k_f)):
                            m = 2 * (l * NT + c) + i
                            pool.wait_ge(fsum_done, m + 1)
                            d = v3(dst[:, c % 2 * T:(c % 2 + 1) * T], HF)
                            tt(d, d, spread(qk_rs[:, c % 2 * 16 + 8 * i:c % 2 * 16 + 8 * i + 8], DF), ALU.mult).then_inc(fn_done, 1)

                    def fnorm(l, i):
                        lo = 128 if i < NPAIR else 64
                        p = v4(p_sb[:], 2, 2)[:, i % 2, :, lo:256]
                        pool.wait_ge(fprec_done, pair(l, i) + 1)
                        tt(p, p, spread(prec[:, 2 * i:2 * i + 2], 256 - lo), ALU.mult).then_inc(fnorm_done, 1)

                    def x1():
                        pool.wait_ge(x1_psum, 1)
                        nc.gpsimd.memset(vaug, 0.0).then_inc(vaug_zeroed, 1)
                        pool.wait_ge(vaug_zeroed, 1)
                        nc.gpsimd.memset(v3(vaug, NT * HM)[:, :, DM:DM + 1], 1.0).then_inc(vaug_zeroed, 1)

                    walk({"kT": kT_, "delta_norm": delta_norm, "fqkv": fqkv, "fT": fT, "fnorm": fnorm, "x1": x1})

                @block.sync
                def _(sp):

                    def gram(c):
                        sp.wait_ge(L_done, c + 1)
                        sp.dma_start(in_dram(L_dram, c), v4(L, 2, H0)[:, c % 2]).then_inc(L_kept[c % 2], 16)

                    def solve():
                        sp.wait_ge(L_kept[0], 32)
                        sp.wait_ge(L_kept[1], 32)
                        sp.dma_start(v3(Lb, BLK), diagonal(L_dram)).then_inc(Lb_loaded, 16)
                        sp.wait_ge(Xb_done, 1)
                        sp.wait_ge(X_zeroed, 16 * NT)
                        sp.dma_start(diagonal(X_dram), v3(Xb, BLK)).then_inc(Xb_kept, 16)

                    def inv_load(c):
                        sp.wait_ge(Xb_kept, 16)
                        if c >= 2:
                            sp.wait_ge(ZV_psum, at_level(LEVELS - 1, c - 2, LEVELS - 1, 1) + 1)
                        sp.dma_start(v4(X, 2, H0)[:, c % 2], in_dram(X_dram, c)).then_inc(X_loaded[c % 2], 16)
                        sp.dma_start(v4(L, 2, H0)[:, c % 2], in_dram(L_dram, c)).then_inc(L_loaded[c % 2], 16)

                    def x1():
                        sp.wait_ge(x1_done, 1)
                        sp.dma_start(v3(x_tm[:], NT), x[bass.ds(b + 1, 1)].rearrange("a (t p) d -> p (a t) d", p=P)).then_inc(x_loaded, 16)
                        for i, dst in enumerate((Qst32, Kst32)):
                            sp.dma_start(dst[9 * DM:P, :], row_fill[i]).then_inc(rows_filled, 16)

                    def send(i):
                        for n in range(3):
                            sp.wait_ge(split_done, 2 * i + 1 + (n > 0))
                            sp.wait_ge(split2_done, 2 * i + 1 + (n > 1))
                            to = parts_dram[i, n * DM:(n + 1) * DM].rearrange("d (h t) -> h d t", h=HM)
                            sp.dma_start(to, parts[:, (3 * i + n) * T:(3 * i + n + 1) * T]).then_inc(parts_kept, 16)
                        sp.wait_ge(parts_kept, 48 * (i + 1))
                        rows = 3 * DM
                        for s in range(3):
                            if i == 1:
                                sp.dma_start(Kst[s * rows:(s + 1) * rows, :], parts_dram[1]).then_inc(parts_sent, 16)
                            else:
                                for n in range(3):
                                    at = (3 * n + s) * DM
                                    sp.dma_start(Qst[at:at + DM, :], parts_dram[0, n * DM:(n + 1) * DM]).then_inc(parts_sent, 16)

                    def mrow(g):
                        sp.wait_ge(mrow_done, g + 1)
                        for i in range(3):
                            dst = Qst[9 * DM + i:9 * DM + i + 1, g * GROUP * T:(g + 1) * GROUP * T].rearrange("a (r t) -> a r t", t=P)
                            sp.dma_start(dst, mparts[0:NROW, i * P:(i + 1) * P]).then_inc(mrow_sent, 16)

                    def final():
                        sp.wait_ge(fin_done, 1)
                        sp.dma_start(out[bass.ds(b, 1)].rearrange("a (t p) d -> p (a t) d", p=P), v3(fin[:], NT)).then_inc(out_stored, 16)
                        sp.wait_ge(out_stored, 16)
                        sp.wait_ge(x_loaded, 16)

                    walk({"gram": gram, "solve": solve, "inv_load": inv_load, "x1": x1, "mq": lambda: send(0), "mk": lambda: send(1), "mrow": mrow, "final": final})

            nc.sync.sem_clear(range(numbers[0], numbers[-1] + 1))
            nc.all_engine_barrier()



def pack(inp):
    f = np.float32
    a = {k: np.asarray(v) for k, v in inp.items()}

    def rows128(m):
        out = np.zeros((P, m.shape[1]), f)
        out[:m.shape[0]] = m
        return out

    def tiles(m):
        n = -(-m.shape[0] // P)
        return np.concatenate([rows128(m[j * P:(j + 1) * P]) for j in range(n)], 1)

    w = {"wk": a["L0_attn_Wk"], "wq": a["L0_attn_Wq"], "wv": a["L0_attn_Wv"],
         "wbg": np.concatenate([a["L0_attn_Wb"], a["L0_attn_Wg"]], 1), "wo0": a["L0_attn_Wo"]}
    for l in range(DEPTH):
        w[f"wqkv{l}"] = a["L0_ffn_wqkv"][l]
        w[f"wof{l}"] = tiles(a["L0_ffn_wo"][l])
        w[f"w1{l}"] = a["L0_ffn_w1"][l]
        w[f"w2{l}"] = tiles(a["L0_ffn_w2"][l])
        b1 = a["L0_ffn_b1"][l]
        w[f"cols{l}"] = np.concatenate([tiles(b1[:HID, None]), tiles(b1[HID:, None]), a["L0_ffn_b2"][l][:, None],
                                        a["L0_ffn_ln_g"][l][:, None], a["L0_ffn_ln_b"][l][:, None]], 1)
    turned = np.arange(D).reshape(HM, 2, DM // 2)[:, ::-1].reshape(-1)
    w["Wq"], w["Wqr"] = a["L1_attn_W_q"], a["L1_attn_W_q"][:, turned]
    w["Wdkv"] = a["L1_attn_W_dkv"]
    w["Wuk"], w["Wukr"], w["Wuv"] = rows128(a["L1_attn_W_uk"]), rows128(a["L1_attn_W_uk"][:, turned]), rows128(a["L1_attn_W_uv"])
    w["Wo"] = a["L1_attn_W_o"]
    w["latcols"] = rows128(np.stack([a["L1_attn_ln_gamma"], a["L1_attn_ln_beta"]], 1))
    w["gate"] = a["L1_ffn_gate_w"].T
    for e in range(NE):
        w[f"eu{e}"], w[f"ew{e}"], w[f"ed{e}"] = a["L1_ffn_ew1"][e].T, a["L1_ffn_ew3"][e].T, a["L1_ffn_ew2"][e].T
    w[f"eu{NE}"], w[f"ew{NE}"], w[f"ed{NE}"] = a["L1_ffn_fc1"].T, a["L1_ffn_fc2"].T, a["L1_ffn_fc3"].T
    packed = np.ascontiguousarray(np.concatenate([w[n] for n, _ in weight_layout()], 1))
    rows = np.concatenate([a["L0_attn_norm_w"], a["L0_ffn_q_scale"].reshape(-1), a["L0_ffn_k_scale"].reshape(-1),
                           a["L1_ffn_gate_b"]])[None]
    return packed, np.ascontiguousarray(rows)


def kernel(**inputs):
    import concourse.bacc as bacc
    from concourse.bass_utils import run_bass_kernel_spmd

    packed, rows = pack(inputs)
    consts, consts_bf = constants()
    row_fill = np.zeros((2, P - 9 * DM, HM * T // 2), np.uint32)
    row_fill[1, 0:3] = 0x3F803F80
    row_fill = row_fill.view(np.float32)
    padded = np.concatenate([inputs["L0_attn_x"], np.zeros((1, T, D), np.float32)])
    arrays = {"x": padded, "weights": packed, "rows": rows, "consts": consts,
              "consts_bf": consts_bf, "row_fill": row_fill}
    nc = bacc.Bacc("TRN2", target_bir_lowering=False, num_devices=1)
    args = [nc.dram_tensor(n, a.shape, mybir.dt.from_np(a.dtype), kind="ExternalInput").ap() for n, a in arrays.items()]
    out = nc.dram_tensor("out", (BATCH, T, D), F32, kind="ExternalOutput").ap()
    parts_dram = nc.dram_tensor("parts_dram", (2, 3 * DM, HM * T), BF16, kind="Internal").ap()
    L_dram, X_dram = (nc.dram_tensor(n, (NT * H0 * HEAD_ROOM,), F32, kind="Internal").ap() for n in ("L_dram", "X_dram"))
    build(nc, *args, parts_dram, L_dram, X_dram, out)
    r = run_bass_kernel_spmd(nc, [arrays], core_ids=[0])
    return r.results[0]["out"]
```

```python
from contextlib import ExitStack

import numpy as np

import concourse.bass as bass
from concourse import mybir

ALU = mybir.AluOpType
ACT = mybir.ActivationFunctionType
AX = mybir.AxisListType.X
F32 = mybir.dt.float32
BF16 = mybir.dt.bfloat16
I32 = mybir.dt.int32

P = 128
BATCH, T, D = 8, 512, 128
NT = T // P
H0, DK, DV = 4, 128, 32
DEPTH, HF, DF, WIN = 2, 8, 64, 64
HID = D * 4 * 2 // 3
HM, DM, LAT = 16, 8, 32
NE = 6
BLK = 16
NBLK = NT * H0 * P // BLK
LEVELS = 4
HEAD_ROOM = P * P + P
BLOCK_STEP = (P + 1) * BLK
NEG = -1e30
EPS = 1e-5
NPAIR = HF // 2
VW = 32
GROUP = 4
NROW = NT * GROUP
LEAD = 7
P_SLOTS = 3
PT_SLOTS = 6
DELTA_AFTER = "000000020000000000000000200000000000001100001000100000000000000000000000001000300010000100010000000200000113010000000000000022000010000100000000000020001000010200000000110000001000110010010020120000300031010150102010420001"
EXPERTS_AFTER = "00012000000000000000000000000001000000010000000010000000010000001100100000101010000100000100000001000100100100011000"
HID_TILES = [(j * P, min(P, HID - j * P)) for j in range((HID + P - 1) // P)]



def weight_layout():
    w = [("wk", H0 * DK), ("wq", H0 * DK), ("wv", H0 * DV), ("wbg", H0 + H0 * DV), ("wqkv0", 3 * HF * DF), ("wo0", D)]
    for l in range(DEPTH):
        w += [("wqkv1", 3 * HF * DF)] if l else []
        w += [(f"wof{l}", 4 * D), (f"w1{l}", 2 * HID), (f"w2{l}", 3 * D), (f"cols{l}", 9)]
    w += [("Wq", D), ("Wqr", D), ("Wdkv", LAT), ("Wuk", D), ("Wukr", D), ("Wuv", D), ("Wo", D), ("latcols", 2)]
    w += [("gate", NE)]
    w += [(f"e{n}{i}", D) for i in range(NE + 1) for n in ("u", "w", "d")]
    return w


CONST_LAYOUT = [("ident", P), ("strict", P), ("upper", P),
                ("qcos", NT * DF), ("qsin", NT * DF), ("kcos", NT * DF), ("ksin", NT * DF),
                ("tri", NE * NE), ("rcos", T), ("rsin", T)]
BF_LAYOUT = [("identb", P), ("band", 192), ("causal", P), ("causalT", P),
             ("lowT", (LEVELS - 1) * P)]


def offsets(layout):
    at, out = 0, {}
    for name, n in layout:
        out[name] = (at, n)
        at += n
    return out, at


def constants():
    f = np.float32
    i, j = np.arange(P)[:, None], np.arange(P)[None, :]
    c = {"ident": np.eye(P, dtype=f), "strict": (j < i).astype(f), "upper": -(i <= j).astype(f)}
    low = [-((i >> (k + 1) == j >> (k + 1)) & ((i >> k) & 1 == 1) & ((j >> k) & 1 == 0)).astype(f) for k in range(4, 7)]
    half = np.arange(0, DF, 2, dtype=f)
    inv = (f(1) / f(10000) ** (half / f(DF))).astype(f)
    t = np.arange(T, dtype=f)
    ang = np.concatenate([t[:, None] * inv[None]] * 2, 1)
    base = ((half + f(0.4 * DF)) / f(1.4 * DF)).astype(f)
    scale = np.concatenate([base[None] ** ((t - T // 2) / f(WIN // 2))[:, None]] * 2, 1).astype(f)
    sign = np.where(np.arange(DF) < DF // 2, f(-1), f(1))[None]
    cos, sin = np.cos(ang), np.sin(ang) * sign
    tiles = lambda a: a.astype(f).reshape(NT, P, DF).transpose(1, 0, 2).reshape(P, NT * DF)
    c["qcos"], c["qsin"] = tiles(8 * cos * scale), tiles(8 * sin * scale)
    c["kcos"], c["ksin"] = tiles(cos / scale), tiles(sin / scale)
    hd = DM // 2
    inv = (f(1) / f(10000) ** (np.arange(hd, dtype=f) / f(hd))).astype(f)
    d = np.arange(D) % DM
    ang = inv[d % hd][:, None] * t[None]
    c["rcos"] = np.cos(ang).astype(f)
    c["rsin"] = (np.sin(ang) * np.where(d < hd, -1, 1)[:, None]).astype(f)
    e = np.arange(NE)
    c["tri"] = np.broadcast_to((e[None] < e[:, None]).astype(f).reshape(1, -1), (P, NE * NE))
    packed = np.concatenate([c[n].astype(f) for n, _ in CONST_LAYOUT], 1)
    key = np.arange(192)[None] - 64
    b = {"identb": np.eye(P), "band": np.where((key <= i) & (key >= i - WIN), 0, NEG),
         "causal": np.where(j <= i, 0, NEG), "causalT": np.where(i <= j, 0, NEG),
         "lowT": np.concatenate([m.T for m in low], 1)}
    return np.ascontiguousarray(packed), np.concatenate([b[n].astype(f) for n, _ in BF_LAYOUT], 1)


def build(nc, x, weights, rows, consts, consts_bf, row_fill, parts_dram, L_dram, X_dram, out):
    W_AT, W_N = offsets(weight_layout())
    C_AT, C_N = offsets(CONST_LAYOUT)
    B_AT, B_N = offsets(BF_LAYOUT)
    R_AT, R_N = offsets([("norm_w", DV), ("qs", DEPTH * DF), ("ks", DEPTH * DF), ("gate_b", NE)])

    with ExitStack() as ctx:
        def sb(name, n, dt=F32):
            return ctx.enter_context(nc.sbuf_tensor(name, [P, n], dt))

        w_sb, c_sb, b_sb, r_sb = sb("w_sb", W_N), sb("c_sb", C_N), sb("b_sb", B_N, BF16), sb("r_sb", R_N)

        def W(name):
            a, n = W_AT[name]
            return w_sb[:, a:a + n]

        def C(name):
            a, n = C_AT[name]
            return c_sb[:, a:a + n]

        def B(name):
            a, n = B_AT[name]
            return b_sb[:, a:a + n]

        def R(name):
            a, n = R_AT[name]
            return r_sb[:, a:a + n]

        def v3(ap, a):
            return ap.rearrange("p (a b) -> p a b", a=a)

        def v4(ap, a, b):
            return ap.rearrange("p (a b c) -> p a b c", a=a, b=b)

        def spread(ap, n):
            return ap[:, :, None].to_broadcast([ap.shape[0], ap.shape[1], n])

        def repeat(ap, n):
            return ap[:, None, :].to_broadcast([ap.shape[0], n, ap.shape[1]])

        tab = {n: [sb(f"tab_{n}", NT * DF)[:, :], C(c)] for n, c in (("qc", "qcos"), ("qs", "qsin"), ("kc", "kcos"), ("ks", "ksin"))}
        norm_w = sb("norm_w_neg", H0 * DV)

        x_tm, norm_tm, xnT, r1T, r2T = sb("x_tm", T), sb("norm_tm", T), sb("xnT", T), sb("r1T", T), sb("r2T", T)
        hT, h2T = sb("hT", T), sb("h2T", T)
        qTz = sb("qTz", 2 * HF * P)
        p_sb, o_sb, gl, hm = sb("p_sb", P_SLOTS * T), sb("o_sb", 2 * T), sb("gl", 2 * T), sb("hm", 3 * T)
        oT0, latT = sb("oT0", T), sb("latT", T)
        NBG = H0 + H0 * DV
        stats, mv = sb("stats", NT * 6), sb("mv", NT * 2)
        rs_in, rs_tmp, rs_out = sb("rs_in", 2 * NT), sb("rs_tmp", 16), sb("rs_out", 16)
        warm = sb("warm", 2)
        kss, krs, beta = sb("kss", NT * H0), sb("krs", NT * H0), sb("beta", NT * H0)
        oss, ors = sb("oss", NT * H0), sb("ors", NT * H0)
        qk_ss, qk_rs = sb("qk_ss", 2 * 16), sb("qk_rs", 2 * 16)
        R_sb, U_sb, Sn = sb("R_sb", P), sb("U_sb", P), sb("Sn", H0 * DV)
        nmax, psums, prec = sb("nmax", NT * HF), sb("psums", NT * HF), sb("prec", NT * HF)
        nmx, mparts, mres = sb("nmx", NT * HM), sb("mparts", 3 * P, BF16), sb("mres", P)
        at_rec, gz, gp, gw_, ge = sb("at_rec", NT * GROUP), sb("gz", 24), sb("gp", 24), sb("gw_", 24), sb("ge", 24)
        gcmp, geq, grank, gsum = sb("gcmp", NT * 36), sb("geq", NT * 36), sb("grank", 24), sb("gsum", 2 * NT)
        PTW = NT * (NT + 1) // 2 * P
        layer0 = [("kn", NT * T), ("kT", NT * T), ("qT", NT * T), ("oTf", 2 * T), ("q_f", 2 * T), ("k_f", 2 * T), ("v_f", NT * T),
                  ("kTf", NPAIR * T), ("pT", 2 * T), ("rot", 2 * T), ("gs", T), ("th", NT * NBG), ("o_all", T), ("hnT", T),
                  ("Z", NT * T), ("Bm", T), ("L", 2 * T), ("X", 2 * T), ("Vm", 2 * T),
                  ("blk", 3 * BLK * BLK)]
        layer1 = [("Qst", HM * T // 2), ("Kst", HM * T // 2), ("qkf", 2 * T), ("res", 2 * T), ("parts", 3 * T), ("rope", 2 * T),
                  ("lat_tm", NT * LAT), ("he", 2 * T), ("vaug", NT * HM * VW), ("PTm", PT_SLOTS * PTW)]
        at0, n0 = offsets(layer0)
        at1, n1 = offsets(layer1)
        shared = sb("shared", max(n0, n1))
        kn, kT, qT, oTf, q_f, k_f, v_f, kTf, pT, rot, gs, th, o_all, hnT, Z, Bm, L, X, Vm, blk = (
            shared[:, a:a + n] for a, n in at0.values())
        Qst, Kst, qkf, res, parts, rope_sb, lat_tm, he, vaug, PTm = (shared[:, a:a + n] for a, n in at1.values())
        Qst32, Kst32 = Qst, Kst
        Qst, Kst, parts = Qst.bitcast(BF16), Kst.bitcast(BF16), parts.bitcast(BF16)
        rc, rsn, atg = rope_sb[:, 0:T], rope_sb[:, T:2 * T], rope_sb
        PTm = [PTm[:, i * PTW:(i + 1) * PTW] for i in range(PT_SLOTS)]
        rot = [rot[:, 0:T], rot[:, T:2 * T]]
        Lb, Xb, prod = blk[:, 0:BLK * BLK], blk[:, BLK * BLK:2 * BLK * BLK], blk[:, 2 * BLK * BLK:]

        def in_dram(m, c):
            return m.rearrange("(g r) -> g r", r=HEAD_ROOM)[c * H0:(c + 1) * H0, 0:P * P].rearrange("h (p t) -> p h t", p=P)

        def diagonal(m):
            return m.rearrange("(b r) -> b r", r=BLOCK_STEP)[:, 0:BLK * P].rearrange("b (i t) -> b i t", t=P)[:, :, 0:BLK]

        the, se, x1_tm, xn2T, at_tm = o_sb, gl, r1T, xnT, r2T
        aT, acc, fin = hm[:, 0:T], hm[:, T:2 * T], hm[:, 2 * T:3 * T]

        bank = [ctx.enter_context(nc.psum_tensor(f"bank{i}", [P, 512], F32)) for i in range(8)]
        BANKS = {
            "head": lambda: 4, "normT": lambda n: 4, "k": lambda c: c % 3, "bg": lambda c: (NT + c) % 3,
            "kT": lambda c: (2 * NT + c) % 3, "G": lambda c: (3 * NT + c) % 3, "qT": lambda h: (4 * NT + h) % 3,
            "V": lambda k, c: c % 2, "VX": lambda k, c: c % 2, "ZV": lambda k, c: 2,
            "B": lambda c: 0, "P": lambda c: 1, "U": lambda c: 2, "O": lambda c: 1, "dS": lambda c: 2, "o": lambda: 1, "oT0": lambda: 0,
            "fq": lambda l, c: 3, "fk": lambda l, c: 4, "fv": lambda l, c: 5, "fqT": lambda l, c: 7 if c else 6, "fkT": lambda l, c: 7,
            "fS": lambda l, i: 3 + i % 2, "fPT": lambda l, i: 5, "fO": lambda l, c: 6, 
            "fwo": lambda l: 7, "h2tm": lambda l: 3, "fg": lambda l, j: (3, 5, 3)[j], "fa": lambda l, j: (4, 6, 4)[j],
            "fw2": lambda l: 7, "x1": lambda: 3,
            "lat": lambda: 0, "latT": lambda: 1, "mq": lambda i: (3, 4, 2, 3)[i], "mv": lambda: 6,
            "mS": lambda h, t: 3 + t, "mrow": lambda g: 6, "mST": lambda h, t: t, "mPV": lambda g: 6,
            "matg": lambda g: 6, "aT": lambda: 6, "gate": lambda: 7, "eu": lambda e: 7, "ew": lambda e: 7, "ey": lambda e: 7,
            "fin": lambda: 3}

        def place(name, *i):
            return bank[BANKS[name](*i)]

        zeros = hm[:, 0:T]
        X_zeroed = ctx.enter_context(nc.semaphore("X_zeroed"))
        out_stored = ctx.enter_context(nc.semaphore("out_stored"))
        late_loads = ctx.enter_context(nc.semaphore("late_loads"))
        setup_loads = ctx.enter_context(nc.semaphore("setup_loads"))
        zeroed, tables_done = ctx.enter_context(nc.semaphore("zeroed")), ctx.enter_context(nc.semaphore("tables_done"))
        signals = []

        def semaphore(name):
            signals.append(ctx.enter_context(nc.semaphore(name)))
            return signals[-1]

        x_loaded = semaphore("x_loaded")
        head_norm_done = semaphore("head_norm_done")
        head_psum = semaphore("head_psum")
        head_copied = semaphore("head_copied")
        norm_done = semaphore("norm_done")
        normT_psum = semaphore("normT_psum")
        h_done = semaphore("h_done")
        r_done = semaphore("r_done")
        k_psum = semaphore("k_psum")
        k_copied = semaphore("k_copied")
        ksq_done = semaphore("ksq_done")
        kss_done = semaphore("kss_done")
        krs_done = semaphore("krs_done")
        kn_done = semaphore("kn_done")
        kT_psum = semaphore("kT_psum")
        kT_copied = semaphore("kT_copied")
        qT_psum = semaphore("qT_psum")
        qT_copied = semaphore("qT_copied")
        bg_psum = semaphore("bg_psum")
        th_done = semaphore("th_done")
        beta_done = semaphore("beta_done")
        gs_done = semaphore("gs_done")
        G_psum = semaphore("G_psum")
        L_done = semaphore("L_done")
        B_psum = semaphore("B_psum")
        Bm_done = semaphore("Bm_done")
        V_psum = semaphore("V_psum")
        Vm_done = semaphore("Vm_done")
        ZV_psum = semaphore("ZV_psum")
        VX_psum = semaphore("VX_psum")
        L_kept = [semaphore("L_kept_even"), semaphore("L_kept_odd")]
        Lb_loaded = semaphore("Lb_loaded")
        Xb_done = semaphore("Xb_done")
        Xb_kept = semaphore("Xb_kept")
        L_loaded = [semaphore("L_loaded_even"), semaphore("L_loaded_odd")]
        X_loaded = [semaphore("X_loaded_even"), semaphore("X_loaded_odd")]
        Z_done = semaphore("Z_done")
        X_done = semaphore("X_done")
        P_psum = semaphore("P_psum")
        R_done = semaphore("R_done")
        U_psum = semaphore("U_psum")
        U_copied = semaphore("U_copied")
        O_psum = semaphore("O_psum")
        o_copied = semaphore("o_copied")
        dS_psum = semaphore("dS_psum")
        S_done = semaphore("S_done")
        o_psum = semaphore("o_psum")
        o_back = semaphore("o_back")
        osq_done = semaphore("osq_done")
        ors_done = semaphore("ors_done")
        on_done = semaphore("on_done")
        og_done = semaphore("og_done")
        oT0_psum = semaphore("oT0_psum")
        oT0_copied = semaphore("oT0_copied")
        fq_psum = semaphore("fq_psum")
        fk_psum = semaphore("fk_psum")
        fv_psum = semaphore("fv_psum")
        fv_copied = semaphore("fv_copied")
        fsq_done = semaphore("fsq_done")
        fss_done = semaphore("fss_done")
        ft1_done = semaphore("ft1_done")
        frot_done = semaphore("frot_done")
        fsum_done = semaphore("fsum_done")
        frs_done = semaphore("frs_done")
        fn_done = semaphore("fn_done")
        fqT_psum = semaphore("fqT_psum")
        fkT_psum = semaphore("fkT_psum")
        fqT_lo = semaphore("fqT_lo")
        fqT_hi = semaphore("fqT_hi")
        fkT_copied = semaphore("fkT_copied")
        fS_psum = semaphore("fS_psum")
        fmax_done = semaphore("fmax_done")
        fexp_done = semaphore("fexp_done")
        fPT_psum = semaphore("fPT_psum")
        fPT_copied = semaphore("fPT_copied")
        fO_psum = semaphore("fO_psum")
        fnorm_done = semaphore("fnorm_done")
        fprec_done = semaphore("fprec_done")
        foT_copied = semaphore("foT_copied")
        fwo_psum = semaphore("fwo_psum")
        r1_done = semaphore("r1_done")
        h2_done = semaphore("h2_done")
        h2tm_psum = semaphore("h2tm_psum")
        hn_done = semaphore("hn_done")
        fa_psum = semaphore("fa_psum")
        fg_psum = semaphore("fg_psum")
        gelu_done = semaphore("gelu_done")
        hm_done = semaphore("hm_done")
        fw2_psum = semaphore("fw2_psum")
        x1_psum = semaphore("x1_psum")
        x1_done = semaphore("x1_done")
        xn2_copied = semaphore("xn2_copied")
        lat_psum = semaphore("lat_psum")
        lat_done = semaphore("lat_done")
        latT_psum = semaphore("latT_psum")
        latT_done = semaphore("latT_done")
        mq_psum = semaphore("mq_psum")
        rope_done = semaphore("rope_done")
        qkf_done = semaphore("qkf_done")
        split_done = semaphore("split_done")
        split2_done = semaphore("split2_done")
        parts_kept = semaphore("parts_kept")
        parts_sent = semaphore("parts_sent")
        late_keys_sent = semaphore("late_keys_sent")
        rows_filled = semaphore("rows_filled")
        mv_psum = semaphore("mv_psum")
        vaug_done = semaphore("vaug_done")
        vaug_zeroed = semaphore("vaug_zeroed")
        mS_psum = semaphore("mS_psum")
        nmx_done = semaphore("nmx_done")
        mrow_psum = semaphore("mrow_psum")
        mrow_done = semaphore("mrow_done")
        mrow_sent = semaphore("mrow_sent")
        mST_psum = semaphore("mST_psum")
        mexp_done = semaphore("mexp_done")
        mPV_psum = semaphore("mPV_psum")
        atg_done = semaphore("atg_done")
        matg_psum = semaphore("matg_psum")
        at_done = semaphore("at_done")
        aT_psum = semaphore("aT_psum")
        aT_copied = semaphore("aT_copied")
        gate_psum = semaphore("gate_psum")
        gz_done = semaphore("gz_done")
        gexp_done = semaphore("gexp_done")
        ge_done = semaphore("ge_done")
        eu_psum = semaphore("eu_psum")
        ew_psum = semaphore("ew_psum")
        eth_done = semaphore("eth_done")
        es_done = semaphore("es_done")
        eh_done = semaphore("eh_done")
        ey_psum = semaphore("ey_psum")
        ey_done = semaphore("ey_done")
        fin_psum = semaphore("fin_psum")
        fin_done = semaphore("fin_done")
        dve_chain = semaphore("dve_chain")
        numbers = sorted(s.num for s in signals)
        assert numbers == list(range(numbers[0], numbers[0] + len(numbers)))

        chain = [0]
        tt, ts, stt = nc.vector.tensor_tensor, nc.vector.tensor_scalar, nc.vector.scalar_tensor_tensor

        def link(ins):
            chain[0] += 1
            ins.then_inc(dve_chain, 1)
            nc.vector.wait_ge(dve_chain, chain[0])

        def rsqrt(dst, src, n, done):
            y, t = rs_out[:, 0:n], rs_tmp[:, 0:n]
            link(ts(y.bitcast(I32), src.bitcast(I32), -0.5, float(0x5f3759df), ALU.mult, ALU.add))
            for i in range(3):
                link(tt(t, y, y, ALU.mult))
                link(stt(t, t, -0.5, src, ALU.mult, ALU.mult))
                last = stt(y if i < 2 else dst, t, 1.5, y, ALU.add, ALU.mult)
                if i < 2 or done is None:
                    link(last)
                else:
                    last.then_inc(done, 1)

        def layernorm(dst, src, width, done):
            for c in range(NT):
                link(nc.vector.bn_stats(v3(stats[:], NT)[:, c], src[:, c])) if c == NT - 1 else nc.vector.bn_stats(
                    v3(stats[:], NT)[:, c], src[:, c])
            for c in range(NT):
                m = nc.vector.bn_aggr(v3(mv[:], NT)[:, c], v3(stats[:], NT)[:, c])
            link(m)
            link(ts(rs_in[:, 0:NT], v3(mv[:], NT)[:, :, 1], EPS, None, ALU.add))
            rsqrt(rs_in[:, NT:2 * NT], rs_in[:, 0:NT], NT, None)
            for c in range(NT):
                m = ts(dst[:, c], src[:, c], v3(mv[:], NT)[:, c, 0:1], rs_in[:, NT + c:NT + c + 1], ALU.subtract, ALU.mult)
            m.then_inc(done, 1)

        def head_norm():
            layernorm(v3(norm_tm[:], NT), v3(x_tm[:], NT), D, head_norm_done)

        def head_transpose():
            nc.tensor.wait_ge(head_norm_done, 1)
            for i in range(NT):
                m = nc.tensor.transpose(place("head")[:, i * P:(i + 1) * P], v3(norm_tm[:], NT)[:, i], C("ident"))
            m.then_inc(head_psum, 1)

        def head_copy():
            nc.vector.wait_ge(head_psum, 1)
            nc.vector.tensor_copy(xnT[:], place("head")[:])
            nc.vector.tensor_copy(hT[0:64, :], place("head")[0:64, :])
            nc.vector.tensor_copy(hT[64:P, 1:T], place("head")[64:P, 0:T - 1]).then_inc(head_copied, 1)
            nc.vector.wait_ge(head_copied, 1)

        early_w, early_c = W_AT["wo0"][0], C_AT["rcos"][0]
        with nc.Block(no_gpsimd_drain=True) as block:
            @block.tensor
            def _(pe):
                pe.wait_ge(setup_loads, 16 * 4)
                head_transpose()

            @block.sync
            def _(sp):
                sp.dma_start(v3(x_tm[:], NT), x[0:1].rearrange("a (t p) d -> p (a t) d", p=P)).then_inc(setup_loads, 16)
                sp.dma_start(c_sb[:, 0:early_c], consts[:, 0:early_c]).then_inc(setup_loads, 16)
                sp.dma_start(w_sb[:, 0:early_w], weights[:, 0:early_w]).then_inc(setup_loads, 16)
                sp.dma_start(w_sb[:, early_w:], weights[:, early_w:]).then_inc(late_loads, 16)
                sp.dma_start(c_sb[:, early_c:], consts[:, early_c:]).then_inc(late_loads, 16)
                sp.wait_ge(setup_loads, 16 * 4)

            @block.scalar
            def _(act):
                act.dma_start(shared[:, 0:B_N], consts_bf).then_inc(out_stored, 16)
                act.dma_start(r_sb[:], rows.to_broadcast([P, R_N])).then_inc(setup_loads, 16)

            @block.gpsimd
            def _(pool):
                for part in (warm[:], zeros, qTz[:], p_sb[:], latT[:], hT[:, 0:1], h2T[:, 0:1]):
                    nc.gpsimd.memset(part, 0.0).then_inc(zeroed, 1)
                pool.wait_ge(zeroed, 7)
                for c in range(NT):
                    pool.dma_start(in_dram(X_dram, c), v3(zeros, H0)).then_inc(X_zeroed, 16)

            @block.vector
            def _(dve):
                dve.wait_ge(setup_loads, 16 * 4)
                dve.wait_ge(out_stored, 16)
                head_norm()
                nc.vector.tensor_copy(b_sb[:], shared[:, 0:B_N]).then_inc(tables_done, 1)
                h = DF // 2
                for l in range(DEPTH):
                    for cos, sin, row, c_out, s_out in (("qcos", "qsin", "qs", "qc", "qs"), ("kcos", "ksin", "ks", "kc", "ks")):
                        g = R(row)[:, l * DF:(l + 1) * DF]
                        c_out, s_out = v3(tab[c_out][l], NT), v3(tab[s_out][l], NT)
                        tt, sines = nc.vector.tensor_tensor, v3(C(sin), NT)
                        tt(c_out, v3(C(cos), NT), repeat(g, NT), ALU.mult).then_inc(tables_done, 1)
                        tt(s_out[:, :, 0:h], sines[:, :, 0:h], repeat(g[:, h:], NT), ALU.mult).then_inc(tables_done, 1)
                        tt(s_out[:, :, h:], sines[:, :, h:], repeat(g[:, 0:h], NT), ALU.mult).then_inc(tables_done, 1)
                nc.vector.tensor_scalar(v3(norm_w[:], H0), repeat(R("norm_w"), H0), -0.5 * DK ** -0.5, None, ALU.mult)\
                    .then_inc(tables_done, 1)
                dve.wait_ge(tables_done, 6 * DEPTH + 2)
                dve.wait_ge(zeroed, 7)
                head_copy()

        nc.sync.sem_clear(range(numbers[0], numbers[-1] + 1))
        nc.all_engine_barrier()

        def steps_delta():
            s = [("k", c) for c in range(NT)] + [("krs",)] + [("bg", c) for c in range(NT)]
            s += [("kT", c) for c in range(NT)] + [("gram", c) for c in range(NT)]
            s += [("qT", h) for h in range(H0)] + [("solve",)]
            for two in ((0, 1), (2, 3)):
                s += [("inv_load", c) for c in two]
                for k in range(LEVELS):
                    s += [("inv_v", k, c) for c in two]
                    if k:
                        s += [("inv_zx", k, c) for c in two]
                for c in two:
                    s += [("seq_b", c), ("seq_p", c), ("seq_u", c), ("seq_o", c)]
            return s + [("delta_norm",), ("oT0",)]

        def steps_ffn(l):
            s = []
            s += [("fqk", l, 0, 0), ("fqk", l, 0, 1), ("fv", l, 0), ("frs", l, 0), ("fscale", l, 0, 0), ("fscale", l, 0, 1)]
            s += [("fqk", l, 1, 0), ("fqk", l, 1, 1), ("fv", l, 1), ("fqT", l, 0), ("fkT", l, 0)]
            s += [("frs", l, 1), ("fscale", l, 1, 0), ("fscale", l, 1, 1)]
            n = NT * NPAIR
            for i in range(n + 4):
                if i >= 2 * NPAIR and i % NPAIR == 0:
                    s += [("fr1", l, i // NPAIR - 2)]
                if i < n:
                    s += [("fS", l, i)]
                if 1 <= i <= n:
                    s += [("fnorm", l, i - 1)]
                if 2 <= i < n + 2:
                    s += [("fPT", l, i - 2)]
                if i >= 7 and i % NPAIR == 3:
                    s += [("fwo", l, (i - 7) // NPAIR)]
                if 3 <= i < n + 3:
                    s += [("fPV", l, i - 3)]
                if i % NPAIR in (1, 2) and i < n - NPAIR:
                    s += [("fqT" if i % NPAIR == 1 else "fkT", l, i // NPAIR + 1)]
                c = i // NPAIR + 2
                if c < NT:
                    s += {0: [], 1: [("fqk", l, c, 0), ("fv", l, c)], 2: [("fqk", l, c, 1)],
                          3: [("frs", l, c), ("fscale", l, c, 0)]}[i % NPAIR]
                if i in (NPAIR, 2 * NPAIR):
                    s += [("fscale", l, c - 1, 1)]
            return s + [("fr1", l, NT - 1), ("fres", l), ("fln", l), ("hnT", l)] + [("fw1", l, j) for j in range(3)] + [("fw2", l)]

        def steps_latent():
            s = []
            for h in range(HM + LEAD):
                done = h - LEAD
                for t in range(3):
                    s += [("mS", h, t)] if h < HM else []
                    s += [("mST", done, t)] if done >= 0 else []
                if h < HM and h % GROUP == GROUP - 1:
                    s += [("mrow", h // GROUP)]
                s += [("head_norm",)] if done == 8 else []
                if done > GROUP and done % GROUP == 1:
                    s += [("mPV", done // GROUP - 1), ("matg", done // GROUP - 1)]
            return s + [("mPV", HM // GROUP - 1), ("head_T",), ("matg", HM // GROUP - 1), ("aT",)]

        def steps_moe():
            return [("gate",)] + [s for e in range(NE) for s in (("eu", e), ("ew", e), ("e_down", e))] + [("eu", NE), ("ew", NE)]

        def fill(main, other, counts):
            assert len(counts) == len(main) and sum(map(int, counts)) == len(other)
            out, other = [], list(other)
            for step, n in zip(main, counts):
                out.append(step)
                for _ in range(int(n)):
                    out.append(other.pop(0))
            return out

        latent = steps_latent()
        schedule = fill(steps_ffn(0) + steps_ffn(1), steps_delta(), DELTA_AFTER) + [("x1",), ("xn2T",)]
        schedule += fill([("lat",), ("mq",), ("latT",), ("mk",), ("mv",)] + latent, steps_moe(), EXPERTS_AFTER) + [("final",)]

        def walk(parts):
            for name, *args in schedule:
                if name in parts:
                    parts[name](*args)

        def pair(l, i):
            return l * NT * NPAIR + i

        def at_level(k, c, levels, first=0):
            return c // 2 * 2 * levels + 2 * (k - first) + c % 2

        with nc.Fori(0, BATCH) as b:
            with nc.Block(no_gpsimd_drain=True) as block:
                @block.tensor
                def _(pe):
                    mm = nc.tensor.matmul
                    ident = C("ident")
                    def transposes(ps, src, n=4, width=P, last=None):
                        for i in range(n):
                            m = nc.tensor.transpose(ps[0:width, i * P:(i + 1) * P], src(i), ident)
                        return m

                    def k(c):
                        if c == 3:
                            pe.wait_ge(ksq_done, 1)
                        ps = place("k", c)
                        mm(ps[:], xnT[:, c * P:(c + 1) * P], W("wk"), start=True, stop=True).then_inc(k_psum, 1)

                    def qT_(h):
                        if h < 3:
                            pe.wait_ge(L_done, h + 2)
                        else:
                            pe.wait_ge(qT_copied, 1)
                        ps = place("qT", h)
                        mm(ps[:], W("wq")[:, h * DK:(h + 1) * DK], xnT[:], start=True, stop=True).then_inc(qT_psum, 1)

                    def bg(c):
                        if c < 3:
                            pe.wait_ge(ksq_done, c + 2)
                        else:
                            pe.wait_ge(gs_done, 1)
                        ps = place("bg", c)
                        mm(ps[:, 0:NBG], xnT[:, c * P:(c + 1) * P], W("wbg"), start=True, stop=True).then_inc(bg_psum, 1)

                    def kT_(c):
                        if c < 3:
                            pe.wait_ge(gs_done, c + 2)
                        else:
                            pe.wait_ge(kT_copied, 1)
                        ps = place("kT", c)
                        pe.wait_ge(kn_done, c + 1)
                        transposes(ps, lambda i: v4(kn[:], NT, H0)[:, c, i]).then_inc(kT_psum, 1)

                    def gram(c):
                        kc = v4(kT[:], NT, H0)[:, c]
                        ps = place("G", c)
                        pe.wait_ge(kT_copied, min(c + 2, NT))
                        if c == 3:
                            pe.wait_ge(L_done, 1)
                        for h in range(H0):
                            m = mm(ps[:, h * P:(h + 1) * P], kc[:, h], kc[:, h], start=True, stop=True)
                        m.then_inc(G_psum, 1)

                    def seq_b(c):
                        kc = v4(kT[:], NT, H0)[:, c]
                        ps = place("B", c)
                        if c:
                            pe.wait_ge(Bm_done, c)
                        pe.wait_ge(qT_copied, H0)
                        for h in range(H0):
                            m = mm(ps[:, h * P:(h + 1) * P], kc[:, h], qT[:, h * T + c * P:h * T + (c + 1) * P], start=True, stop=True)
                        m.then_inc(B_psum, 1)

                    def inv_v(k, c):
                        n = at_level(k, c, LEVELS)
                        Lc, Xc, Zc = v4(L, 2, H0)[:, c % 2], v4(X, 2, H0)[:, c % 2], v4(Z, NT, H0)[:, c]
                        ps = place("V", k, c)
                        if k == 0:
                            pe.wait_ge(X_loaded[c % 2], 16 * (c // 2 + 1))
                            if c < 2:
                                pe.wait_ge(qT_copied, 3 + c)
                            elif c == 2:
                                pe.wait_ge(Bm_done, 2)
                            else:
                                pe.wait_ge(o_copied, 2)
                            m = transposes(ps, lambda i: Xc[:, i])
                        else:
                            if k == 1:
                                pe.wait_ge(L_loaded[c % 2], 16 * (c // 2 + 1))
                            else:
                                pe.wait_ge(X_done, at_level(k, c, LEVELS - 2, 1) - 1)
                            pe.wait_ge(Z_done, n - 1)
                            for h in range(H0):
                                m = mm(ps[:, h * P:(h + 1) * P], Lc[:, h], Zc[:, h], start=True, stop=True)
                        m.then_inc(V_psum, 1)

                    def inv_zx(k, c):
                        n = at_level(k, c, LEVELS)
                        Xc, Vc = v4(X, 2, H0)[:, c % 2], v4(Vm, 2, H0)[:, c % 2]
                        pe.wait_ge(Z_done, n)
                        if k == 1 and c == 2:
                            pe.wait_ge(S_done, 2)
                        ps = place("ZV", k, c)
                        pe.wait_ge(Vm_done, at_level(k, c, LEVELS - 1, 1) + 1)
                        for h in range(H0):
                            m = mm(ps[:, h * P:(h + 1) * P], Xc[:, h], Vc[:, h], start=True, stop=True)
                        m.then_inc(ZV_psum, 1)
                        if k < LEVELS - 1:
                            ps = place("VX", k, c)
                            for h in range(H0):
                                m = mm(ps[:, h * P:(h + 1) * P], Vc[:, h], Xc[:, h], start=True, stop=True)
                            m.then_inc(VX_psum, 1)

                    def seq_p(c):
                        if c:
                            pe.wait_ge(o_copied, c)
                        ps = place("P", c)
                        m = mm(ps[:, 0:P], xnT[:, c * P:(c + 1) * P], W("wv"), start=True, stop=c == 0, skip_group_check=True)
                        if c:
                            pe.wait_ge(S_done, c)
                            for h in range(H0):
                                m = mm(ps[:, h * DV:(h + 1) * DV], v4(kT[:], NT, H0)[:, c, h], Sn[:, h * DV:(h + 1) * DV],
                                       start=False, stop=True, skip_group_check=True)
                        m.then_inc(P_psum, 1)

                    def seq_u(c):
                        if c % 2 == 0:
                            pe.wait_ge(Z_done, LEVELS * (c + 2))
                        ps = place("U", c)
                        pe.wait_ge(R_done, c + 1)
                        pe.wait_ge(Z_done, at_level(LEVELS - 1, c, LEVELS) + 1)
                        for h in range(H0):
                            m = mm(ps[:, h * DV:(h + 1) * DV], v4(Z, NT, H0)[:, c, h], R_sb[:, h * DV:(h + 1) * DV], start=True, stop=True)
                        m.then_inc(U_psum, 1)

                    def seq_o(c):
                        pe.wait_ge(U_copied, c + 1)
                        pe.wait_ge(Bm_done, c + 1)
                        ps = place("O", c)
                        for k in range(2 if c else 1):
                            for h in range(H0):
                                left = (Sn if k else U_sb)[:, h * DV:(h + 1) * DV]
                                right = qT[:, h * T + c * P:h * T + (c + 1) * P] if k else v3(Bm, H0)[:, h]
                                m = mm(ps[h * DV:(h + 1) * DV, 0:P], left, right, start=k == 0, stop=k == (1 if c else 0),
                                       skip_group_check=True)
                        m.then_inc(O_psum, 1)
                        if c < NT - 1:
                            ps = place("dS", c)
                            for h in range(H0):
                                m = mm(ps[:, h * DV:(h + 1) * DV], v4(kn[:], NT, H0)[:, c, h], U_sb[:, h * DV:(h + 1) * DV],
                                       start=True, stop=True)
                            m.then_inc(dS_psum, 1)

                    def delta_norm():
                        ps = place("o")
                        pe.wait_ge(o_copied, NT)
                        pe.wait_ge(Bm_done, NT)
                        transposes(ps, lambda i: oT0[:, i * P:(i + 1) * P]).then_inc(o_psum, 1)

                    def oT0_():
                        ps = place("oT0")
                        pe.wait_ge(og_done, 1)
                        transposes(ps, lambda i: v3(o_all[:], NT)[:, i]).then_inc(oT0_psum, 1)

                    def fqk(l, c, i):
                        n = 2 * (l * NT + c) + i
                        if l:
                            pe.wait_ge(h_done, 1)
                        if c == 1:
                            pe.wait_ge(fsq_done, n - 1)
                            pe.wait_ge(frot_done, n - 1)
                        elif c >= 2:
                            pe.wait_ge(fexp_done, 2 * pair(l, (c - 2) * NPAIR + i) + 2)
                        m = mm(place(("fq", "fk")[i], l, c)[:], hT[:, c * P:(c + 1) * P], W(f"wqkv{l}")[:, i * T:(i + 1) * T],
                               start=True, stop=True)
                        m.then_inc(fk_psum if i else fq_psum, 1)

                    def fv(l, c):
                        n = l * NT + c + 1
                        if c in (1, 2):
                            pe.wait_ge(fv_copied, n - 1)
                        elif c == 3:
                            pe.wait_ge(fPT_copied, pair(l, 3) + 1)
                        mm(place("fv", l, c)[:], hT[:, c * P:(c + 1) * P], W(f"wqkv{l}")[:, 2 * T:3 * T], start=True, stop=True)\
                            .then_inc(fv_psum, 1)

                    def fqT(l, c):
                        n = l * NT + c + 1
                        pe.wait_ge(fn_done, 2 * n - 1)
                        if c in (1, 2):
                            pe.wait_ge(fkT_copied, n - 1)
                        elif c == 3:
                            pe.wait_ge(r1_done, l * NT + 1)
                        ps = place("fqT", l, c)
                        transposes(ps, lambda i: v4(q_f[:], 2, 4)[:, c % 2, i]).then_inc(fqT_psum, 1)

                    def fkT(l, c):
                        n = l * NT + c + 1
                        if c:
                            pe.wait_ge(fqT_lo, n)
                            pe.wait_ge(fqT_hi, n)
                        pe.wait_ge(fn_done, 2 * n)
                        ps = place("fkT", l, c)
                        transposes(ps, lambda i: v4(k_f[:], 2, 4)[:, c % 2, i]).then_inc(fkT_psum, 1)

                    def fS(l, i):
                        c, g = divmod(i, NPAIR)
                        n = l * NT + c + 1
                        pe.wait_ge(fqT_lo, n)
                        pe.wait_ge(fqT_hi, n)
                        pe.wait_ge(fkT_copied, n)
                        if i in (0, 1, 2, 3, 6, 7):
                            later = 2 * (l * NT + (i + 2) // 2 - (i > 3)) + i % 2 + 1
                            pe.wait_ge(frot_done, later)
                            pe.wait_ge(fsq_done, later)
                        else:
                            pe.wait_ge(fexp_done, 2 * pair(l, i - 2) + 2)
                        ps = v3(place("fS", l, i)[:], 2)
                        lo = 128 if c == 0 else 64
                        mm(ps[:, :, lo:256], B("identb"), repeat(B("band")[:, lo - 64:192], 2), start=True, stop=False,
                           skip_group_check=True)
                        keys = kTf[:, g * T + c * P - 128 + lo:g * T + (c + 1) * P]
                        for j in range(2):
                            q = v4(qTz[:], 2, HF)[:, c % 2, 2 * g + j]
                            m = mm(ps[:, j, lo:256], q, keys, start=False, stop=True, skip_group_check=True)
                        m.then_inc(fS_psum, 1)

                    def fPT(l, i):
                        c = i // NPAIR
                        n = pair(l, i) + 1
                        if i in (0, NPAIR):
                            pe.wait_ge(fv_copied, l * NT + (3 if i == 0 else 4))
                        else:
                            pe.wait_ge(fPT_copied, n - 1)
                        ps = place("fPT", l, i)
                        pe.wait_ge(fnorm_done, n)
                        p = v4(p_sb[:], P_SLOTS, 4)[:, pair(l, i) % P_SLOTS]
                        for j in ((1, 3) if c == 0 else range(4)):
                            m = nc.tensor.transpose(ps[:, j * P:(j + 1) * P], p[:, j], ident)
                        m.then_inc(fPT_psum, 1)

                    def fPV(l, i):
                        c, g = divmod(i, NPAIR)
                        ps = place("fO", l, c)
                        pe.wait_ge(fPT_copied, pair(l, i) + 1)
                        if g == 0:
                            pe.wait_ge(fv_copied, l * NT + c + 1)
                        pt = v4(pT[:], 2, 4)[:, i % 2]
                        for k in ((0, 1) if c else (1,)):
                            for j in range(2):
                                v = (c - 1 + k) * T + (2 * g + j) * DF
                                m = mm(ps[j * DF:(j + 1) * DF, g * P:(g + 1) * P], v_f[:, v:v + DF], pt[:, 2 * j + k],
                                       start=k == (0 if c else 1), stop=k == 1, skip_group_check=True)
                        m.then_inc(fO_psum, 1)

                    def fwo(l, c):
                        n = l * NT + c + 1
                        if n == 1:
                            pe.wait_ge(late_loads, 32)
                        pe.wait_ge(foT_copied, n)
                        if c < 2:
                            pe.wait_ge(fkT_copied, n + 2)
                        else:
                            pe.wait_ge(r1_done, n - 1)
                        for j in range(4):
                            m = mm(place("fwo", l)[:, c * P:(c + 1) * P], W(f"wof{l}")[:, j * D:(j + 1) * D],
                                   v4(oTf, 2, 4)[:, c % 2, j], start=j == 0, stop=j == 3)
                        m.then_inc(fwo_psum, 1)

                    def fln(l):
                        ps = place("h2tm", l)
                        pe.wait_ge(h2_done, l + 1)
                        transposes(ps, lambda i: h2T[:, i * P:(i + 1) * P]).then_inc(h2tm_psum, 1)

                    def hnT_(l):
                        ps = place("normT", l)
                        pe.wait_ge(norm_done, l + 1)
                        transposes(ps, lambda i: v3(norm_tm[:], NT)[:, i]).then_inc(normT_psum, 1)

                    def fw1(l, j):
                        at, m = HID_TILES[j]
                        n = 3 * l + j + 1
                        pe.wait_ge(hn_done, l + 1)
                        if j == 2:
                            pe.wait_ge(gelu_done, 3 * l + 1)
                            pe.wait_ge(hm_done, 3 * l + 1)
                        ps = place("fg", l, j)
                        mm(ps[0:m, :], W(f"w1{l}")[:, HID + at:HID + at + m], hnT[:], start=True, stop=True).then_inc(fg_psum, 1)
                        ps = place("fa", l, j)
                        mm(ps[0:m, :], W(f"w1{l}")[:, at:at + m], hnT[:], start=True, stop=True).then_inc(fa_psum, 1)

                    def fw2(l):
                        ps = place("fw2", l)
                        for j, (_, m) in enumerate(HID_TILES):
                            pe.wait_ge(hm_done, 3 * l + j + 1)
                            i = mm(ps[:], W(f"w2{l}")[0:m, j * D:(j + 1) * D], hm[0:m, j * T:(j + 1) * T], start=j == 0, stop=j == 2)
                        i.then_inc(fw2_psum, 1)

                    def x1():
                        ps = place("x1")
                        pe.wait_ge(r_done, DEPTH)
                        pe.wait_ge(oT0_copied, 1)
                        for c in range(NT):
                            o = ps[:, c * P:(c + 1) * P]
                            mm(o, oT0[:, c * P:(c + 1) * P], W("wo0"), start=True, stop=False)
                            m = mm(o, r2T[:, c * P:(c + 1) * P], ident, start=False, stop=True)
                        m.then_inc(x1_psum, 1)

                    def xn2T_():
                        ps = place("normT", 2)
                        pe.wait_ge(norm_done, 3)
                        transposes(ps, lambda i: v3(norm_tm[:], NT)[:, i]).then_inc(normT_psum, 1)

                    def lat():
                        ps = place("lat")
                        pe.wait_ge(xn2_copied, 1)
                        for c in range(NT):
                            m = mm(ps[:, c * LAT:(c + 1) * LAT], xn2T[:, c * P:(c + 1) * P], W("Wdkv"), start=True, stop=True)
                        m.then_inc(lat_psum, 1)

                    def latT_():
                        ps = place("latT")
                        pe.wait_ge(lat_done, 1)
                        transposes(ps, lambda i: v3(lat_tm[:], NT)[:, i], width=LAT).then_inc(latT_psum, 1)

                    def project(first, weights, src):
                        for i, w in enumerate(weights):
                            if first + i == 3:
                                pe.wait_ge(rope_done, 1)
                            ps = place("mq", first + i)
                            mm(ps[:], W(w), src, start=True, stop=True).then_inc(mq_psum, 1)

                    def mq():
                        project(0, ("Wq", "Wqr"), xn2T[:])

                    def mk():
                        pe.wait_ge(latT_done, 1)
                        project(2, ("Wuk", "Wukr"), latT[:])

                    def mv_():
                        ps = place("mv")
                        for c in range(NT):
                            m = mm(ps[:, c * P:(c + 1) * P], latT[:, c * P:(c + 1) * P], W("Wuv"), start=True, stop=True)
                        m.then_inc(mv_psum, 1)

                    def mS(h, t):
                        if (h, t) == (0, 0):
                            pe.wait_ge(parts_sent, 12 * 16)
                            pe.wait_ge(rows_filled, 32)
                        if h == HM // 2:
                            pe.wait_ge(late_keys_sent, 3 * 16)
                        if h:
                            pe.wait_ge(nmx_done, 4 * (h - 1) + (2, 3, 4)[t])
                        ps = place("mS", h, t)
                        at = 0
                        for c in ((0, 2), (1,), (3,))[t]:
                            n = (c + 1) * P
                            mm(ps[:, at + c * P:at + n], B("identb"), B("causal"), start=True, stop=False, skip_group_check=True)
                            m = mm(ps[:, at:at + n], Qst[:, h * T + c * P:h * T + (c + 1) * P], Kst[:, h * T:h * T + n],
                                   start=False, stop=True, skip_group_check=True)
                            at += n
                        m.then_inc(mS_psum, 1)

                    def mrow(g):
                        pe.wait_ge(nmx_done, NT * GROUP * (g + 1))
                        if g == 0:
                            pe.wait_ge(vaug_done, 1)
                        elif g < 3:
                            pe.wait_ge(mrow_done, g)
                        else:
                            pe.wait_ge(at_done, 1)
                        nc.tensor.transpose(place("mrow", g)[0:NROW, 0:P], nmx[:, g * NROW:(g + 1) * NROW], ident)\
                            .then_inc(mrow_psum, 1)

                    def mST(h, t):
                        if h % GROUP == 0 and t == 0:
                            pe.wait_ge(mrow_sent, 48 * (h // GROUP + 1))
                        if h:
                            pe.wait_ge(mexp_done, 3 * (h - 1) + t + 1)
                        ps = place("mST", h, t)
                        at = 0
                        for j in ((0,), (1, 3), (2,))[t]:
                            n = T - j * P
                            mm(ps[:, at:at + P], B("identb"), B("causalT"), start=True, stop=False, skip_group_check=True)
                            m = mm(ps[:, at:at + n], Kst[:, h * T + j * P:h * T + (j + 1) * P], Qst[:, h * T + j * P:(h + 1) * T],
                                   start=False, stop=True, skip_group_check=True)
                            at += n
                        m.then_inc(mST_psum, 1)

                    def mPV(g):
                        if g < 2:
                            pe.wait_ge(mrow_done, 3 + g)
                        if g:
                            pe.wait_ge(at_done, g)
                        ps = place("mPV", g)
                        pe.wait_ge(mexp_done, 3 * GROUP * (g + 1))
                        pe.wait_ge(vaug_done, 1)
                        start = {0: 0, 1: T, 3: 2 * T - P, 2: 2 * T}
                        for j in range(NT):
                            n = T - j * P
                            for i in range(GROUP):
                                h = GROUP * g + i
                                m = mm(ps[VW * i:VW * (i + 1), j * P:T], v3(vaug[:], NT * HM)[:, j * HM + h],
                                       PTm[h % PT_SLOTS][:, start[j]:start[j] + n], start=j == 0, stop=j == NT - 1,
                                       skip_group_check=True)
                        m.then_inc(mPV_psum, 1)

                    def matg(g):
                        ps = place("matg", g)
                        pe.wait_ge(atg_done, g + 1)
                        transposes(ps, lambda i: atg[:, (g % 2) * T + i * P:(g % 2) * T + (i + 1) * P]).then_inc(matg_psum, 1)

                    def aT_():
                        ps = place("aT")
                        pe.wait_ge(at_done, HM // GROUP)
                        transposes(ps, lambda i: v3(at_tm[:], NT)[:, i]).then_inc(aT_psum, 1)

                    def gate():
                        ps = place("gate")
                        pe.wait_ge(xn2_copied, 1)
                        for c in range(NT):
                            m = mm(ps[:, c * NE:(c + 1) * NE], xn2T[:, c * P:(c + 1) * P], W("gate"), start=True, stop=True)
                        m.then_inc(gate_psum, 1)

                    def eu(e):
                        if e:
                            pe.wait_ge(ey_done, e)
                        else:
                            pe.wait_ge(gz_done, 1)
                        mm(place("eu", e)[:], W(f"eu{e}"), xn2T[:], start=True, stop=True).then_inc(eu_psum, 1)

                    def ew(e):
                        pe.wait_ge(es_done, e + 1)
                        mm(place("ew", e)[:], W(f"ew{e}"), xn2T[:], start=True, stop=True).then_inc(ew_psum, 1)

                    def e_down(e):
                        ps = place("ey", e)
                        pe.wait_ge(eh_done, e + 1)
                        for c in range(NT):
                            m = mm(ps[:, c * P:(c + 1) * P], he[:, (e % 2) * T + c * P:(e % 2) * T + (c + 1) * P], W(f"ed{e}"),
                                   start=True, stop=True)
                        m.then_inc(ey_psum, 1)

                    def final():
                        ps = place("fin")
                        pe.wait_ge(eh_done, NE + 1)
                        pe.wait_ge(aT_copied, 1)
                        for c in range(NT):
                            o = ps[:, c * P:(c + 1) * P]
                            s = NE % 2 * T + c * P
                            mm(o, he[:, s:s + P], W(f"ed{NE}"), start=True, stop=False)
                            m = mm(o, aT[:, c * P:(c + 1) * P], W("Wo"), start=False, stop=True)
                        m.then_inc(fin_psum, 1)

                    walk({"k": k, "qT": qT_, "bg": bg, "kT": kT_, "gram": gram, "inv_v": inv_v, "inv_zx": inv_zx,
                          "seq_b": seq_b, "seq_p": seq_p, "seq_u": seq_u, "seq_o": seq_o, "delta_norm": delta_norm, "oT0": oT0_, "fqk": fqk, "fv": fv, "fqT": fqT, "fkT": fkT, "fS": fS,
                          "fPT": fPT, "fPV": fPV, "fwo": fwo, "fln": fln, "hnT": hnT_, "fw1": fw1, "fw2": fw2,
                          "x1": x1, "xn2T": xn2T_, "lat": lat, "latT": latT_, "mq": mq, "mk": mk, "mv": mv_, "mS": mS,
                          "mrow": mrow, "head_T": head_transpose, "mST": mST, "mPV": mPV, "matg": matg, "aT": aT_, "gate": gate, "eu": eu, "ew": ew,
                          "e_down": e_down, "final": final})

                @block.scalar
                def _(act):
                    af = nc.scalar.activation


                    def copy_out(dst, key, full, n, done):
                        act.wait_ge(full, n)
                        af(dst, place(*key)[:], ACT.Copy).then_inc(done, 1)

                    def k(c):
                        copy_out(kn[:, c * T:(c + 1) * T], ("k", c), k_psum, c + 1, k_copied)
                        af(kT[:, c * T:(c + 1) * T], place("k", c)[:], ACT.Square).then_inc(ksq_done, 1)

                    def bg(c):
                        act.wait_ge(bg_psum, c + 1)
                        af(th[:, c * NBG:(c + 1) * NBG], place("bg", c)[:, 0:NBG], ACT.Tanh, scale=0.5).then_inc(th_done, 1)

                    def inv_v(k, c):
                        if k == 0:
                            copy_out(Z[:, c * T:(c + 1) * T], ("V", k, c), V_psum, at_level(k, c, LEVELS) + 1, Z_done)

                    def seq_u(c):
                        act.wait_ge(U_psum, c + 1)
                        if c >= 2:
                            act.wait_ge(dS_psum, c)
                        elif c == 1:
                            act.wait_ge(dS_psum, 1)
                        af(U_sb[:], place("U", c)[:, 0:P], ACT.Copy).then_inc(U_copied, 1)

                    def seq_o(c):
                        act.wait_ge(O_psum, c + 1)
                        af(oT0[:, c * P:(c + 1) * P], place("O", c)[:, 0:P], ACT.Copy).then_inc(o_copied, 1)

                    def delta_norm():
                        act.wait_ge(o_psum, 1)
                        af(o_all[:], place("o")[:], ACT.Copy).then_inc(o_back, 1)
                        af(kn[:, 0:T], place("o")[:], ACT.Square).then_inc(osq_done, 1)

                    def fqk(l, c, i):
                        m = 2 * (l * NT + c) + i
                        if m >= 2:
                            act.wait_ge(fsum_done, m - 1)
                        act.wait_ge(fk_psum if i else fq_psum, l * NT + c + 1)
                        af(rot[m % 2][:], place(("fq", "fk")[i], l, c)[:], ACT.Square).then_inc(fsq_done, 1)

                    def fv(l, c):
                        act.wait_ge(fv_psum, l * NT + c + 1)
                        if l:
                            act.wait_ge(fO_psum, NT * NPAIR)
                        af(v_f[:, c * T:(c + 1) * T], place("fv", l, c)[:], ACT.Copy).then_inc(fv_copied, 1)

                    def fqT(l, c):
                        n = l * NT + c
                        act.wait_ge(fqT_psum, n + 1)
                        if n >= 2:
                            act.wait_ge(fS_psum, (n - 1) * NPAIR)
                        half = slice(0, DF)
                        af(v4(qTz[:], 2, HF)[half, c % 2, 0:HF:2], v3(place("fqT", l, c)[:], NPAIR)[half], ACT.Copy).then_inc(fqT_lo, 1)

                    def fkT(l, c):
                        act.wait_ge(fkT_psum, l * NT + c + 1)
                        if l:
                            act.wait_ge(fS_psum, NT * NPAIR)
                        af(v4(kTf[:], NPAIR, NT)[:, :, c], v3(place("fkT", l, c)[:], NPAIR), ACT.Copy).then_inc(fkT_copied, 1)

                    def fS(l, i):
                        c, g = divmod(i, NPAIR)
                        n = pair(l, i)
                        act.wait_ge(fmax_done, n + 1)
                        if n >= P_SLOTS:
                            act.wait_ge(fPT_psum, n + 1 - P_SLOTS)
                        lo = 128 if c == 0 else 64
                        for j in range(2):
                            h = c * HF + 2 * g + j
                            af(v3(p_sb[:, pair(l, i) % P_SLOTS * T:(pair(l, i) % P_SLOTS + 1) * T], 2)[:, j, lo:256], v3(place("fS", l, i)[:], 2)[:, j, lo:256], ACT.Exp,
                               bias=nmax[:, h:h + 1], accum_out=psums[:, h:h + 1]).then_inc(fexp_done, 1)

                    def fPT(l, i):
                        n = pair(l, i)
                        act.wait_ge(fPT_psum, n + 1)
                        if n >= 2:
                            act.wait_ge(fO_psum, n - 1)
                        ps, dst = v4(place("fPT", l, i)[:], 2, 2), v4(pT[:, (i % 2) * T:(i % 2 + 1) * T], 2, 2)
                        if i // NPAIR == 0:
                            ps, dst = ps[:, :, 1], dst[:, :, 1]
                        af(dst, ps, ACT.Copy).then_inc(fPT_copied, 1)

                    def fPV(l, i):
                        c, g = divmod(i, NPAIR)
                        if g < NPAIR - 1:
                            return
                        n = l * NT + c
                        act.wait_ge(fO_psum, pair(l, i) + 1)
                        if n >= 2:
                            act.wait_ge(fwo_psum, n - 1)
                        af(oTf[:, c % 2 * T:(c % 2 + 1) * T], place("fO", l, c)[:], ACT.Copy).then_inc(foT_copied, 1)

                    def fln(l):
                        af(warm[:, 1:2], warm[:, 0:1], ACT.Gelu)

                    def fw2(l):
                        af(warm[:, 1:2], warm[:, 0:1], ACT.Exp)

                    def fw1(l, j):
                        _, m = HID_TILES[j]
                        n = 3 * l + j
                        act.wait_ge(late_loads, 32)
                        act.wait_ge(fg_psum, n + 1)
                        if n >= 2:
                            act.wait_ge(hm_done, n - 1)
                        af(gl[0:m, (n % 2) * T:(n % 2 + 1) * T], place("fg", l, j)[0:m, :], ACT.Gelu,
                           bias=W(f"cols{l}")[0:m, 3 + j:4 + j]).then_inc(gelu_done, 1)

                    def split(i):
                        act.wait_ge(qkf_done, i + 1)
                        af(parts[:, 3 * i * T:(3 * i + 1) * T], qkf[:, i * T:(i + 1) * T], ACT.Copy).then_inc(split_done, 1)
                        act.wait_ge(split2_done, 2 * i + 1)
                        af(parts[:, (3 * i + 1) * T:(3 * i + 2) * T], res[:, i * T:(i + 1) * T], ACT.Copy).then_inc(split_done, 1)

                    def mv_():
                        act.wait_ge(mv_psum, 1)
                        act.wait_ge(vaug_zeroed, 2)
                        af(v3(vaug[:], NT * HM)[:, :, 0:DM], v3(place("mv")[:], NT * HM), ACT.Copy).then_inc(vaug_done, 1)

                    def mST(h, t):
                        if h >= PT_SLOTS and t == 0:
                            act.wait_ge(mPV_psum, (h - PT_SLOTS) // GROUP + 1)
                        at, n = ((0, T), (T, T), (2 * T, 2 * P))[t]
                        act.wait_ge(mST_psum, 3 * h + t + 1)
                        af(PTm[h % PT_SLOTS][:, at:at + n], place("mST", h, t)[:, 0:n], ACT.Exp).then_inc(mexp_done, 1)

                    def mPV(g):
                        if g >= 2:
                            act.wait_ge(matg_psum, g - 1)
                        act.wait_ge(mPV_psum, g + 1)
                        af(atg[:, (g % 2) * T:(g % 2 + 1) * T], place("mPV", g)[:], ACT.Copy).then_inc(atg_done, 1)

                    def gate():
                        act.wait_ge(gz_done, 1)
                        af(gp[:], gz[:], ACT.Exp, scale=-1.0).then_inc(gexp_done, 1)

                    def eu(e):
                        act.wait_ge(eu_psum, e + 1)
                        if e >= 2:
                            act.wait_ge(es_done, e - 1)
                        af(the[:, (e % 2) * T:(e % 2 + 1) * T], place("eu", e)[:], ACT.Tanh, scale=0.5).then_inc(eth_done, 1)

                    walk({"k": k,
                          "qT": lambda h: copy_out(qT[:, h * T:(h + 1) * T], ("qT", h), qT_psum, h + 1, qT_copied), "bg": bg,
                          "kT": lambda c: copy_out(kT[:, c * T:(c + 1) * T], ("kT", c), kT_psum, c + 1, kT_copied),
                          "inv_v": inv_v, "seq_u": seq_u, "seq_o": seq_o, "delta_norm": delta_norm,
                          "oT0": lambda: copy_out(oT0[:], ("oT0",), oT0_psum, 1, oT0_copied), "fqk": fqk, "fv": fv, "fqT": fqT, "fkT": fkT,
                          "fS": fS, "fPT": fPT, "fPV": fPV, "fw1": fw1, "fln": fln, "fw2": fw2,
                          "xn2T": lambda: copy_out(xn2T[:], ("normT", 2), normT_psum, 3, xn2_copied),
                          "mq": lambda: split(0), "mk": lambda: split(1), "mv": mv_, "mST": mST, "mPV": mPV,
                          "aT": lambda: copy_out(aT[:], ("aT",), aT_psum, 1, aT_copied), "gate": gate, "eu": eu})

                @block.vector
                def _(dve):
                    tt, ts, stt = nc.vector.tensor_tensor, nc.vector.tensor_scalar, nc.vector.scalar_tensor_tensor


                    chain[0] = 0

                    def shifted(dst, src):
                        nc.vector.tensor_copy(dst[0:64, :], src[0:64, :])
                        return nc.vector.tensor_copy(dst[64:P, 1:T], src[64:P, 0:T - 1])

                    def k(c):
                        dve.wait_ge(ksq_done, c + 1)
                        nc.vector.tensor_reduce(kss[:, c * H0:(c + 1) * H0], v3(kT[:, c * T:(c + 1) * T], H0), AX, ALU.add).then_inc(kss_done, 1)

                    def krs_():
                        dve.wait_ge(kss_done, NT)
                        link(ts(kss[:], kss[:], 1e-12, None, ALU.add))
                        rsqrt(krs[:], kss[:], NT * H0, krs_done)

                    def bg(c):
                        t = th[:, c * NBG:(c + 1) * NBG]
                        dve.wait_ge(th_done, c + 1)
                        ts(beta[:, c * H0:(c + 1) * H0], t[:, 0:H0], 0.5, 0.5, ALU.mult, ALU.add).then_inc(beta_done, 1)
                        stt(gs[:, c * P:(c + 1) * P], t[:, H0:NBG], 1.0, place("bg", c)[:, H0:NBG], ALU.add, ALU.mult).then_inc(gs_done, 1)

                    def gram(c):
                        dve.wait_ge(G_psum, c + 1)
                        dve.wait_ge(beta_done, c + 1)
                        if c >= 2:
                            dve.wait_ge(L_kept[c % 2], 16)
                        for h in range(H0):
                            m = stt(v4(L, 2, H0)[:, c % 2, h], v3(place("G", c)[:], H0)[:, h], beta[:, c * H0 + h:c * H0 + h + 1],
                                    C("strict"), ALU.mult, ALU.mult)
                        m.then_inc(L_done, 1)

                    def seq_b(c):
                        dve.wait_ge(B_psum, c + 1)
                        if c:
                            dve.wait_ge(O_psum, c)
                        tt(v3(Bm, H0), v3(place("B", c)[:], H0), repeat(C("upper"), H0), ALU.mult).then_inc(Bm_done, 1)

                    def solve():
                        dve.wait_ge(Lb_loaded, 16)
                        l, x = v3(Lb, BLK), v3(Xb, BLK)
                        link(nc.vector.memset(Xb, 0.0))
                        link(nc.vector.memset(Xb[:, 0:BLK * BLK:BLK + 1], 1.0))
                        for i in range(1, BLK):
                            t = v3(prod[:, 0:i * i], i)
                            link(tt(t, repeat(l[:, i, 0:i], i), x[:, 0:i, 0:i].rearrange("p j n -> p n j"), ALU.mult))
                            m = nc.vector.tensor_reduce(x[:, i, 0:i], t, AX, ALU.add, negate=True)
                            link(m) if i < BLK - 1 else m.then_inc(Xb_done, 1)

                    def inv_v(k, c):
                        if k == 0:
                            return
                        dve.wait_ge(V_psum, at_level(k, c, LEVELS) + 1)
                        mask = repeat(B("lowT")[:, (k - 1) * P:k * P], H0)
                        tt(v4(Vm, 2, H0)[:, c % 2], v3(place("V", k, c)[:], H0), mask, ALU.mult).then_inc(Vm_done, 1)

                    def inv_zx(k, c):
                        Zc, Xc = v4(Z, NT, H0)[:, c], v4(X, 2, H0)[:, c % 2]
                        dve.wait_ge(ZV_psum, at_level(k, c, LEVELS - 1, 1) + 1)
                        dve.wait_ge(Z_done, at_level(k - 1, c, LEVELS) + 1)
                        tt(Zc, Zc, v3(place("ZV", k, c)[:], H0), ALU.add).then_inc(Z_done, 1)
                        if k < LEVELS - 1:
                            dve.wait_ge(VX_psum, at_level(k, c, LEVELS - 2, 1) + 1)
                            if k > 1:
                                dve.wait_ge(X_done, at_level(k - 1, c, LEVELS - 2, 1) + 1)
                            tt(Xc, Xc, v3(place("VX", k, c)[:], H0), ALU.add).then_inc(X_done, 1)

                    def seq_p(c):
                        dve.wait_ge(P_psum, c + 1)
                        if c:
                            dve.wait_ge(U_psum, c)
                        tt(v3(R_sb[:], H0), v3(place("P", c)[:, 0:P], H0), spread(beta[:, c * H0:(c + 1) * H0], DV), ALU.mult)\
                            .then_inc(R_done, 1)

                    def seq_o(c):
                        if c < NT - 1:
                            dve.wait_ge(dS_psum, c + 1)
                            ps = place("dS", c)[:, 0:P]
                            if c:
                                dve.wait_ge(S_done, c)
                                tt(Sn[:], Sn[:], ps, ALU.subtract).then_inc(S_done, 1)
                            else:
                                ts(Sn[:], ps, -1.0, None, ALU.mult).then_inc(S_done, 1)

                    def delta_norm():
                        dve.wait_ge(osq_done, 1)
                        link(nc.vector.tensor_reduce(oss[:], v3(kn[:, 0:T], NT * H0), AX, ALU.add))
                        link(ts(oss[:], oss[:], 1.0 / (DK * DV), EPS, ALU.mult, ALU.add))
                        rsqrt(ors[:], oss[:], NT * H0, ors_done)

                    def fqk(l, c, i):
                        n = l * NT + c
                        full, turned, dst, tc, tsn = ((fq_psum, fqT_psum, q_f, "qc", "qs"), (fk_psum, fkT_psum, k_f, "kc", "ks"))[i]
                        m = 2 * n + i
                        at = c * DF
                        dve.wait_ge(fsq_done, m + 1)
                        nc.vector.tensor_reduce(qk_ss[:, c % 2 * 16 + 8 * i:c % 2 * 16 + 8 * i + 8], v3(rot[m % 2][:], HF), AX, ALU.add)\
                            .then_inc(fss_done, 1)
                        dve.wait_ge(full, n + 1)
                        if n >= 2:
                            dve.wait_ge(turned, n - 1)
                        ps = v3(place(("fq", "fk")[i], l, c)[:], HF)
                        tt(v3(dst[:, c % 2 * T:(c % 2 + 1) * T], HF), ps, repeat(tab[tc][l][:, at:at + DF], HF), ALU.mult).then_inc(ft1_done, 1)
                        dve.wait_ge(fss_done, m + 1)
                        r = v3(rot[m % 2][:], HF)
                        hd = DF // 2
                        tt(r[:, :, 0:hd], ps[:, :, hd:DF], repeat(tab[tsn][l][:, at:at + hd], HF), ALU.mult)
                        tt(r[:, :, hd:DF], ps[:, :, 0:hd], repeat(tab[tsn][l][:, at + hd:at + DF], HF), ALU.mult).then_inc(frot_done, 1)

                    def frs(l, c):
                        n = l * NT + c
                        if n >= 2:
                            dve.wait_ge(fn_done, 2 * (n - 1))
                        dve.wait_ge(fss_done, 2 * n + 2)
                        v = qk_ss[:, c % 2 * 16:c % 2 * 16 + 16]
                        link(ts(v, v, 1e-24, None, ALU.max))
                        rsqrt(qk_rs[:, c % 2 * 16:c % 2 * 16 + 16], v, 16, frs_done)

                    def fqT(l, c):
                        n = l * NT + c
                        dve.wait_ge(fqT_psum, n + 1)
                        if n >= 2:
                            dve.wait_ge(fS_psum, (n - 1) * NPAIR)
                        half = slice(DF, P)
                        nc.vector.tensor_copy(v4(qTz[:], 2, HF)[half, c % 2, 1:HF:2], v3(place("fqT", l, c)[:], NPAIR)[half])\
                            .then_inc(fqT_hi, 1)

                    def fS(l, i):
                        c, g = divmod(i, NPAIR)
                        n = pair(l, i)
                        lo = 128 if c == 0 else 64
                        dve.wait_ge(fS_psum, n + 1)
                        if l:
                            dve.wait_ge(fexp_done, 2 * NT * NPAIR)
                        nc.vector.tensor_reduce(nmax[:, c * HF + 2 * g:c * HF + 2 * g + 2], v3(place("fS", l, i)[:], 2)[:, :, lo:256],
                                                AX, ALU.max, negate=True).then_inc(fmax_done, 1)

                    def fnorm(l, i):
                        n = pair(l, i)
                        at = 2 * i
                        dve.wait_ge(fexp_done, 2 * n + 2)
                        nc.vector.reciprocal(prec[:, at:at + 2], psums[:, at:at + 2]).then_inc(fprec_done, 1)

                    def fr1(l, c):
                        n = l * NT + c + 1
                        dve.wait_ge(fwo_psum, n)
                        if l:
                            dve.wait_ge(r_done, 1)
                            dve.wait_ge(h2_done, 1)
                        tile, old = slice(c * P, (c + 1) * P), r2T if l else xnT
                        tt(r1T[:, tile], place("fwo", l)[:, tile], old[:, tile], ALU.add).then_inc(r1_done, 1)

                    def fres(l):
                        dve.wait_ge(r1_done, NT * (l + 1))
                        if l:
                            dve.wait_ge(h2tm_psum, l)
                        shifted(h2T, r1T).then_inc(h2_done, 1)

                    def fln(l):
                        dve.wait_ge(h2tm_psum, l + 1)
                        if l:
                            dve.wait_ge(normT_psum, 1)
                        layernorm(v3(norm_tm[:], NT), v3(place("h2tm", l)[:], NT), D, norm_done)

                    def hnT_(l):
                        dve.wait_ge(normT_psum, l + 1)
                        if l:
                            dve.wait_ge(fa_psum, 3)
                        cols = W(f"cols{l}")
                        dve.wait_ge(late_loads, 32)
                        ts(hnT[:], place("normT", l)[:], cols[:, 7:8], cols[:, 8:9], ALU.mult, ALU.add).then_inc(hn_done, 1)

                    def fw1(l, j):
                        _, m = HID_TILES[j]
                        n = 3 * l + j
                        if n == 0:
                            dve.wait_ge(X_zeroed, 16 * NT)
                        dve.wait_ge(gelu_done, n + 1)
                        dve.wait_ge(fa_psum, n + 1)
                        if l:
                            dve.wait_ge(fw2_psum, 1)
                        elif j == 2:
                            dve.wait_ge(out_stored, 16)
                        stt(hm[0:m, j * T:(j + 1) * T], place("fa", l, j)[0:m, :], W(f"cols{l}")[0:m, j:j + 1],
                            gl[0:m, (n % 2) * T:(n % 2 + 1) * T], ALU.add, ALU.mult).then_inc(hm_done, 1)

                    def fw2(l):
                        dve.wait_ge(fw2_psum, l + 1)
                        stt(r2T[:], place("fw2", l)[:], W(f"cols{l}")[:, 6:7], r1T[:], ALU.add, ALU.add).then_inc(r_done, 1)
                        if l == 0:
                            dve.wait_ge(r_done, 1)
                            shifted(hT, r2T).then_inc(h_done, 1)

                    def x1():
                        dve.wait_ge(x1_psum, 1)
                        dve.wait_ge(normT_psum, 2)
                        tt(x1_tm[:], place("x1")[:], x_tm[:], ALU.add).then_inc(x1_done, 1)
                        dve.wait_ge(x1_done, 1)
                        layernorm(v3(norm_tm[:], NT), v3(x1_tm[:], NT), D, norm_done)

                    def lat():
                        dve.wait_ge(lat_psum, 1)
                        layernorm(v3(lat_tm[:], NT), v3(place("lat")[:, 0:NT * LAT], NT), LAT, lat_done)

                    def latT_():
                        dve.wait_ge(latT_psum, 1)
                        cols = W("latcols")
                        ts(latT[0:LAT, :], place("latT")[0:LAT, :], cols[0:LAT, 0:1], cols[0:LAT, 1:2], ALU.mult, ALU.add)\
                            .then_inc(latT_done, 1)

                    def rope(i, scale):
                        f = qkf[:, i * T:(i + 1) * T]
                        dve.wait_ge(mq_psum, 2 * i + 1)
                        stt(rc[:], place("mq", 2 * i)[:], scale, C("rcos"), ALU.mult, ALU.mult).then_inc(rope_done, 1)
                        dve.wait_ge(mq_psum, 2 * i + 2)
                        stt(rsn[:], place("mq", 2 * i + 1)[:], scale, C("rsin"), ALU.mult, ALU.mult).then_inc(rope_done, 1)
                        dve.wait_ge(rope_done, 2 * i + 2)
                        tt(f, rc[:], rsn[:], ALU.add).then_inc(qkf_done, 1)
                        p = [parts[:, (3 * i + n) * T:(3 * i + n + 1) * T] for n in range(3)]
                        r = res[:, i * T:(i + 1) * T]
                        dve.wait_ge(split_done, 2 * i + 1)
                        tt(r, f, p[0], ALU.subtract).then_inc(split2_done, 1)
                        dve.wait_ge(split_done, 2 * i + 2)
                        tt(p[2], r, p[1], ALU.subtract).then_inc(split2_done, 1)

                    def mS(h, t):
                        for c, at in (((0, 0), (2, P)), ((1, 0),), ((3, 0),))[t]:
                            dve.wait_ge(mS_psum, 3 * h + t + 1)
                            nc.vector.tensor_reduce(nmx[:, h * NT + c:h * NT + c + 1], place("mS", h, t)[:, at:at + (c + 1) * P],
                                                    AX, ALU.max, negate=True).then_inc(nmx_done, 1)

                    def mrow(g):
                        dve.wait_ge(mrow_psum, g + 1)
                        if g:
                            dve.wait_ge(mrow_sent, 48 * g)
                        p = [mparts[0:NROW, n * P:(n + 1) * P] for n in range(3)]
                        ps, left = place("mrow", g)[0:NROW, 0:P], mres[0:NROW, :]
                        link(nc.vector.tensor_copy(p[0], ps))
                        link(tt(left, ps, p[0], ALU.subtract))
                        link(nc.vector.tensor_copy(p[1], left))
                        tt(p[2], left, p[1], ALU.subtract).then_inc(mrow_done, 1)

                    def next_norm():
                        dve.wait_ge(x_loaded, 16)
                        dve.wait_ge(normT_psum, 3)
                        head_norm()

                    def next_copy():
                        dve.wait_ge(ew_psum, NE + 1)
                        head_copy()

                    def matg(g):
                        dve.wait_ge(matg_psum, g + 1)
                        ps = v3(place("matg", g)[:], NT * GROUP)
                        r = at_rec[:, 0:NT * GROUP]
                        link(nc.vector.reciprocal(r, ps[:, :, DM]))
                        o = v3(at_tm[:], NT)[:, :, g * GROUP * DM:(g + 1) * GROUP * DM].rearrange("p c (h d) -> p c h d", h=GROUP)
                        for c in range(NT):
                            m = tt(o[:, c], ps[:, c * GROUP:(c + 1) * GROUP, 0:DM], spread(r[:, c * GROUP:(c + 1) * GROUP], DM), ALU.mult)
                        m.then_inc(at_done, 1)

                    def gate():
                        dve.wait_ge(gate_psum, 1)
                        tt(v3(gz[:], NT), v3(place("gate")[:, 0:NT * NE], NT), repeat(R("gate_b"), NT), ALU.add).then_inc(gz_done, 1)
                        dve.wait_ge(gexp_done, 1)
                        link(ts(gw_[:], gp[:], 1.0, None, ALU.add))
                        link(nc.vector.reciprocal(gp[:], gw_[:]))
                        for c in range(NT):
                            p = gp[:, c * NE:(c + 1) * NE]
                            other, own = repeat(p, NE), spread(p, NE)
                            tt(v3(gcmp[:, c * 36:(c + 1) * 36], NE), other, own, ALU.is_gt)
                            m = tt(v3(geq[:, c * 36:(c + 1) * 36], NE), other, own, ALU.is_equal)
                        link(m)
                        link(tt(v3(geq[:], NT), v3(geq[:], NT), repeat(C("tri"), NT), ALU.mult))
                        link(tt(gcmp[:], gcmp[:], geq[:], ALU.add))
                        link(nc.vector.tensor_reduce(grank[:], v3(gcmp[:], NT * NE), AX, ALU.add))
                        link(stt(gw_[:], grank[:], 1.5, gp[:], ALU.is_lt, ALU.mult))
                        link(nc.vector.tensor_reduce(gsum[:, 0:NT], v3(gw_[:], NT), AX, ALU.add))
                        link(ts(gsum[:, 0:NT], gsum[:, 0:NT], 1e-8, None, ALU.add))
                        link(nc.vector.reciprocal(gsum[:, NT:2 * NT], gsum[:, 0:NT]))
                        tt(v3(ge[:], NT), v3(gw_[:], NT), spread(gsum[:, NT:2 * NT], NE), ALU.mult).then_inc(ge_done, 1)

                    def eu(e):
                        slot = slice((e % 2) * T, (e % 2 + 1) * T)
                        dve.wait_ge(eth_done, e + 1)
                        stt(se[:, slot], the[:, slot], 1.0, place("eu", e)[:], ALU.add, ALU.mult).then_inc(es_done, 1)

                    def ew(e):
                        slot = slice((e % 2) * T, (e % 2 + 1) * T)
                        dve.wait_ge(es_done, e + 1)
                        dve.wait_ge(ew_psum, e + 1)
                        if e >= 2:
                            dve.wait_ge(ey_psum, e - 1)
                        stt(he[:, slot], se[:, slot], 0.5, place("ew", e)[:], ALU.mult, ALU.mult).then_inc(eh_done, 1)

                    def e_down(e):
                        dve.wait_ge(ey_psum, e + 1)
                        dve.wait_ge(ge_done, 1)
                        if e:
                            dve.wait_ge(ey_done, e)
                        for c in range(NT):
                            s = ge[:, c * NE + e:c * NE + e + 1]
                            o, y = acc[:, c * P:(c + 1) * P], place("ey", e)[:, c * P:(c + 1) * P]
                            m = stt(o, y, s, o, ALU.mult, ALU.add) if e else ts(o, y, s, None, ALU.mult)
                        m.then_inc(ey_done, 1)

                    def final():
                        dve.wait_ge(ey_done, NE)
                        link(tt(acc[:], acc[:], x1_tm[:], ALU.add))
                        dve.wait_ge(fin_psum, 1)
                        tt(fin[:], place("fin")[:], acc[:], ALU.add).then_inc(fin_done, 1)

                    walk({"k": k, "krs": krs_, "bg": bg, "gram": gram, "solve": solve, "inv_v": inv_v,
                          "inv_zx": inv_zx, "seq_b": seq_b, "seq_p": seq_p, "seq_o": seq_o, "delta_norm": delta_norm, "fqk": fqk, "frs": frs, "fqT": fqT, "fr1": fr1, "fS": fS,
                          "fnorm": fnorm, "fres": fres, "fln": fln, "hnT": hnT_, "fw1": fw1, "fw2": fw2, "x1": x1, "lat": lat,
                          "latT": latT_, "mq": lambda: rope(0, DM ** -0.5), "mk": lambda: rope(1, 1.0),
                          "mS": mS, "mrow": mrow, "head_norm": next_norm, "head_T": next_copy, "matg": matg,
                          "gate": gate, "eu": eu, "ew": ew, "e_down": e_down, "final": final})

                @block.gpsimd
                def _(pool):
                    tt = nc.gpsimd.tensor_tensor


                    def kT_(c):
                        pool.wait_ge(krs_done, 1)
                        pool.wait_ge(k_copied, c + 1)
                        tt(v4(kn[:], NT, H0)[:, c], v4(kn[:], NT, H0)[:, c], spread(krs[:, c * H0:(c + 1) * H0], DK), ALU.mult)\
                            .then_inc(kn_done, 1)

                    def delta_norm():
                        pool.wait_ge(ors_done, 1)
                        pool.wait_ge(o_back, 1)
                        o = v3(o_all[:], NT * H0)
                        pool.wait_ge(osq_done, 1)
                        tt(o, o, spread(ors[:], DV), ALU.mult).then_inc(on_done, 1)
                        pool.wait_ge(on_done, 1)
                        tt(v3(o_all[:], NT), v3(o_all[:], NT), repeat(norm_w[:], NT), ALU.mult).then_inc(on_done, 1)
                        pool.wait_ge(on_done, 2)
                        pool.wait_ge(gs_done, NT)
                        tt(o_all[:], o_all[:], gs[:], ALU.mult).then_inc(og_done, 1)

                    def fqk(l, c, i):
                        m = 2 * (l * NT + c) + i
                        pool.wait_ge(ft1_done, m + 1)
                        pool.wait_ge(frot_done, m + 1)
                        d = (q_f, k_f)[i][:, c % 2 * T:(c % 2 + 1) * T]
                        tt(d, d, rot[m % 2][:], ALU.add).then_inc(fsum_done, 1)

                    def fscale(l, c, i):
                        m = 2 * (l * NT + c) + i
                        pool.wait_ge(frs_done, l * NT + c + 1)
                        pool.wait_ge(fsum_done, m + 1)
                        d = v3((q_f, k_f)[i][:, c % 2 * T:(c % 2 + 1) * T], HF)
                        tt(d, d, spread(qk_rs[:, c % 2 * 16 + 8 * i:c % 2 * 16 + 8 * i + 8], DF), ALU.mult).then_inc(fn_done, 1)

                    def fnorm(l, i):
                        lo = 128 if i < NPAIR else 64
                        p = v3(p_sb[:, pair(l, i) % P_SLOTS * T:(pair(l, i) % P_SLOTS + 1) * T], 2)[:, :, lo:256]
                        pool.wait_ge(fprec_done, pair(l, i) + 1)
                        tt(p, p, spread(prec[:, 2 * i:2 * i + 2], 256 - lo), ALU.mult).then_inc(fnorm_done, 1)

                    def x1():
                        pool.wait_ge(x1_psum, 1)
                        nc.gpsimd.memset(vaug, 0.0).then_inc(vaug_zeroed, 1)
                        pool.wait_ge(vaug_zeroed, 1)
                        nc.gpsimd.memset(v3(vaug, NT * HM)[:, :, DM:DM + 1], 1.0).then_inc(vaug_zeroed, 1)

                    walk({"kT": kT_, "delta_norm": delta_norm, "fqk": fqk, "fscale": fscale, "fnorm": fnorm, "x1": x1})

                @block.sync
                def _(sp):

                    def gram(c):
                        sp.wait_ge(L_done, c + 1)
                        sp.dma_start(in_dram(L_dram, c), v4(L, 2, H0)[:, c % 2]).then_inc(L_kept[c % 2], 16)

                    def solve():
                        sp.wait_ge(L_kept[0], 32)
                        sp.wait_ge(L_kept[1], 32)
                        sp.dma_start(v3(Lb, BLK), diagonal(L_dram)).then_inc(Lb_loaded, 16)
                        sp.wait_ge(Xb_done, 1)
                        sp.wait_ge(X_zeroed, 16 * NT)
                        sp.dma_start(diagonal(X_dram), v3(Xb, BLK)).then_inc(Xb_kept, 16)

                    def inv_load(c):
                        sp.wait_ge(Xb_kept, 16)
                        if c >= 2:
                            sp.wait_ge(ZV_psum, at_level(LEVELS - 1, c - 2, LEVELS - 1, 1) + 1)
                        sp.dma_start(v4(X, 2, H0)[:, c % 2], in_dram(X_dram, c)).then_inc(X_loaded[c % 2], 16)
                        sp.dma_start(v4(L, 2, H0)[:, c % 2], in_dram(L_dram, c)).then_inc(L_loaded[c % 2], 16)

                    def x1():
                        sp.wait_ge(x1_done, 1)
                        sp.dma_start(v3(x_tm[:], NT), x[bass.ds(b + 1, 1)].rearrange("a (t p) d -> p (a t) d", p=P)).then_inc(x_loaded, 16)
                        for i, dst in enumerate((Qst32, Kst32)):
                            sp.dma_start(dst[9 * DM:P, :], row_fill[i]).then_inc(rows_filled, 16)

                    def send(i):
                        for n in range(3):
                            sp.wait_ge(split_done, 2 * i + 1 + (n > 0))
                            sp.wait_ge(split2_done, 2 * i + 1 + (n > 1))
                            to = parts_dram[i, n * DM:(n + 1) * DM].rearrange("d (h t) -> h d t", h=HM)
                            sp.dma_start(to, parts[:, (3 * i + n) * T:(3 * i + n + 1) * T]).then_inc(parts_kept, 16)
                        sp.wait_ge(parts_kept, 48 * (i + 1))
                        rows, half = 3 * DM, HM // 2 * T
                        for s in range(3):
                            if i == 1:
                                sp.dma_start(Kst[s * rows:(s + 1) * rows, 0:half], parts_dram[1][:, 0:half]).then_inc(parts_sent, 16)
                            else:
                                for n in range(3):
                                    at = (3 * n + s) * DM
                                    sp.dma_start(Qst[at:at + DM, :], parts_dram[0, n * DM:(n + 1) * DM]).then_inc(parts_sent, 16)
                        if i == 1:
                            for s in range(3):
                                sp.dma_start(Kst[s * rows:(s + 1) * rows, half:], parts_dram[1][:, half:]).then_inc(late_keys_sent, 16)

                    def mrow(g):
                        sp.wait_ge(mrow_done, g + 1)
                        for i in range(3):
                            dst = Qst[9 * DM + i:9 * DM + i + 1, g * GROUP * T:(g + 1) * GROUP * T].rearrange("a (r t) -> a r t", t=P)
                            sp.dma_start(dst, mparts[0:NROW, i * P:(i + 1) * P]).then_inc(mrow_sent, 16)

                    def final():
                        sp.wait_ge(fin_done, 1)
                        sp.sem_clear(out_stored)
                        sp.dma_start(out[bass.ds(b, 1)].rearrange("a (t p) d -> p (a t) d", p=P), v3(fin[:], NT)).then_inc(out_stored, 16)
                        sp.wait_ge(x_loaded, 16)

                    walk({"gram": gram, "solve": solve, "inv_load": inv_load, "x1": x1, "mq": lambda: send(0), "mk": lambda: send(1), "mrow": mrow, "final": final})

            nc.sync.sem_clear(range(numbers[0], numbers[-1] + 1))
            nc.all_engine_barrier()

        with nc.Block(no_gpsimd_drain=True) as block:
            @block.sync
            def _(sp):
                sp.wait_ge(out_stored, 16)



def pack(inp):
    f = np.float32
    a = {k: np.asarray(v) for k, v in inp.items()}

    def rows128(m):
        out = np.zeros((P, m.shape[1]), f)
        out[:m.shape[0]] = m
        return out

    def tiles(m):
        n = -(-m.shape[0] // P)
        return np.concatenate([rows128(m[j * P:(j + 1) * P]) for j in range(n)], 1)

    w = {"wk": a["L0_attn_Wk"], "wq": a["L0_attn_Wq"], "wv": a["L0_attn_Wv"],
         "wbg": np.concatenate([a["L0_attn_Wb"], a["L0_attn_Wg"]], 1), "wo0": a["L0_attn_Wo"]}
    for l in range(DEPTH):
        w[f"wqkv{l}"] = a["L0_ffn_wqkv"][l]
        w[f"wof{l}"] = tiles(a["L0_ffn_wo"][l])
        w[f"w1{l}"] = a["L0_ffn_w1"][l]
        w[f"w2{l}"] = tiles(a["L0_ffn_w2"][l])
        b1 = a["L0_ffn_b1"][l]
        w[f"cols{l}"] = np.concatenate([tiles(b1[:HID, None]), tiles(b1[HID:, None]), a["L0_ffn_b2"][l][:, None],
                                        a["L0_ffn_ln_g"][l][:, None], a["L0_ffn_ln_b"][l][:, None]], 1)
    turned = np.arange(D).reshape(HM, 2, DM // 2)[:, ::-1].reshape(-1)
    w["Wq"], w["Wqr"] = a["L1_attn_W_q"], a["L1_attn_W_q"][:, turned]
    w["Wdkv"] = a["L1_attn_W_dkv"]
    w["Wuk"], w["Wukr"], w["Wuv"] = rows128(a["L1_attn_W_uk"]), rows128(a["L1_attn_W_uk"][:, turned]), rows128(a["L1_attn_W_uv"])
    w["Wo"] = a["L1_attn_W_o"]
    w["latcols"] = rows128(np.stack([a["L1_attn_ln_gamma"], a["L1_attn_ln_beta"]], 1))
    w["gate"] = a["L1_ffn_gate_w"].T
    for e in range(NE):
        w[f"eu{e}"], w[f"ew{e}"], w[f"ed{e}"] = a["L1_ffn_ew1"][e].T, a["L1_ffn_ew3"][e].T, a["L1_ffn_ew2"][e].T
    w[f"eu{NE}"], w[f"ew{NE}"], w[f"ed{NE}"] = a["L1_ffn_fc1"].T, a["L1_ffn_fc2"].T, a["L1_ffn_fc3"].T
    packed = np.ascontiguousarray(np.concatenate([w[n] for n, _ in weight_layout()], 1))
    rows = np.concatenate([a["L0_attn_norm_w"], a["L0_ffn_q_scale"].reshape(-1), a["L0_ffn_k_scale"].reshape(-1),
                           a["L1_ffn_gate_b"]])[None]
    return packed, np.ascontiguousarray(rows)


def kernel(**inputs):
    import concourse.bacc as bacc
    from concourse.bass_utils import run_bass_kernel_spmd

    packed, rows = pack(inputs)
    consts, consts_bf = constants()
    row_fill = np.zeros((2, P - 9 * DM, HM * T // 2), np.uint32)
    row_fill[1, 0:3] = 0x3F803F80
    row_fill = row_fill.view(np.float32)
    padded = np.concatenate([inputs["L0_attn_x"], np.zeros((1, T, D), np.float32)])
    arrays = {"x": padded, "weights": packed, "rows": rows, "consts": consts,
              "consts_bf": consts_bf, "row_fill": row_fill}
    nc = bacc.Bacc("TRN2", target_bir_lowering=False, num_devices=1)
    args = [nc.dram_tensor(n, a.shape, mybir.dt.from_np(a.dtype), kind="ExternalInput").ap() for n, a in arrays.items()]
    out = nc.dram_tensor("out", (BATCH, T, D), F32, kind="ExternalOutput").ap()
    parts_dram = nc.dram_tensor("parts_dram", (2, 3 * DM, HM * T), BF16, kind="Internal").ap()
    L_dram, X_dram = (nc.dram_tensor(n, (NT * H0 * HEAD_ROOM,), F32, kind="Internal").ap() for n in ("L_dram", "X_dram"))
    build(nc, *args, parts_dram, L_dram, X_dram, out)
    r = run_bass_kernel_spmd(nc, [arrays], core_ids=[0])
    return r.results[0]["out"]
```
